# Optimizing a Trainium2 kernel written in Bass

```python
import numpy as np
import jax
import jax.numpy as jnp

def _softmax(x, axis=-1):
    return jax.nn.softmax(x, axis=axis)

def _gelu(x):
    return jax.nn.gelu(x, approximate=True)

def _silu(x):
    return jax.nn.silu(x)

def _sigmoid(x):
    return jax.nn.sigmoid(x)

def _layernorm(x, axis=-1, eps=1e-05):
    m = jnp.mean(x, axis=axis, keepdims=True)
    v = jnp.var(x, axis=axis, keepdims=True)
    return (x - m) / jnp.sqrt(v + eps)

def _scatter_add(tgt, idx, src, axis=0):
    return tgt.at[idx].add(src)

def _segment_sum(src, seg, n):
    return jax.ops.segment_sum(src, seg, n)
kernel_name = 'mk_conv_attn_hybrid_d2_conv_nhwc512_r4_5d5030'

def setup_inputs(seed: int=0):
    np.random.seed(seed)
    _w = jnp.asarray

    def _rec_inputs():
        import jax
        import jax.numpy as jnp
        _gk = jax.random.key(seed)
        x = 7.22e-05 + 1 * jax.random.normal(jax.random.fold_in(_gk, 1), (4, 16, 16, 128), jnp.float32)
        return x
    x = _rec_inputs()

    def _L0_conv_setup():
        import jax, jax.numpy as jnp
        import numpy as np
        B, H, W, C = (4, 16, 16, 128)
        R, NH, KS = (2, 8, 7)
        S = 1.0

        def layernorm(t, g, b):
            m = t.mean(-1, keepdims=True)
            v = ((t - m) ** 2).mean(-1, keepdims=True)
            return (t - m) / jnp.sqrt(v + 1e-05) * g + b

        def grid_sample_bilinear_zeros(img, grid):
            b, c, h, w = img.shape
            gh, gw = (grid.shape[1], grid.shape[2])
            x = (grid[..., 0] + 1.0) * 0.5 * (w - 1)
            y = (grid[..., 1] + 1.0) * 0.5 * (h - 1)
            x0 = jnp.floor(x)
            y0 = jnp.floor(y)
            wx1 = x - x0
            wy1 = y - y0
            x0i = x0.astype(jnp.int32)
            y0i = y0.astype(jnp.int32)
            flat = img.reshape(b, c, h * w)

            def corner(xi, yi, wt):
                valid = ((xi >= 0) & (xi < w) & (yi >= 0) & (yi < h)).astype(img.dtype)
                idx = jnp.clip(yi, 0, h - 1) * w + jnp.clip(xi, 0, w - 1)
                vals = jnp.take_along_axis(flat, idx.reshape(b, 1, gh * gw), axis=2)
                return vals * (valid * wt).reshape(b, 1, gh * gw)
            out = corner(x0i, y0i, (1 - wx1) * (1 - wy1)) + corner(x0i + 1, y0i, wx1 * (1 - wy1)) + corner(x0i, y0i + 1, (1 - wx1) * wy1) + corner(x0i + 1, y0i + 1, wx1 * wy1)
            return out.reshape(b, c, gh, gw)
        key = jax.random.key(seed)
        ks = jax.random.split(key, 12)
        sd = 0.02
        f32 = jnp.float32
        return {'x': jax.random.normal(ks[0], (B, H, W, C), f32), 'ln_g': jnp.ones((C,), f32), 'ln_b': jnp.zeros((C,), f32), 'wq': jax.random.normal(ks[1], (C, C), f32) * sd, 'bq': jnp.zeros((C,), f32), 'wv': jax.random.normal(ks[2], (C, C), f32) * sd, 'bv': jnp.zeros((C,), f32), 'dw_w': jax.random.normal(ks[3], (C, 1, KS, KS), f32) * sd, 'dw_b': jnp.zeros((C,), f32), 'pw_w': jax.random.normal(ks[4], (2, C, 1, 1), f32) * sd, 'mq_w': jax.random.normal(ks[5], (C, C), f32) * sd, 'mq_b': jnp.zeros((C,), f32), 'mk_w': jax.random.normal(ks[6], (C, C), f32) * sd, 'mk_b': jnp.zeros((C,), f32), 'mv_w': jax.random.normal(ks[7], (C, C), f32) * sd, 'mv_b': jnp.zeros((C,), f32), 'mo_w': jax.random.normal(ks[8], (C, C), f32) * sd, 'mo_b': jnp.zeros((C,), f32), 'mlp_w': jax.random.normal(ks[9], (C, C), f32) * sd, 'mlp_b': jnp.zeros((C,), f32)}
    _L0_conv_all = _L0_conv_setup()
    _L0_conv_in = {k: v for k, v in _L0_conv_all.items() if k in ('ln_g', 'ln_b', 'wq', 'bq', 'wv', 'bv', 'dw_w', 'dw_b', 'pw_w', 'mq_w', 'mq_b', 'mk_w', 'mk_b', 'mv_w', 'mv_b', 'mo_w', 'mo_b', 'mlp_w', 'mlp_b')}
    del _L0_conv_all

    def _L1_attn_setup():
        import jax, jax.numpy as jnp
        import numpy as np
        NUM_HEADS = 8
        NUM_LANDMARKS = 16
        TOPK_LANDMARKS = 4
        key = jax.random.key(seed)
        k1, k2, k3, k4 = jax.random.split(key, 4)
        B, N, C = (1, 512, 128)
        return {'x': jax.random.normal(k1, (B, N, C), jnp.float32), 'w_qkv': jax.random.normal(k2, (3 * C, C), jnp.float32) * 0.02, 'w_proj': jax.random.normal(k3, (C, C), jnp.float32) * 0.02, 'b_proj': jax.random.normal(k4, (C,), jnp.float32) * 0.02}
    _L1_attn_all = _L1_attn_setup()
    _L1_attn_in = {k: v for k, v in _L1_attn_all.items() if k in ('w_qkv', 'w_proj', 'b_proj')}
    del _L1_attn_all

    def _L1_ffn_setup():
        import jax, jax.numpy as jnp
        import numpy as np
        B, S, D, O = (1, 512, 128, 128)
        H, QD, K, PK = (8, 64, 16, 64)
        N = PK * PK
        HALF = QD // 2

        def _l2norm(x):
            n = jnp.sqrt(jnp.sum(x * x, axis=-1, keepdims=True))
            return x / jnp.maximum(n, 1e-12)
        key = jax.random.key(seed)
        ks = jax.random.split(key, 9)
        return {'hidden_states': jax.random.normal(ks[0], (B, S, D), jnp.float32), 'Wq': jax.random.normal(ks[1], (H * QD, D), jnp.float32) * 0.02, 'bq': jnp.zeros((H * QD,), jnp.float32), 'ln_g': jnp.ones((QD,), jnp.float32), 'ln_b': jnp.zeros((QD,), jnp.float32), 'keys0': jax.random.normal(ks[2], (PK, HALF), jnp.float32) * 0.02, 'keys1': jax.random.normal(ks[3], (PK, HALF), jnp.float32) * 0.02, 'expert_down': jax.random.normal(ks[4], (N, D), jnp.float32) * 0.02, 'expert_up': jax.random.normal(ks[5], (N, O), jnp.float32) * 0.02}
    _L1_ffn_all = _L1_ffn_setup()
    _L1_ffn_in = {k: v for k, v in _L1_ffn_all.items() if k in ('Wq', 'bq', 'ln_g', 'ln_b', 'keys0', 'keys1', 'expert_down', 'expert_up')}
    del _L1_ffn_all
    return {'x': x, 'L0_conv_ln_g': _L0_conv_in['ln_g'], 'L0_conv_ln_b': _L0_conv_in['ln_b'], 'L0_conv_wq': _L0_conv_in['wq'], 'L0_conv_bq': _L0_conv_in['bq'], 'L0_conv_wv': _L0_conv_in['wv'], 'L0_conv_bv': _L0_conv_in['bv'], 'L0_conv_dw_w': _L0_conv_in['dw_w'], 'L0_conv_dw_b': _L0_conv_in['dw_b'], 'L0_conv_pw_w': _L0_conv_in['pw_w'], 'L0_conv_mq_w': _L0_conv_in['mq_w'], 'L0_conv_mq_b': _L0_conv_in['mq_b'], 'L0_conv_mk_w': _L0_conv_in['mk_w'], 'L0_conv_mk_b': _L0_conv_in['mk_b'], 'L0_conv_mv_w': _L0_conv_in['mv_w'], 'L0_conv_mv_b': _L0_conv_in['mv_b'], 'L0_conv_mo_w': _L0_conv_in['mo_w'], 'L0_conv_mo_b': _L0_conv_in['mo_b'], 'L0_conv_mlp_w': _L0_conv_in['mlp_w'], 'L0_conv_mlp_b': _L0_conv_in['mlp_b'], 'L1_attn_w_qkv': _L1_attn_in['w_qkv'], 'L1_attn_w_proj': _L1_attn_in['w_proj'], 'L1_attn_b_proj': _L1_attn_in['b_proj'], 'L1_ffn_Wq': _L1_ffn_in['Wq'], 'L1_ffn_bq': _L1_ffn_in['bq'], 'L1_ffn_ln_g': _L1_ffn_in['ln_g'], 'L1_ffn_ln_b': _L1_ffn_in['ln_b'], 'L1_ffn_keys0': _L1_ffn_in['keys0'], 'L1_ffn_keys1': _L1_ffn_in['keys1'], 'L1_ffn_expert_down': _L1_ffn_in['expert_down'], 'L1_ffn_expert_up': _L1_ffn_in['expert_up']}

def reference(x, L0_conv_ln_g, L0_conv_ln_b, L0_conv_wq, L0_conv_bq, L0_conv_wv, L0_conv_bv, L0_conv_dw_w, L0_conv_dw_b, L0_conv_pw_w, L0_conv_mq_w, L0_conv_mq_b, L0_conv_mk_w, L0_conv_mk_b, L0_conv_mv_w, L0_conv_mv_b, L0_conv_mo_w, L0_conv_mo_b, L0_conv_mlp_w, L0_conv_mlp_b, L1_attn_w_qkv, L1_attn_w_proj, L1_attn_b_proj, L1_ffn_Wq, L1_ffn_bq, L1_ffn_ln_g, L1_ffn_ln_b, L1_ffn_keys0, L1_ffn_keys1, L1_ffn_expert_down, L1_ffn_expert_up):
    import jax
    import jax.numpy as jnp

    def _L0_conv_ref(x, ln_g, ln_b, wq, bq, wv, bv, dw_w, dw_b, pw_w, mq_w, mq_b, mk_w, mk_b, mv_w, mv_b, mo_w, mo_b, mlp_w, mlp_b):
        import jax, jax.numpy as jnp
        import numpy as np
        B, H, W, C = (4, 16, 16, 128)
        R, NH, KS = (2, 8, 7)
        S = 1.0

        def layernorm(t, g, b):
            m = t.mean(-1, keepdims=True)
            v = ((t - m) ** 2).mean(-1, keepdims=True)
            return (t - m) / jnp.sqrt(v + 1e-05) * g + b

        def grid_sample_bilinear_zeros(img, grid):
            b, c, h, w = img.shape
            gh, gw = (grid.shape[1], grid.shape[2])
            x = (grid[..., 0] + 1.0) * 0.5 * (w - 1)
            y = (grid[..., 1] + 1.0) * 0.5 * (h - 1)
            x0 = jnp.floor(x)
            y0 = jnp.floor(y)
            wx1 = x - x0
            wy1 = y - y0
            x0i = x0.astype(jnp.int32)
            y0i = y0.astype(jnp.int32)
            flat = img.reshape(b, c, h * w)

            def corner(xi, yi, wt):
                valid = ((xi >= 0) & (xi < w) & (yi >= 0) & (yi < h)).astype(img.dtype)
                idx = jnp.clip(yi, 0, h - 1) * w + jnp.clip(xi, 0, w - 1)
                vals = jnp.take_along_axis(flat, idx.reshape(b, 1, gh * gw), axis=2)
                return vals * (valid * wt).reshape(b, 1, gh * gw)
            out = corner(x0i, y0i, (1 - wx1) * (1 - wy1)) + corner(x0i + 1, y0i, wx1 * (1 - wy1)) + corner(x0i, y0i + 1, (1 - wx1) * wy1) + corner(x0i + 1, y0i + 1, wx1 * wy1)
            return out.reshape(b, c, gh, gw)
        b, h, w, c = x.shape
        x_ln = layernorm(x, ln_g, ln_b).transpose(0, 3, 1, 2)
        x_flat = x_ln.reshape(b, h * w, c)
        q = x_flat @ wq + bq
        q_img = q.reshape(b, c, h, w)
        o = jax.lax.conv_general_dilated(q_img, dw_w, (R, R), [(KS // 2, KS // 2)] * 2, dimension_numbers=('NCHW', 'OIHW', 'NCHW'), feature_group_count=c)
        o = jax.nn.gelu(o + dw_b[None, :, None, None], approximate=False)
        offsets = jax.lax.conv_general_dilated(o, pw_w, (1, 1), [(0, 0), (0, 0)], dimension_numbers=('NCHW', 'OIHW', 'NCHW'))
        hg, wg = (offsets.shape[2], offsets.shape[3])
        ref_x = (jnp.arange(wg, dtype=x.dtype) + 0.5) * (2.0 / wg) - 1.0
        ref_y = (jnp.arange(hg, dtype=x.dtype) + 0.5) * (2.0 / hg) - 1.0
        gx, gy = jnp.meshgrid(ref_x, ref_y, indexing='ij')
        refs = jnp.stack([gx, gy], axis=0)
        deformed = refs[None] + S * jnp.tanh(offsets)
        deformed = (deformed + 1.0) * (h / R) / 2.0
        grid = deformed[:, ::-1].transpose(0, 2, 3, 1)
        interp = grid_sample_bilinear_zeros(x.transpose(0, 3, 1, 2), grid)
        interp_flat = interp.reshape(b, hg * wg, c)
        v = interp_flat @ wv + bv
        k = interp_flat @ wv + bv
        hd = c // NH

        def heads(t):
            return t.reshape(b, -1, NH, hd).transpose(0, 2, 1, 3)
        qh = heads(q @ mq_w + mq_b)
        kh = heads(k @ mk_w + mk_b)
        vh = heads(v @ mv_w + mv_b)
        attn = jax.nn.softmax(jnp.einsum('bnqd,bnkd->bnqk', qh, kh), axis=-1)
        att = jnp.einsum('bnqk,bnkd->bnqd', attn, vh).transpose(0, 2, 1, 3).reshape(b, h * w, c)
        msa = att @ mo_w + mo_b
        z = msa + x.reshape(b, h * w, c)
        z_ln = layernorm(z, ln_g, ln_b)
        out = jax.nn.gelu(z_ln @ mlp_w + mlp_b, approximate=False) + z
        return out.reshape(b, w, h, c)

    def _L1_attn_ref(x, w_qkv, w_proj, b_proj):
        import jax, jax.numpy as jnp
        import numpy as np
        NUM_HEADS = 8
        NUM_LANDMARKS = 16
        TOPK_LANDMARKS = 4
        B, N, C = x.shape
        H = NUM_HEADS
        Dh = C // H
        m = min(NUM_LANDMARKS, N)
        kl = min(TOPK_LANDMARKS, m)
        scale = Dh ** (-0.5)
        qkv = (x @ w_qkv.T).reshape(B, N, 3, H, Dh).transpose(2, 0, 3, 1, 4)
        q, k, v = (qkv[0], qkv[1], qkv[2])
        seg = -(-N // m)
        pad = seg * m - N

        def segmentize(t):
            if pad > 0:
                t = jnp.pad(t, ((0, 0), (0, 0), (0, pad), (0, 0)))
            return t.reshape(B, H, m, seg, Dh)
        k_seg = segmentize(k)
        v_seg = segmentize(v)
        centroids = k_seg.mean(axis=3)
        route = jnp.einsum('bhnd,bhmd->bhnm', q, centroids) * scale
        _, topk_idx = jax.lax.top_k(route, kl)
        gather = jax.vmap(jax.vmap(lambda segs, ix: segs[ix]))
        sel_k = gather(k_seg, topk_idx).reshape(B, H, N, kl * seg, Dh)
        sel_v = gather(v_seg, topk_idx).reshape(B, H, N, kl * seg, Dh)
        attn = jnp.einsum('bhnd,bhnkd->bhnk', q, sel_k) * scale
        attn = jax.nn.softmax(attn, axis=-1)
        out = jnp.einsum('bhnk,bhnkd->bhnd', attn, sel_v)
        out = out.transpose(0, 2, 1, 3).reshape(B, N, C)
        return out @ w_proj.T + b_proj

    def _L1_ffn_ref(hidden_states, Wq, bq, ln_g, ln_b, keys0, keys1, expert_down, expert_up):
        import jax, jax.numpy as jnp
        import numpy as np
        B, S, D, O = (1, 512, 128, 128)
        H, QD, K, PK = (8, 64, 16, 64)
        N = PK * PK
        HALF = QD // 2

        def _l2norm(x):
            n = jnp.sqrt(jnp.sum(x * x, axis=-1, keepdims=True))
            return x / jnp.maximum(n, 1e-12)
        b, s, d = hidden_states.shape
        q = (hidden_states @ Wq.T + bq).reshape(b, s, H, QD)
        mu = jnp.mean(q, axis=-1, keepdims=True)
        var = jnp.mean((q - mu) ** 2, axis=-1, keepdims=True)
        q = (q - mu) / jnp.sqrt(var + 1e-05) * ln_g + ln_b
        q0, q1 = (q[..., :HALF], q[..., HALF:])
        s0 = jnp.einsum('bshq,eq->bshe', _l2norm(q0), _l2norm(keys0))
        s1 = jnp.einsum('bshq,eq->bshe', _l2norm(q1), _l2norm(keys1))
        sc0, ix0 = jax.lax.top_k(s0, K)
        sc1, ix1 = jax.lax.top_k(s1, K)
        cs = (sc0[..., :, None] + sc1[..., None, :]).reshape(b, s, H, K * K)
        ci = (ix0[..., :, None] + ix1[..., None, :]).reshape(b, s, H, K * K)
        fs, pos = jax.lax.top_k(cs, K)
        fi = jnp.take_along_axis(ci, pos, axis=-1)
        w = jax.nn.softmax(fs, axis=-1)
        down = expert_down[fi]
        up = expert_up[fi]
        inner = jnp.einsum('bsd,bshkd->bshk', hidden_states, down)
        act = jax.nn.gelu(inner, approximate=False)
        out = jnp.einsum('bshk,bshko->bso', act * w, up)
        return out

    def _gn(v, G=32, eps=1e-05):
        B_, H_, W_, C_ = v.shape
        g = v.reshape(B_, H_, W_, G, C_ // G)
        m = jnp.mean(g, axis=(1, 2, 4), keepdims=True)
        s = jnp.var(g, axis=(1, 2, 4), keepdims=True)
        return ((g - m) / jnp.sqrt(s + eps)).reshape(v.shape)

    def _ln_c(v, eps=1e-06):
        m = jnp.mean(v, axis=-1, keepdims=True)
        s = jnp.var(v, axis=-1, keepdims=True)
        return (v - m) / jnp.sqrt(s + eps)

    def _ln_t(v, eps=1e-05):
        m = jnp.mean(v, axis=-1, keepdims=True)
        s = jnp.var(v, axis=-1, keepdims=True)
        return (v - m) / jnp.sqrt(s + eps)

    def _to_tokens(v):
        B_, H_, W_, C_ = v.shape
        return v.reshape(B_, H_ * W_, C_)

    def _from_tokens(t, like):
        return t.reshape(like.shape)
    x = _L0_conv_ref(x, L0_conv_ln_g, L0_conv_ln_b, L0_conv_wq, L0_conv_bq, L0_conv_wv, L0_conv_bv, L0_conv_dw_w, L0_conv_dw_b, L0_conv_pw_w, L0_conv_mq_w, L0_conv_mq_b, L0_conv_mk_w, L0_conv_mk_b, L0_conv_mv_w, L0_conv_mv_b, L0_conv_mo_w, L0_conv_mo_b, L0_conv_mlp_w, L0_conv_mlp_b)
    t = _to_tokens(x)
    t = t + _L1_attn_ref(_ln_t(t), L1_attn_w_qkv, L1_attn_w_proj, L1_attn_b_proj)
    t = t + _L1_ffn_ref(_ln_t(t), L1_ffn_Wq, L1_ffn_bq, L1_ffn_ln_g, L1_ffn_ln_b, L1_ffn_keys0, L1_ffn_keys1, L1_ffn_expert_down, L1_ffn_expert_up)
    x = _from_tokens(t, x)
    return x

_drawn_inputs = setup_inputs


def setup_inputs(seed=0):
    import zlib

    import numpy as np

    out = dict(_drawn_inputs(seed))
    spreads = {'L0_conv_ln_g': (1.0, 0.575),
     'L0_conv_ln_b': (0.0, 0.725),
     'L0_conv_bq': (0.0, 0.8),
     'L0_conv_bv': (0.0, 0.8),
     'L0_conv_dw_b': (0.0, 0.8),
     'L0_conv_mq_b': (0.0, 0.8),
     'L0_conv_mk_b': (0.0, 0.8),
     'L0_conv_mv_b': (0.0, 0.363),
     'L0_conv_mo_b': (0.0, 0.1),
     'L0_conv_mlp_b': (0.0, 0.1),
     'L1_ffn_bq': (0.0, 0.8),
     'L1_ffn_ln_g': (1.0, 0.6),
     'L1_ffn_ln_b': (0.0, 0.8)}
    factors = {'L0_conv_wq': 8.0,
     'L0_conv_wv': 8.0,
     'L0_conv_dw_w': 8.0,
     'L0_conv_pw_w': 8.0,
     'L0_conv_mq_w': 8.0,
     'L0_conv_mk_w': 8.0,
     'L0_conv_mv_w': 8.0,
     'L1_attn_w_qkv': 6.358,
     'L1_attn_w_proj': 6.202,
     'L1_attn_b_proj': 2.799,
     'L1_ffn_Wq': 8.0,
     'L1_ffn_keys0': 8.0,
     'L1_ffn_keys1': 8.0,
     'L1_ffn_expert_down': 8.0,
     'L1_ffn_expert_up': 8.0}
    for name, (base, spread) in spreads.items():
        noise = np.random.default_rng([zlib.crc32(name.encode()), seed]).standard_normal(out[name].shape)
        drawn = base * np.exp(spread * noise) if base else spread * noise
        out[name] = jnp.asarray(drawn.astype(out[name].dtype))
    for name, factor in factors.items():
        out[name] = (out[name] * factor).astype(out[name].dtype)
    return out
```

```python
from contextlib import ExitStack

import concourse.bass as bass
from concourse import mybir

ALU = mybir.AluOpType
ACT = mybir.ActivationFunctionType
X = mybir.AxisListType.X
F32 = mybir.dt.float32
F16 = mybir.dt.float16
U16 = mybir.dt.uint16

P = 128
B = 4
SIDE = 16
C = 128
NT = 2
N = NT * P
H = 8
DH = C // H
KS = 7
PADDED = SIDE + 6
G8 = 8
NP_ = G8 * G8
SEG = 16
TOP = 16
NK = 64
QD = 64
E = 128
LN_EPS = 1e-5
MARK = -3.0e38
LARGE = 3.0e38
HIDE = -1.0e30
LO = 4
HI = E // LO
W_SCALE = 2.0 ** 15

CELL_BLOCKS = [(0, 1, 16, 0), (1, 1, 8, 16), (2, 2, 5, 24), (4, 4, 3, 34), (8, 8, 1, 46)]
CELLS = 54
SLOT_SUMS = [
    (1, 1, 1, 53, -1, 8),
    (9, 9, 1, 43, -3, 4),
    (13, 13, 1, 29, -5, 2),
    (15, 15, 1, 16, -5, 1),
    (16, 18, 1, 44, -3, 4),
    (20, 22, 1, 30, -5, 2),
    (22, 27, 1, 36, -5, 2),
]
SLOT_COPIES = [(0, 0, 1, 1), (24, 17, 9, 2), (26, 32, 1, 1)]
SLOTS = 27
HC = 4
KC = HC * SLOTS
NCH = H // HC

FRONT_JOBS = {
    "F0": [],
    "F1": ["qimg", "qT", "qhT"],
    "F2": ["conv", "offs"],
    "F3": ["WT", "interp", "vT"],
    "F4": ["kh", "vh"],
    "F5": ["S0_0", "S0_1", "mT", "P0_0", "P0_1"],
    "F6": ["O0", "aT", "msa"],
    "F7": ["zT", "mlp"],
    "F8": ["tT", "q1", "k1", "v1"],
    "F9": ["route"] + [f"S1_{t}{i}" for t in range(NT) for i in range(4)] + ["bT"],
    "F10": [f"P1_{h}" for h in range(H)],
    "F11": ["O1", "a1T", "proj", "fT"],
}
EXPERT_JOBS = {
    "NS": ["keys"],
    "N0": ["Q0", "Q1", "qsT0", "S2_00", "S2_01", "qsT1", "S2_10", "S2_11"],
    "N1": [],
    "N2": [],
    "N3": ["wT", "eT"],
    "N4": ["I0", "I1"],
    "N5": ["G00", "G01", "G10", "G11"],
    "N6": ["Y", "YT"],
}
FRONT_BANKS = [0, 1, 2, 3]
EXPERT_BANKS = [4, 5, 6, 7]


def schedule():
    front = [f"F{i}" for i in range(12)]
    expert = [f"N{i}" for i in range(7)]
    out = []
    for s in front:
        out.append((s, 0))
        if s == "F1":
            out.append(("NS", 0))
    after = {"F1": ["N0"], "F4": ["N1"], "F6": ["N2"], "F8": ["N3", "N4"], "F9": ["N5"], "F10": ["N6"]}
    for b in range(1, B):
        for s in front:
            out.append((s, b))
            out += [(n, b - 1) for n in after.get(s, [])]
    out += [(n, B - 1) for n in expert]
    return out


def place_jobs(steps):
    turn, count, out = {0: 0, 1: 0}, [0] * 8, {}
    for s, b in steps:
        ring = 0 if s[0] == "F" else 1
        banks = (FRONT_BANKS, EXPERT_BANKS)[ring]
        for job in (FRONT_JOBS if ring == 0 else EXPERT_JOBS)[s]:
            k = banks[turn[ring] % len(banks)]
            turn[ring] += 1
            count[k] += 1
            out[job, b] = (k, count[k])
    return out


WEIGHTS_A = [("ident", 128), ("wq", 128), ("lng", 128), ("lnb", 128), ("vecs", 8), ("pw", 2), ("refs", 2),
             ("iota", 16), ("hm", 8), ("dw", 49), ("wv2", 256), ("mq", 128), ("mk", 128), ("mv", 128),
             ("mo", 128), ("mlp", 128), ("E0", 512)]
WEIGHTS_B = [("wqkv", 384), ("wproj", 128), ("Wq", 512), ("flng", 64), ("flnb", 64), ("downR", 512),
             ("upR", 512), ("qmask", 4), ("keys", 128), ("E1", H * N)]
ROWS = [("bq", 128), ("mvb", 128), ("mob", 128), ("mlpb", 128), ("bproj", 128), ("fbq", 512)]
VEC = {n: i for i, n in enumerate(["lng", "lnb", "bq", "bv", "dwb", "mqb", "mkb"])}


def offsets(parts):
    out, at = {}, 0
    for n, k in parts:
        out[n] = (at, k)
        at += k
    return out, at


def build(nc, x_in, wa_in, wb_in, rows_in, out):
    steps = schedule()
    jobs = place_jobs(steps)
    offA, NA = offsets(WEIGHTS_A)
    offB, NB = offsets(WEIGHTS_B)
    offR, NR = offsets(ROWS)

    ctx = ExitStack()
    with ctx:
        def sb(name, shape, dt=F32):
            return ctx.enter_context(nc.sbuf_tensor(name, [P] + list(shape), dt))

        def sem(name):
            return ctx.enter_context(nc.semaphore(name))

        wa = sb("wa", [NA])
        wb = sb("wb", [NB])
        rows = sb("rows", [NR])
        diag = sb("diag", [KS * KS, P])
        KB = sb("KB", [2 * 2 * NK])
        upM = sb("upM", [4, LO, C])
        mhalf = sb("mhalf", [16])
        ones = sb("ones", [P])

        def A(n):
            at, k = offA[n]
            return wa[:, at:at + k]

        def Bw(n):
            at, k = offB[n]
            return wb[:, at:at + k]

        def row(n):
            at, k = offR[n]
            return rows[0:1, at:at + k]

        def vec(n):
            at = offA["vecs"][0] + VEC[n]
            return wa[:, at:at + 1]

        ident = A("ident")
        hm = A("hm")

        x_sb = sb("x_sb", [B, NT, C])
        stats = sb("stats", [4, NT, 6])
        mv = sb("mv", [4, NT, 2])
        veps = sb("veps", [4, NT])
        rstd = sb("rstd", [4, NT])
        hat = sb("hat", [4, NT, C])
        xln = sb("xln", [NT, C])
        qpad = sb("qpad", [PADDED, PADDED])
        qT = sb("qT", [N])
        qhT = sb("qhT", [N])
        osb = sb("osb", [NP_])
        tanh_ = sb("tanh_", [2])
        crd = sb("crd", [3, 2])
        hatw = sb("hatw", [3, 2, SIDE])
        Wp = sb("Wp", [SIDE, SIDE])
        WTs = sb("WTs", [NT, NP_])
        ips = sb("ips", [C])
        vT = sb("vT", [2, NP_])
        khT = sb("khT", [NP_])
        vBD0 = sb("vBD0", [4, 2, DH + 1])
        negM = sb("negM", [NT, H])
        negMT = sb("negMT", [N])
        rec = sb("rec", [2, NT * H])
        att = sb("att", [2, NT, C])
        attT = sb("attT", [2, N])
        z = sb("z", [NT, C])
        zT = sb("zT", [N])
        gl = sb("gl", [NT, C])
        xg = gl
        t0 = sb("t0", [NT, C])
        tlT = sb("tlT", [N])
        q1T = sb("q1T", [N])
        k1T = sb("k1T", [N])
        vA = sb("vA", [NT, H, DH + 1])
        cent = sb("cent", [SEG])
        centBD = sb("centBD", [H, SEG])
        kBD1 = sb("kBD1", [H, N])
        rts = sb("rts", [NT * H, SEG + 4])
        rtm = sb("rtm", [NT * H, SEG + 4])
        r8 = sb("r8", [NT * H, 8])
        segmax = sb("segmax", [NT * H, SEG])
        pen = sb("pen", [NT * H, SEG])
        sel = sb("sel", [NT * H, SEG])
        selM = sb("selM", [NT * H])
        bias = sb("bias", [NT * H, SEG])
        biasT = sb("biasT", [N])
        late = sb("late", [H * 2 * N])
        PT1 = late[:, :].rearrange("p (h k n) -> p h k n", h=H, k=2)
        kBD0 = late[:, 0:H * NP_].rearrange("p (h k) -> p h k", h=H)
        PT0 = late[:, H * NP_:H * NP_ + 4 * N].rearrange("p (a n) -> p a n", a=4)
        t1 = sb("t1", [2, NT, C])
        fT = sb("fT", [2, N])
        onehot = sb("onehot", [HI * NCH * N], F16)
        OH = onehot[:, :].rearrange("p (n q v g) -> p n q v g", n=NCH * NT, q=4, v=HI)
        early = onehot[:, :].bitcast(F32)
        Q = NT * H * QD

        def early_part(i, n):
            return early[:, i * Q:i * Q + n]
        sq = early_part(0, Q).rearrange("p (t n) -> p t n", t=NT)
        qn = early_part(1, Q).rearrange("p (t n) -> p t n", t=NT)
        qf = early_part(2, Q).rearrange("p (t n) -> p t n", t=NT)
        qsT = early_part(3, Q).rearrange("p (t c n) -> p t c n", t=NT, c=4)
        S = early_part(4, 2 * Q).rearrange("p (t g e) -> p t g e", t=NT, g=2 * H)
        Sx = early_part(6, 2 * Q).rearrange("p (t g e) -> p t g e", t=NT, g=2 * H)
        qg = qn
        qs = qn
        ssq = sb("ssq", [NT, 2, 2 * H])
        inv = sb("inv", [NT, 2, 2 * H])
        v16 = sb("v16", [NT * H, 2, TOP])
        i16 = sb("i16", [NT * H, 2, TOP], U16)
        act_store = sb("act_store", [2 * NT * H * 2 * TOP])
        act = act_store[:, :].rearrange("p (t g q l) -> p t g q l", t=NT, g=32, q=4)
        if_, ab = (act_store[:, i * NT * H * 2 * TOP:(i + 1) * NT * H * 2 * TOP].rearrange(
            "p (g a k) -> p g a k", g=NT * H, a=2) for i in range(2))
        dv = ab
        cands = sb("cands", [2 * NT * H * CELLS])
        cand, candx = (cands[:, i * NT * H * CELLS:(i + 1) * NT * H * CELLS].rearrange(
            "p (g c) -> p g c", g=NT * H) for i in range(2))
        candm = cand
        lom = cands[:, 0:LO * NCH * N // 2].bitcast(F16).rearrange("p (l n) -> p l n", l=LO)
        c8 = sb("c8", [NT * H, 2, 8])
        weights = sb("weights", [LO * NCH * N])
        we = weights[:, 0:2 * NT * H * CELLS].rearrange("p (a g c) -> p a g c", a=2, g=NT * H)
        R = weights[:, :].bitcast(F16).rearrange("p (s l n) -> p s l n", s=2, l=LO)
        masked = sb("masked", [NT * 32 * 2 * 4 * LO])
        prod = masked[:, :].rearrange("p (t g s e) -> p t g s e", t=NT, g=32, s=2)
        wem = masked[:, 0:2 * NT * H * CELLS].rearrange("p (a g c) -> p a g c", a=2, g=NT * H)
        zs = sb("zs", [3, NT * H])
        slots = sb("slots", [2, NT * H, SLOTS])
        wn = sb("wn", [NT * H, SLOTS])
        W2 = sb("W2", [2, NCH * N], F16)
        eT = sb("eT", [3, NCH * N], U16)
        YTs = sb("YTs", [N])
        outs = sb("outs", [NT, C])
        ksq = sb("ksq", [P])
        kss = sb("kss", [3, 4])
        kn = sb("kn", [P])
        wmean = sb("wmean", [2, H])
        WqC = Bw("Wq")
        rowC = rows[:, offR["fbq"][0]:offR["fbq"][0] + H * QD]

        psum = [ctx.enter_context(nc.psum_tensor(f"bank{k}", [P, 512], F32)) for k in range(8)]

        bank_full = [sem(f"bank_full{k}") for k in range(8)]
        bank_free = [sem(f"bank_free{k}") for k in range(8)]
        x_loaded = [sem(f"x_loaded{b}") for b in range(B)]
        wa_loaded = sem("wa_loaded")
        wb_loaded = sem("wb_loaded")
        rows_loaded = sem("rows_loaded")
        preset = sem("preset")
        diag_ready = sem("diag_ready")
        var_ready = [sem(f"var_ready{k}") for k in range(4)]
        rstd_ready = [sem(f"rstd_ready{k}") for k in range(4)]
        hat_ready = [sem(f"hat_ready{k}") for k in range(4)]
        xln_ready = sem("xln_ready")
        hatw_ready = sem("hatw_ready")
        kbd0_ready = sem("kbd0_ready")
        negm_ready = sem("negm_ready")
        gl_ready = sem("gl_ready")
        t0_ready = sem("t0_ready")
        centbd_ready = sem("centbd_ready")
        kbd1_ready = sem("kbd1_ready")
        bias_ready = sem("bias_ready")
        kss_ready = sem("kss_ready")
        kinv_ready = sem("kinv_ready")
        kn_ready = sem("kn_ready")
        KB_ready = sem("KB_ready")
        WqC_ready = sem("WqC_ready")
        upM_ready = sem("upM_ready")
        sq_ready = sem("sq_ready")
        qvar_ready = sem("qvar_ready")
        qrstd_ready = sem("qrstd_ready")
        qf_ready = sem("qf_ready")
        sq2_ready = sem("sq2_ready")
        qss_ready = sem("qss_ready")
        qinv_ready = sem("qinv_ready")
        qs_ready = sem("qs_ready")
        v16_ready = sem("v16_ready")
        i16_ready = sem("i16_ready")
        dv_ready = sem("dv_ready")
        ab_ready = sem("ab_ready")
        if_ready = sem("if_ready")
        we_ready = sem("we_ready")
        wem_ready = sem("wem_ready")
        slots_ready = sem("slots_ready")
        eT_ready = sem("eT_ready")
        onehot_dve_ready = sem("onehot_dve_ready")
        onehot_pool_ready = sem("onehot_pool_ready")
        act_ready = sem("act_ready")
        out_ready = sem("out_ready")
        out_stored = sem("out_stored")
        dve_chain = sem("dve_chain")
        act_chain = sem("act_chain")
        pool_chain = sem("pool_chain")

        def full(eng, job, b):
            k, n = jobs[job, b]
            eng.wait_ge(bank_full[k], n)
            return psum[k]

        def freed(ins, job, b):
            ins.then_inc(bank_free[jobs[job, b][0]], 1)

        def read_out(eng, job, b):
            k, n = jobs[job, b]
            eng.wait_ge(bank_free[k], n)

        def chained(eng, semaphore):
            count = [0]

            def link(ins):
                count[0] += 1
                ins.then_inc(semaphore, 1)
                eng.wait_ge(semaphore, count[0])
            return link

        def front_buffers_free(eng, b):
            if b >= 1:
                read_out(eng, "fT", b - 1)

        def stored(eng, b, back):
            if b >= back:
                eng.wait_ge(out_stored, 16 * (b - back + 1))

        def hi_view(e):
            return e[0:KC, 2, :].rearrange("p (n q g) -> p n q g", n=NCH * NT, q=4)

        block = ctx.enter_context(nc.Block())

        @block.sync
        def _(sp):
            sp.dma_start(x_sb[:, 0, :, :], x_in[0]).then_inc(x_loaded[0], 16)
            sp.dma_start(wa[:, :], wa_in).then_inc(wa_loaded, 16)
            sp.dma_start(rows[0:1, :], rows_in).then_inc(rows_loaded, 16)
            for b in range(1, B):
                sp.dma_start(x_sb[:, b, :, :], x_in[b]).then_inc(x_loaded[b], 16)
            sp.dma_start(wb[:, :], wb_in).then_inc(wb_loaded, 16)
            for b in range(B):
                sp.wait_ge(out_ready, b + 1)
                sp.dma_start(out[b], outs[:, :, :]).then_inc(out_stored, 16)
            sp.wait_ge(out_stored, 16 * B)

        @block.tensor
        def _(pe):
            def take(job, b):
                k, n = jobs[job, b]
                if n > 1:
                    pe.wait_ge(bank_free[k], n - 1)
                return psum[k]

            def done(ins, job, b):
                ins.then_inc(bank_full[jobs[job, b][0]], 1)

            def transposes(job, b, pairs):
                o = take(job, b)
                for at, src in pairs:
                    k, m = src.shape
                    last = nc.tensor.transpose(o[0:m, at:at + k], src, ident[0:k, 0:k])
                done(last, job, b)

            mm = nc.tensor.matmul

            def F0(b):
                pass

            def F1(b):
                p = b % 2
                if b == 0:
                    pe.wait_ge(wa_loaded, 16)
                    pe.wait_ge(rows_loaded, 16)
                    pe.wait_ge(preset, 1)
                pe.wait_ge(xln_ready, b + 1)
                o = take("qimg", b)
                for s in range(NT):
                    c = slice(s * P, s * P + P)
                    mm(o[:, c], xln[:, s, :], A("wq"), start=True, stop=False)
                    last = mm(o[:, c], ones[0:1, :], row("bq"), start=False, stop=True)
                done(last, "qimg", b)
                o = take("qT", b)
                last = mm(o[:, 0:N], A("wq"), xln[:, :, :], start=True, stop=True)
                done(last, "qT", b)
                read_out(pe, "qT", b)
                o = take("qhT", b)
                done(mm(o[:, 0:N], A("mq"), qT[:, :], start=True, stop=True), "qhT", b)

            def F2(b):
                p = b % 2
                if b == 0:
                    pe.wait_ge(diag_ready, 1)
                read_out(pe, "qimg", b)
                o = take("conv", b)
                for tap in range(KS * KS):
                    ky, kx = tap // KS, tap % KS
                    last = mm(o[:, 0:NP_], diag[:, tap, :], qpad[:, ky:ky + 15:2, kx:kx + 15:2],
                              start=(tap == 0), stop=(tap == KS * KS - 1))
                done(last, "conv", b)
                read_out(pe, "conv", b)
                o = take("offs", b)
                done(mm(o[0:NP_, 0:2], osb[:, :], A("pw"), start=True, stop=True), "offs", b)

            def F3(b):
                p = b % 2
                pe.wait_ge(hatw_ready, b + 1)
                Wf = Wp[0:NP_, :, :].rearrange("p a b -> p (a b)")
                transposes("WT", b, [(s * NP_, Wf[:, s * P:s * P + P]) for s in range(NT)])
                read_out(pe, "WT", b)
                o = take("interp", b)
                for s in range(NT):
                    last = mm(o[0:NP_, 0:C], WTs[:, s, :], x_sb[:, b, s, :], start=(s == 0), stop=(s == NT - 1))
                done(last, "interp", b)
                read_out(pe, "interp", b)
                o = take("vT", b)
                wv2 = A("wv2").rearrange("p (u n) -> p u n", u=2)
                for u in range(2):
                    last = mm(o[:, 0:NP_], wv2[0:NP_, u, :], ips[0:NP_, u:C:2], start=(u == 0), stop=(u == 1))
                done(last, "vT", b)

            def F4(b):
                p = b % 2
                read_out(pe, "vT", b)
                o = take("kh", b)
                done(mm(o[:, 0:NP_], A("mk"), vT[:, 0, :], start=True, stop=True), "kh", b)
                o = take("vh", b)
                mm(o[:, 0:C], vT[:, :, :], A("mv"), start=True, stop=False)
                done(mm(o[:, 0:C], ones[0:1, :], row("mvb"), start=False, stop=True), "vh", b)

            def F5(b):
                p = b % 2
                read_out(pe, "qhT", b)
                pe.wait_ge(kbd0_ready, b + 1)
                for t in range(NT):
                    o = take(f"S0_{t}", b)
                    done(mm(o[:, :], qhT[:, t * P:t * P + P], kBD0[:, :, :], start=True, stop=True),
                         f"S0_{t}", b)
                pe.wait_ge(negm_ready, b + 1)
                transposes("mT", b, [(t * P, negM[:, t, :]) for t in range(NT)])
                read_out(pe, "mT", b)
                E0 = A("E0")
                for j in range(2):
                    o = take(f"P0_{j}", b)
                    for i in range(2):
                        hp = 2 * j + i
                        mm(o[:, i * N:i * N + N], kBD0[:, 2 * hp:2 * hp + 2, :], qhT[:, :],
                           start=True, stop=False)
                        last = mm(o[:, i * N:i * N + N], E0[0:H, hp * P:hp * P + P], negMT[0:H, :],
                                  start=False, stop=True)
                    done(last, f"P0_{j}", b)

            def F6(b):
                p = b % 2
                read_out(pe, "P0_0", b)
                read_out(pe, "P0_1", b)
                read_out(pe, "vh", b)
                o = take("O0", b)
                for t in range(NT):
                    for hp in range(4):
                        at = (t * H + 2 * hp) * (DH + 1)
                        last = mm(o[:, at:at + 2 * (DH + 1)], PT0[:, hp, t * P:t * P + P], vBD0[:, hp, :, :],
                                  start=True, stop=True)
                done(last, "O0", b)
                read_out(pe, "O0", b)
                transposes("aT", b, [(t * P, att[:, 0, t, :]) for t in range(NT)])
                read_out(pe, "aT", b)
                o = take("msa", b)
                for t in range(NT):
                    c = slice(t * P, t * P + P)
                    mm(o[:, c], attT[:, 0, c], A("mo"), start=True, stop=False)
                    last = mm(o[:, c], ones[0:1, :], row("mob"), start=False, stop=True)
                done(last, "msa", b)

            def F7(b):
                p = b % 2
                pe.wait_ge(hat_ready[1], b + 1)
                transposes("zT", b, [(t * P, hat[:, 1, t, :]) for t in range(NT)])
                read_out(pe, "zT", b)
                o = take("mlp", b)
                for t in range(NT):
                    c = slice(t * P, t * P + P)
                    mm(o[:, c], zT[:, c], A("mlp"), start=True, stop=False)
                    last = mm(o[:, c], ones[0:1, :], row("mlpb"), start=False, stop=True)
                done(last, "mlp", b)

            def F8(b):
                p = b % 2
                if b == 0:
                    pe.wait_ge(wb_loaded, 16)
                pe.wait_ge(hat_ready[2], b + 1)
                transposes("tT", b, [(t * P, hat[:, 2, t, :]) for t in range(NT)])
                read_out(pe, "tT", b)
                wqkv = Bw("wqkv")
                for i, job in ((0, "q1"), (1, "k1")):
                    o = take(job, b)
                    done(mm(o[:, 0:N], wqkv[:, i * P:i * P + P], tlT[:, :], start=True, stop=True), job, b)
                o = take("v1", b)
                for t in range(NT):
                    c = slice(t * P, t * P + P)
                    last = mm(o[:, c], tlT[:, c], wqkv[:, 2 * P:3 * P], start=True, stop=True)
                done(last, "v1", b)

            def F9(b):
                p = b % 2
                read_out(pe, "q1", b)
                pe.wait_ge(centbd_ready, b + 1)
                o = take("route", b)
                for t in range(NT):
                    c = slice(t * P, t * P + P)
                    last = mm(o[:, c], q1T[:, c], centBD[:, :, :], start=True, stop=True)
                done(last, "route", b)
                pe.wait_ge(kbd1_ready, b + 1)
                for t in range(NT):
                    for i in range(4):
                        job = f"S1_{t}{i}"
                        o = take(job, b)
                        done(mm(o[:, :], q1T[:, t * P:t * P + P], kBD1[:, 2 * i:2 * i + 2, :],
                                start=True, stop=True), job, b)
                pe.wait_ge(bias_ready, b + 1)
                transposes("bT", b, [(t * P, bias[:, t * H:t * H + H, :].rearrange("p h s -> p (h s)"))
                                     for t in range(NT)])

            def F10(b):
                p = b % 2
                read_out(pe, "bT", b)
                E1 = Bw("E1").rearrange("p (h k) -> p h k", h=H)
                for h in range(H):
                    job = f"P1_{h}"
                    o = take(job, b)
                    for kc in range(NT):
                        k = slice(kc * P, kc * P + P)
                        mm(o[:, kc * N:kc * N + N], kBD1[:, h, k], q1T[:, :], start=True, stop=False)
                        last = mm(o[:, kc * N:kc * N + N], E1[:, h, k], biasT[:, :], start=False, stop=True)
                    done(last, job, b)

            def F11(b):
                p = b % 2
                read_out(pe, "v1", b)
                o = take("O1", b)
                for h in range(H):
                    read_out(pe, f"P1_{h}", b)
                    for t in range(NT):
                        at = (t * H + h) * (DH + 1)
                        for kc in range(NT):
                            last = mm(o[:, at:at + DH + 1], PT1[:, h, kc, t * P:t * P + P], vA[:, kc, h, :],
                                      start=(kc == 0), stop=(kc == NT - 1))
                done(last, "O1", b)
                read_out(pe, "O1", b)
                transposes("a1T", b, [(t * P, att[:, 1, t, :]) for t in range(NT)])
                read_out(pe, "a1T", b)
                o = take("proj", b)
                for t in range(NT):
                    c = slice(t * P, t * P + P)
                    mm(o[:, c], attT[:, 1, c], Bw("wproj"), start=True, stop=False)
                    last = mm(o[:, c], ones[0:1, :], row("bproj"), start=False, stop=True)
                done(last, "proj", b)
                pe.wait_ge(hat_ready[3], b + 1)
                transposes("fT", b, [(t * P, hat[:, 3, t, :]) for t in range(NT)])

            def NS(b):
                pe.wait_ge(kn_ready, 1)
                transposes("keys", b, [(0, kn[0:NK, :])])

            def N0(b):
                p = b % 2
                if b == 0:
                    pe.wait_ge(WqC_ready, 2)
                read_out(pe, "fT", b)
                for t in range(NT):
                    o = take(f"Q{t}", b)
                    mm(o[:, :], fT[:, p, t * P:t * P + P], WqC[:, :], start=True, stop=False)
                    done(mm(o[:, :], ones[0:1, :], rowC[0:1, :], start=False, stop=True), f"Q{t}", b)
                if b == 0:
                    pe.wait_ge(KB_ready, 1)
                for t in range(NT):
                    pe.wait_ge(qs_ready, NT * b + t + 1)
                    transposes(f"qsT{t}", b, [(c * P, qs[:, t, c * P:c * P + P]) for c in range(4)])
                    read_out(pe, f"qsT{t}", b)
                    for j in range(2):
                        o = take(f"S2_{t}{j}", b)
                        for i in range(2):
                            last = mm(o[:, i * 256:i * 256 + 256], qsT[:, t, 2 * j + i, :], KB[:, :],
                                      start=True, stop=True)
                        done(last, f"S2_{t}{j}", b)

            def N1(b):
                pass

            def N2(b):
                pass

            def N3(b):
                pe.wait_ge(slots_ready, b + 1)
                for job, src in (("wT", wn[:, :, :]), ("eT", slots[:, 1, :, :])):
                    transposes(job, b, [((c * NT + t) * P,
                                         src[:, t * H + c * HC:t * H + (c + 1) * HC, :].rearrange("p h s -> p (h s)"))
                                        for c in range(NCH) for t in range(NT)])

            def N4(b):
                p = b % 2
                downR = Bw("downR").rearrange("p (l m) -> p l m", l=LO)
                for j in range(2):
                    o = take(f"I{j}", b)
                    for i in range(2):
                        last = mm(o[:, i * N:i * N + N], downR[:, 2 * j + i, :], fT[:, p, :], start=True, stop=True)
                    done(last, f"I{j}", b)

            def N5(b):
                pe.wait_ge(onehot_dve_ready, b + 1)
                pe.wait_ge(onehot_pool_ready, b + 1)
                OHv = OH[0:KC, :, :, :, :].rearrange("p n q v g -> p n g (q v)")
                Rv = R[0:KC, :, :, :].rearrange("p s l (c t q g) -> p c t g s q l", c=NCH, t=NT, g=32)
                for t in range(NT):
                    for j in range(2):
                        o = take(f"G{t}{j}", b)
                        for g in range(16):
                            for c in range(NCH):
                                last = mm(o[:, g * 32:g * 32 + 32], OHv[:, c * NT + t, 16 * j + g], Rv[:, c, t, 16 * j + g],
                                          start=(c == 0), stop=(c == NCH - 1))
                        done(last, f"G{t}{j}", b)

            def N6(b):
                if b == 0:
                    pe.wait_ge(upM_ready, 1)
                for t in range(NT):
                    for j in range(2):
                        read_out(pe, f"G{t}{j}", b)
                o = take("Y", b)
                ov = o[:, 0:N].rearrange("p (t q g) -> p t q g", t=NT, q=4)
                for q in range(4):
                    for lo in range(LO):
                        for s in range(2):
                            last = mm(ov[:, :, q, :], upM[:, q, lo, :], prod[:, :, :, s, q * LO + lo],
                                      start=(lo == 0 and s == 0), stop=(lo == LO - 1 and s == 1))
                done(last, "Y", b)
                read_out(pe, "Y", b)
                transposes("YT", b, [(t * P, YTs[:, t * P:t * P + P]) for t in range(NT)])

            do = {"F0": F0, "F1": F1, "F2": F2, "F3": F3, "F4": F4, "F5": F5, "F6": F6, "F7": F7, "F8": F8,
                  "F9": F9, "F10": F10, "F11": F11, "NS": NS, "N0": N0, "N1": N1, "N2": N2, "N3": N3, "N4": N4,
                  "N5": N5, "N6": N6}
            for s, b in steps:
                do[s](b)

        @block.scalar
        def _(ac):
            fn = nc.scalar.activation
            link = chained(ac, act_chain)

            def F0(b):
                front_buffers_free(ac, b)

            def F1(b):
                p = b % 2
                if b == 0:
                    ac.wait_ge(wa_loaded, 16)
                    ac.wait_ge(preset, 1)
                o = full(ac, "qimg", b)
                inner = qpad[:, 3:3 + SIDE, 3:3 + SIDE]
                freed(fn(inner, o[:, 0:N].rearrange("p (a b) -> p a b", b=SIDE), ACT.Identity), "qimg", b)
                o = full(ac, "qT", b)
                freed(fn(qT[:, :].rearrange("p (c s) -> p s c", s=2),
                         o[:, 0:N].rearrange("p (s c) -> p s c", s=2), ACT.Identity, bias=vec("bq")), "qT", b)
                o = full(ac, "qhT", b)
                freed(fn(qhT[:, :], o[:, 0:N], ACT.Identity, bias=vec("mqb")), "qhT", b)

            def F2(b):
                p = b % 2
                o = full(ac, "conv", b)
                freed(fn(osb[:, :], o[:, 0:NP_], ACT.Gelu, bias=vec("dwb")), "conv", b)
                o = full(ac, "offs", b)
                freed(fn(tanh_[0:NP_, :], o[0:NP_, 0:2], ACT.Tanh), "offs", b)

            def F3(b):
                p = b % 2
                o = full(ac, "WT", b)
                freed(fn(WTs[:, :, :], o[:, 0:NT * NP_].rearrange("p (s n) -> p s n", s=NT), ACT.Identity), "WT", b)
                o = full(ac, "interp", b)
                freed(fn(ips[0:NP_, :], o[0:NP_, 0:C], ACT.Identity), "interp", b)
                o = full(ac, "vT", b)
                freed(fn(vT[:, :, :], o[:, 0:NP_].unsqueeze(1).broadcast_to([P, 2, NP_]), ACT.Identity,
                         bias=vec("bv")), "vT", b)

            def F4(b):
                p = b % 2
                o = full(ac, "kh", b)
                freed(fn(khT[:, :], o[:, 0:NP_], ACT.Identity, bias=vec("mkb")), "kh", b)
                o = full(ac, "vh", b)
                for r in range(2):
                    q = slice(NP_ * r, NP_ * r + NP_)
                    last = fn(vBD0[q, :, r, 0:DH],
                              o[q, 0:C].rearrange("p (a r d) -> p a r d", a=4, r=2)[:, :, r, :], ACT.Identity)
                freed(last, "vh", b)

            def F5(b):
                p = b % 2
                o = full(ac, "mT", b)
                freed(fn(negMT[0:H, :], o[0:H, 0:N], ACT.Identity), "mT", b)
                for j in range(2):
                    o = full(ac, f"P0_{j}", b)
                    freed(fn(PT0[:, 2 * j:2 * j + 2, :], o[:, :].rearrange("p (i n) -> p i n", i=2), ACT.Exp),
                          f"P0_{j}", b)

            def F6(b):
                p = b % 2
                o = full(ac, "aT", b)
                freed(fn(attT[:, 0, :], o[:, 0:N], ACT.Identity), "aT", b)

            def F7(b):
                p = b % 2
                o = full(ac, "zT", b)
                freed(fn(zT[:, :], o[:, 0:N], ACT.Identity, bias=vec("lnb"), scale=vec("lng")), "zT", b)
                o = full(ac, "mlp", b)
                freed(fn(gl[:, :, :], o[:, 0:N].rearrange("p (t c) -> p t c", t=NT), ACT.Gelu), "mlp", b)

            def F8(b):
                p = b % 2
                o = full(ac, "tT", b)
                freed(fn(tlT[:, :], o[:, 0:N], ACT.Identity), "tT", b)
                o = full(ac, "q1", b)
                freed(fn(q1T[:, :], o[:, 0:N], ACT.Identity), "q1", b)
                o = full(ac, "k1", b)
                freed(fn(k1T[:, :], o[:, 0:N], ACT.Identity), "k1", b)
                o = full(ac, "v1", b)
                freed(fn(vA[:, :, :, 0:DH], o[:, 0:N].rearrange("p (t h d) -> p t h d", t=NT, h=H), ACT.Identity),
                      "v1", b)

            def F9(b):
                p = b % 2
                o = full(ac, "route", b)
                freed(fn(rts[:, :, 0:SEG], o[:, 0:N].rearrange("p (g s) -> p g s", s=SEG), ACT.Identity),
                      "route", b)
                o = full(ac, "bT", b)
                freed(fn(biasT[:, :], o[:, 0:N], ACT.Identity), "bT", b)

            def F10(b):
                if b >= 1:
                    full(ac, "O1", b - 1)
                for h in range(H):
                    o = full(ac, f"P1_{h}", b)
                    freed(fn(PT1[:, h, :, :], o[:, :].rearrange("p (k n) -> p k n", k=NT), ACT.Exp,
                             scale=DH ** -0.5), f"P1_{h}", b)

            def F11(b):
                p = b % 2
                o = full(ac, "a1T", b)
                freed(fn(attT[:, 1, :], o[:, 0:N], ACT.Identity), "a1T", b)
                stored(ac, b, 2)
                o = full(ac, "fT", b)
                freed(fn(fT[:, p, :], o[:, 0:N], ACT.Identity), "fT", b)

            def NS(b):
                pass

            def N0(b):
                for t in range(NT):
                    o = full(ac, f"Q{t}", b)
                    if b >= 1:
                        ac.wait_ge(qss_ready, NT * b)
                    fn(sq[:, t, :], o[:, :], ACT.Square).then_inc(sq_ready, 1)
                for t in range(NT):
                    ac.wait_ge(qf_ready, NT * b + t + 1)
                    ac.wait_ge(qvar_ready, NT * b + t + 1)
                    fn(sq[:, t, :], qf[:, t, :], ACT.Square).then_inc(sq2_ready, 1)
                for t in range(NT):
                    o = full(ac, f"qsT{t}", b)
                    freed(fn(qsT[:, t, :, :], o[:, :].rearrange("p (c n) -> p c n", c=4), ACT.Identity),
                          f"qsT{t}", b)
                    for j in range(2):
                        o = full(ac, f"S2_{t}{j}", b)
                        freed(fn(S[:, t, 8 * j:8 * j + 8, :], o[:, :].rearrange("p (l e) -> p l e", e=NK),
                                 ACT.Identity), f"S2_{t}{j}", b)

            def N1(b):
                pass

            def N2(b):
                p = b % 2
                if b >= 1:
                    read_out(ac, "G11", b - 1)
                ac.wait_ge(i16_ready, b + 1)
                fn(if_[:, :, :, :], i16[:, :, :, :], ACT.Copy).then_inc(if_ready, 1)
                ac.wait_ge(dv_ready, b + 1)
                fn(ab[:, :, :, :], dv[:, :, :, :], ACT.Exp).then_inc(ab_ready, 1)

            def N3(b):
                if b >= 1:
                    ac.wait_ge(onehot_dve_ready, b)
                    ac.wait_ge(onehot_pool_ready, b)
                o = full(ac, "wT", b)
                link(fn(W2[0:KC, 0, :], o[0:KC, :], ACT.Copy))
                o = full(ac, "eT", b)
                freed(fn(eT[0:KC, 0, :], o[0:KC, :], ACT.Copy), "eT", b)

            def N4(b):
                if b >= 1:
                    read_out(ac, "G11", b - 1)
                for j in range(2):
                    o = full(ac, f"I{j}", b)
                    for i in range(2):
                        for t in range(NT):
                            src = o[:, i * N + t * P:i * N + t * P + P].rearrange("p (q g) -> p g q", q=4)
                            last = fn(act[:, t, :, :, 2 * j + i], src, ACT.Gelu)
                    freed(last, f"I{j}", b)

            def N5(b):
                pass

            def N6(b):
                o = full(ac, "Y", b)
                freed(fn(YTs[:, :], o[:, 0:N], ACT.Identity), "Y", b)

            do = {"F0": F0, "F1": F1, "F2": F2, "F3": F3, "F4": F4, "F5": F5, "F6": F6, "F7": F7, "F8": F8,
                  "F9": F9, "F10": F10, "F11": F11, "NS": NS, "N0": N0, "N1": N1, "N2": N2, "N3": N3, "N4": N4,
                  "N5": N5, "N6": N6}
            for s, b in steps:
                do[s](b)

        @block.vector
        def _(dve):
            v = nc.vector
            link = chained(dve, dve_chain)

            def layernorm(k, src, b):
                p = b % 2
                for t in range(NT):
                    last = v.bn_stats(stats[:, k, t, :], src[:, t, :])
                link(last)
                for t in range(NT):
                    last = v.bn_aggr(mv[:, k, t, :], stats[:, k, t, :])
                link(last)
                v.tensor_scalar(veps[:, k, :], mv[:, k, :, 1], LN_EPS, None, ALU.add).then_inc(var_ready[k], 1)
                dve.wait_ge(rstd_ready[k], b + 1)
                for t in range(NT):
                    last = v.tensor_scalar(hat[:, k, t, :], src[:, t, :], mv[:, k, t, 0:1],
                                           rstd[:, k, t:t + 1], ALU.subtract, ALU.mult)
                last.then_inc(hat_ready[k], 1)

            def F0(b):
                front_buffers_free(dve, b)
                dve.wait_ge(x_loaded[b], 16)
                layernorm(0, x_sb[:, b, :, :], b)
                if b == 0:
                    dve.wait_ge(wa_loaded, 16)
                    v.tensor_tensor(diag[:, :, :], ident.unsqueeze(1).broadcast_to([P, KS * KS, P]),
                                    A("dw").unsqueeze(2).broadcast_to([P, KS * KS, P]),
                                    ALU.mult).then_inc(diag_ready, 1)

            def F1(b):
                pass

            def F2(b):
                pass

            def F3(b):
                p = b % 2
                n = slice(0, NP_)
                read_out(dve, "offs", b)
                link(v.tensor_tensor(crd[n, 0, :], tanh_[n, :], A("refs")[n, :], ALU.add))
                link(v.tensor_scalar(crd[n, 1, :], crd[n, 0, :], 1.0, 4.0, ALU.add, ALU.mult))
                link(v.tensor_scalar(crd[n, 2, :], crd[n, 1, :], 1.0, 0.5 * (SIDE - 1), ALU.add, ALU.mult))
                link(v.tensor_tensor(hatw[n, 0, :, :], A("iota")[n, :].unsqueeze(1).broadcast_to([NP_, 2, SIDE]),
                                     crd[n, 2, :].unsqueeze(2).broadcast_to([NP_, 2, SIDE]), ALU.subtract))
                link(v.scalar_tensor_tensor(hatw[n, 1, :, :], hatw[n, 0, :, :], -1.0, hatw[n, 0, :, :],
                                            ALU.mult, ALU.min))
                link(v.tensor_scalar(hatw[n, 2, :, :], hatw[n, 1, :, :], 1.0, 0.0, ALU.add, ALU.max))
                v.tensor_tensor(Wp[n, :, :], hatw[n, 2, 1, :].unsqueeze(2).broadcast_to([NP_, SIDE, SIDE]),
                                hatw[n, 2, 0, :].unsqueeze(1).broadcast_to([NP_, SIDE, SIDE]),
                                ALU.mult).then_inc(hatw_ready, 1)

            def F4(b):
                p = b % 2
                read_out(dve, "kh", b)
                v.tensor_tensor(kBD0[:, :, :], khT[:, :].unsqueeze(1).broadcast_to([P, H, NP_]),
                                hm.unsqueeze(2).broadcast_to([P, H, NP_]), ALU.mult).then_inc(kbd0_ready, 1)

            def F5(b):
                p = b % 2
                for t in range(NT):
                    o = full(dve, f"S0_{t}", b)
                    freed(v.tensor_reduce(negM[:, t, :], o[:, :].rearrange("p (h k) -> p h k", h=H), X, ALU.max,
                                          negate=True), f"S0_{t}", b)
                for t in range(NT):
                    read_out(dve, f"S0_{t}", b)
                v.engine_nop().then_inc(negm_ready, 1)

            def normalize(job, k, b):
                p = b % 2
                o = full(dve, job, b)
                ov = o[:, 0:NT * H * (DH + 1)].rearrange("p (g d) -> p g d", d=DH + 1)
                link(v.reciprocal(rec[:, k, :], ov[:, :, DH]))
                freed(v.tensor_tensor(att[:, k, :, :].rearrange("p t (h d) -> p (t h) d", d=DH), ov[:, :, 0:DH],
                                      rec[:, k, :].unsqueeze(2).broadcast_to([P, NT * H, DH]), ALU.mult), job, b)

            def F6(b):
                p = b % 2
                normalize("O0", 0, b)
                o = full(dve, "msa", b)
                freed(v.tensor_tensor(z[:, :, :], o[:, 0:N].rearrange("p (t c) -> p t c", t=NT),
                                      x_sb[:, b, :, :], ALU.add), "msa", b)
                read_out(dve, "msa", b)
                layernorm(1, z[:, :, :], b)

            def F7(b):
                p = b % 2
                read_out(dve, "mlp", b)
                v.tensor_tensor(t0[:, :, :], gl[:, :, :], z[:, :, :], ALU.add).then_inc(t0_ready, 1)
                dve.wait_ge(t0_ready, b + 1)
                layernorm(2, t0[:, :, :], b)

            def F8(b):
                p = b % 2
                read_out(dve, "k1", b)
                link(v.tensor_reduce(cent[:, :], k1T[:, :].rearrange("p (s n) -> p s n", n=SEG), X, ALU.add))
                v.tensor_tensor(centBD[:, :, :], cent[:, :].unsqueeze(1).broadcast_to([P, H, SEG]),
                                hm.unsqueeze(2).broadcast_to([P, H, SEG]), ALU.mult).then_inc(centbd_ready, 1)

            def F9(b):
                p = b % 2
                read_out(dve, "route", b)
                for g in range(NT * H):
                    last = v.max(r8[:, g, :], rts[:, g, :])
                link(last)
                for g in range(NT * H):
                    last = v.match_replace(rtm[:, g, :], r8[:, g, :], rts[:, g, :], MARK)
                link(last)
                v.tensor_scalar(pen[:, :, :], rtm[:, :, 0:SEG], 0.5 * MARK, HIDE, ALU.is_gt, ALU.mult)
                for t in range(NT):
                    for i in range(4):
                        job = f"S1_{t}{i}"
                        o = full(dve, job, b)
                        freed(v.tensor_reduce(segmax[:, t * H + 2 * i:t * H + 2 * i + 2, :],
                                              o[:, :].rearrange("p (g n) -> p g n", n=SEG), X, ALU.max), job, b)
                read_out(dve, "S1_13", b)
                link(v.tensor_tensor(sel[:, :, :], segmax[:, :, :], pen[:, :, :], ALU.add))
                link(v.tensor_reduce(selM[:, :], sel[:, :, :], X, ALU.max))
                v.tensor_tensor(bias[:, :, :], pen[:, :, :],
                                selM[:, :].unsqueeze(2).broadcast_to([P, NT * H, SEG]),
                                ALU.subtract).then_inc(bias_ready, 1)

            def F10(b):
                pass

            def F11(b):
                p = b % 2
                stored(dve, b, 2)
                normalize("O1", 1, b)
                o = full(dve, "proj", b)
                freed(v.tensor_tensor(t1[:, p, :, :], o[:, 0:N].rearrange("p (t c) -> p t c", t=NT),
                                      t0[:, :, :], ALU.add), "proj", b)
                read_out(dve, "proj", b)
                layernorm(3, t1[:, p, :, :], b)

            def NS(b):
                k = slice(0, NK)
                dve.wait_ge(wb_loaded, 16)
                dve.wait_ge(rows_loaded, 16)
                keys = Bw("keys")
                link(v.tensor_tensor(ksq[k, :], keys[k, :], keys[k, :], ALU.mult))
                link(v.tensor_reduce(kss[k, 0, :], ksq[k, :].rearrange("p (a d) -> p a d", a=4), X, ALU.add))
                v.tensor_scalar(kss[k, 1, :], kss[k, 0, :], 1e-24, None, ALU.max).then_inc(kss_ready, 1)
                dve.wait_ge(kinv_ready, 1)
                v.tensor_tensor(kn[k, :].rearrange("p (a d) -> p a d", a=4),
                                keys[k, :].rearrange("p (a d) -> p a d", a=4),
                                kss[k, 2, :].unsqueeze(2).broadcast_to([NK, 4, 32]), ALU.mult).then_inc(kn_ready, 1)
                for i, (src, dst, n) in enumerate(((Bw("Wq"), WqC, P), (row("fbq"), rowC, 1))):
                    sv = src.rearrange("p (h q) -> p h q", h=H)
                    link(v.tensor_reduce(wmean[0:n, i, :], sv, X, ALU.add))
                    v.scalar_tensor_tensor(dst[0:n, :].rearrange("p (h q) -> p h q", h=H),
                                           wmean[0:n, i, :].unsqueeze(2).broadcast_to([n, H, QD]), -1.0 / QD, sv,
                                           ALU.mult, ALU.add).then_inc(WqC_ready, 1)
                link(v.memset(KB[:, :], 0.0))
                o = full(dve, "keys", b)
                for i in range(4):
                    q = slice(32 * i, 32 * i + 32)
                    last = v.tensor_copy(KB[q, NK * i:NK * i + NK], o[q, 0:NK])
                freed(last, "keys", b)
                read_out(dve, "keys", b)
                v.engine_nop().then_inc(KB_ready, 1)

            def N0(b):
                for t in range(NT):
                    dve.wait_ge(sq_ready, NT * b + t + 1)
                    link(v.tensor_reduce(ssq[:, t, 0, 0:H], sq[:, t, :].rearrange("p (h q) -> p h q", h=H), X, ALU.add))
                    v.tensor_scalar(ssq[:, t, 1, 0:H], ssq[:, t, 0, 0:H], 1.0 / QD, LN_EPS, ALU.mult,
                                    ALU.add).then_inc(qvar_ready, 1)
                for t in range(NT):
                    dve.wait_ge(qrstd_ready, NT * b + t + 1)
                    o = full(dve, f"Q{t}", b)
                    freed(v.tensor_tensor(qn[:, t, :].rearrange("p (h q) -> p h q", h=H),
                                          o[:, :].rearrange("p (h q) -> p h q", h=H),
                                          inv[:, t, 0, 0:H].unsqueeze(2).broadcast_to([P, H, QD]), ALU.mult),
                          f"Q{t}", b)
                for t in range(NT):
                    dve.wait_ge(sq2_ready, NT * b + t + 1)
                    link(v.tensor_reduce(ssq[:, t, 0, :], sq[:, t, :].rearrange("p (h q) -> p h q", h=2 * H), X,
                                         ALU.add))
                    v.tensor_scalar(ssq[:, t, 1, :], ssq[:, t, 0, :], 1e-24, None, ALU.max).then_inc(qss_ready, 1)
                for t in range(NT):
                    dve.wait_ge(qinv_ready, NT * b + t + 1)
                    v.tensor_tensor(qs[:, t, :].rearrange("p (h q) -> p h q", h=2 * H),
                                    qf[:, t, :].rearrange("p (h q) -> p h q", h=2 * H),
                                    inv[:, t, 1, :].unsqueeze(2).broadcast_to([P, 2 * H, 32]),
                                    ALU.mult).then_inc(qs_ready, 1)

            def N1(b):
                p = b % 2
                for t in range(NT):
                    vt = v16[:, t * H:t * H + H, :, :].rearrange("p h a k -> p (h a) k")
                    it = i16[:, t * H:t * H + H, :, :].rearrange("p h a k -> p (h a) k")
                    read_out(dve, f"S2_{t}0", b)
                    read_out(dve, f"S2_{t}1", b)
                    for g in range(2 * H):
                        last = v.max(vt[:, g, 0:8], S[:, t, g, :])
                    link(last)
                    for g in range(2 * H):
                        last = v.match_replace(Sx[:, t, g, :], vt[:, g, 0:8], S[:, t, g, :], MARK)
                    link(last)
                    for g in range(2 * H):
                        last = v.max(vt[:, g, 8:16], Sx[:, t, g, :])
                    if t == NT - 1:
                        last.then_inc(v16_ready, 1)
                        dve.wait_ge(v16_ready, b + 1)
                    else:
                        link(last)
                    for g in range(2 * H):
                        v.max_index(it[:, g, 0:8], vt[:, g, 0:8], S[:, t, g, :])
                        last = v.max_index(it[:, g, 8:16], vt[:, g, 8:16], Sx[:, t, g, :])
                last.then_inc(i16_ready, 1)

            def N2(b):
                p = b % 2
                for i0, r, c, at in CELL_BLOCKS:
                    last = v.tensor_tensor(cand[:, :, at:at + r * c].rearrange("p g (r c) -> p g r c", r=r),
                                           v16[:, :, 0, i0:i0 + r].unsqueeze(3).broadcast_to([P, NT * H, r, c]),
                                           v16[:, :, 1, 0:c].unsqueeze(2).broadcast_to([P, NT * H, r, c]), ALU.add)
                link(last)
                for g in range(NT * H):
                    last = v.max(c8[:, g, 0, :], cand[:, g, :])
                link(last)
                for g in range(NT * H):
                    last = v.match_replace(candx[:, g, :], c8[:, g, 0, :], cand[:, g, :], MARK)
                link(last)
                for g in range(NT * H):
                    last = v.max(c8[:, g, 1, :], candx[:, g, :])
                link(last)
                for g in range(NT * H):
                    last = v.match_replace(candm[:, g, :], c8[:, g, 1, :], candx[:, g, :], MARK)
                link(last)
                dve.wait_ge(we_ready, b + 1)
                n = NT * H * CELLS
                if b >= 1:
                    dve.wait_ge(slots_ready, b)
                link(v.scalar_tensor_tensor(
                    wem[:, :, :, :].rearrange("p a g c -> p a (g c)"),
                    candm[:, :, :].rearrange("p g c -> p (g c)").unsqueeze(1).broadcast_to([P, 2, n]), MARK,
                    we[:, :, :, :].rearrange("p a g c -> p a (g c)"), ALU.is_equal, ALU.mult))
                link(v.tensor_reduce(zs[:, 0, :], wem[:, 0, :, :], X, ALU.add))
                link(v.reciprocal(zs[:, 1, :], zs[:, 0, :]))
                v.tensor_scalar(zs[:, 2, :], zs[:, 1, :], W_SCALE, None, ALU.mult).then_inc(wem_ready, 1)

            def N3(b):
                if b >= 1:
                    full(dve, "G11", b - 1)
                read_out(dve, "eT", b)
                v.tensor_scalar(eT[0:KC, 1, :], eT[0:KC, 0, :], LO - 1, None, ALU.bitwise_and)
                v.tensor_scalar(eT[0:KC, 2, :], eT[0:KC, 0, :], E - LO, None,
                                ALU.bitwise_and).then_inc(eT_ready, 1)
                o = full(dve, "wT", b)
                dve.wait_ge(act_chain, b + 1)
                freed(v.tensor_tensor(W2[0:KC, 1, :], o[0:KC, :], W2[0:KC, 0, :], ALU.subtract), "wT", b)
                dve.wait_ge(eT_ready, b + 1)
                for lo in range(LO):
                    last = v.tensor_scalar(lom[0:KC, lo, :], eT[0:KC, 1, :], float(lo), None, ALU.is_equal)
                link(last)
                read_out(dve, "wT", b)
                for lo in range(LO):
                    v.tensor_tensor(R[0:KC, :, lo, :], W2[0:KC, :, :],
                                    lom[0:KC, lo, :].unsqueeze(1).broadcast_to([KC, 2, NCH * N]), ALU.mult)
                for hi in range(HI // 4, HI):
                    last = v.tensor_scalar(OH[0:KC, :, :, hi, :], hi_view(eT), float(LO * hi), None, ALU.is_equal)
                last.then_inc(onehot_dve_ready, 1)

            def N4(b):
                pass

            def N5(b):
                read_out(dve, "I0", b)
                read_out(dve, "I1", b)
                if b >= 1:
                    full(dve, "Y", b - 1)
                for t in range(NT):
                    for j in range(2):
                        g = slice(16 * j, 16 * j + 16)
                        o = full(dve, f"G{t}{j}", b)
                        freed(v.tensor_tensor(
                            prod[:, t, g, :, :], o[:, :].rearrange("p (g s e) -> p g s e", g=16, s=2),
                            act[:, t, g, :, :].rearrange("p g q l -> p g (q l)").unsqueeze(2).broadcast_to(
                                [P, 16, 2, 16]), ALU.mult), f"G{t}{j}", b)

            def N6(b):
                p = b % 2
                stored(dve, b, 1)
                o = full(dve, "YT", b)
                ins = v.tensor_tensor(outs[:, :, :], o[:, 0:N].rearrange("p (t c) -> p t c", t=NT),
                                      t1[:, p, :, :], ALU.add)
                freed(ins, "YT", b)
                read_out(dve, "YT", b)
                v.engine_nop().then_inc(out_ready, 1)

            do = {"F0": F0, "F1": F1, "F2": F2, "F3": F3, "F4": F4, "F5": F5, "F6": F6, "F7": F7, "F8": F8,
                  "F9": F9, "F10": F10, "F11": F11, "NS": NS, "N0": N0, "N1": N1, "N2": N2, "N3": N3, "N4": N4,
                  "N5": N5, "N6": N6}
            for s, b in steps:
                do[s](b)

        @block.gpsimd
        def _(pool):
            g_ = nc.gpsimd
            link = chained(pool, pool_chain)

            g_.memset(mhalf[:, :], -0.5)
            g_.memset(ones[:, :], 1.0)
            g_.memset(qpad[:, :, :], 0.0)
            g_.memset(rts[:, :, :], LARGE)
            link(g_.memset(vBD0[:, :, :, :], 0.0))
            for r in range(2):
                link(g_.memset(vBD0[NP_ * r:NP_ * r + NP_, :, r, DH:DH + 1], 1.0))
            g_.memset(vA[:, :, :, DH:DH + 1], 1.0).then_inc(preset, 1)
            pool.wait_ge(preset, 1)

            def inverse_root(k, b):
                p = b % 2
                pool.wait_ge(var_ready[k], b + 1)
                g_.tensor_tensor(rstd[:, k, :], veps[:, k, :], mhalf[:, 0:NT], ALU.pow)\
                    .then_inc(rstd_ready[k], 1)

            def F0(b):
                p = b % 2
                front_buffers_free(pool, b)
                inverse_root(0, b)
                if b == 0:
                    pool.wait_ge(wa_loaded, 16)
                pool.wait_ge(hat_ready[0], b + 1)
                link(g_.tensor_tensor(xg[:, :, :], hat[:, 0, :, :],
                                      A("lng").unsqueeze(1).broadcast_to([P, NT, C]), ALU.mult))
                g_.tensor_tensor(xln[:, :, :], xg[:, :, :],
                                 A("lnb").unsqueeze(1).broadcast_to([P, NT, C]), ALU.add).then_inc(xln_ready, 1)

            def F6(b):
                inverse_root(1, b)

            def F7(b):
                inverse_root(2, b)

            def F8(b):
                p = b % 2
                read_out(pool, "k1", b)
                g_.tensor_tensor(kBD1[:, :, :], k1T[:, :].unsqueeze(1).broadcast_to([P, H, N]),
                                 hm.unsqueeze(2).broadcast_to([P, H, N]), ALU.mult).then_inc(kbd1_ready, 1)

            def F11(b):
                inverse_root(3, b)

            def NS(b):
                k = slice(0, NK)
                pool.wait_ge(kss_ready, 1)
                g_.tensor_tensor(kss[k, 2, :], kss[k, 1, :], mhalf[k, 0:4], ALU.pow).then_inc(kinv_ready, 1)
                pool.wait_ge(wb_loaded, 16)
                qm = Bw("qmask")
                for q in range(4):
                    last = g_.tensor_scalar(upM[:, q, :, :].rearrange("p l c -> p (l c)"), Bw("upR"), qm[:, q:q + 1],
                                            None, ALU.mult)
                last.then_inc(upM_ready, 1)

            def N0(b):
                fg = Bw("flng").unsqueeze(1).broadcast_to([P, H, QD])
                fb = Bw("flnb").unsqueeze(1).broadcast_to([P, H, QD])
                for t in range(NT):
                    pool.wait_ge(qvar_ready, NT * b + t + 1)
                    g_.tensor_tensor(inv[:, t, 0, 0:H], ssq[:, t, 1, 0:H], mhalf[:, 0:H], ALU.pow)\
                        .then_inc(qrstd_ready, 1)
                for t in range(NT):
                    read_out(pool, f"Q{t}", b)
                    link(g_.tensor_tensor(qg[:, t, :].rearrange("p (h q) -> p h q", h=H),
                                          qn[:, t, :].rearrange("p (h q) -> p h q", h=H), fg, ALU.mult))
                    if b >= 1:
                        pool.wait_ge(qs_ready, NT * b)
                    g_.tensor_tensor(qf[:, t, :].rearrange("p (h q) -> p h q", h=H),
                                     qg[:, t, :].rearrange("p (h q) -> p h q", h=H), fb, ALU.add)\
                        .then_inc(qf_ready, 1)
                for t in range(NT):
                    pool.wait_ge(qss_ready, NT * b + t + 1)
                    g_.tensor_tensor(inv[:, t, 1, :], ssq[:, t, 1, :], mhalf[:, :], ALU.pow).then_inc(qinv_ready, 1)

            def N2(b):
                p = b % 2
                pool.wait_ge(v16_ready, b + 1)
                if b >= 1:
                    full(pool, "G11", b - 1)
                    read_out(pool, "G11", b - 1)
                vv = v16[:, :, :, :].rearrange("p g a k -> p (g a) k")
                g_.tensor_tensor(dv[:, :, :, :].rearrange("p g a k -> p (g a) k"), vv,
                                 vv[:, :, 0:1].broadcast_to([P, 2 * NT * H, TOP]), ALU.subtract).then_inc(dv_ready, 1)
                for s, (src, ready, op) in enumerate(((ab, ab_ready, ALU.mult), (if_, if_ready, ALU.add))):
                    pool.wait_ge(ready, b + 1)
                    for i0, r, c, at in CELL_BLOCKS:
                        last = g_.tensor_tensor(
                            we[:, s, :, at:at + r * c].rearrange("p g (r c) -> p g r c", r=r),
                            src[:, :, 0, i0:i0 + r].unsqueeze(3).broadcast_to([P, NT * H, r, c]),
                            src[:, :, 1, 0:c].unsqueeze(2).broadcast_to([P, NT * H, r, c]), op)
                last.then_inc(we_ready, 1)
                if b >= 1:
                    read_out(pool, "eT", b - 1)
                    read_out(pool, "wT", b - 1)
                pool.wait_ge(wem_ready, b + 1)
                src = wem[:, :, :, :].rearrange("p a g c -> p (a g) c")
                dst = slots[:, :, :, :].rearrange("p a g c -> p (a g) c")
                for at, c, step, n in SLOT_COPIES:
                    g_.tensor_copy(dst[:, :, at:at + n], src[:, :, c:c + step * (n - 1) + 1:step])
                for at, c, step, c2, step2, n in SLOT_SUMS:
                    end = c2 + step2 * (n - 1) - 1
                    last = g_.tensor_tensor(dst[:, :, at:at + n], src[:, :, c:c + n], src[:, :, c2:end:step2], ALU.add)
                link(last)
                g_.tensor_tensor(wn[:, :, :], slots[:, 0, :, :],
                                 zs[:, 2, :].unsqueeze(2).broadcast_to([P, NT * H, SLOTS]), ALU.mult)\
                    .then_inc(slots_ready, 1)

            def N3(b):
                if b >= 1:
                    full(pool, "G11", b - 1)
                pool.wait_ge(eT_ready, b + 1)
                for hi in range(0, HI // 4):
                    last = g_.tensor_scalar(OH[0:KC, :, :, hi, :], hi_view(eT), float(LO * hi), None, ALU.is_equal)
                last.then_inc(onehot_pool_ready, 1)

            do = {"F0": F0, "F6": F6, "F7": F7, "F8": F8, "F11": F11, "NS": NS, "N0": N0, "N2": N2, "N3": N3}
            for s, b in steps:
                if s in do:
                    do[s](b)


def kernel(**inputs):
    import numpy as np
    import concourse.bacc as bacc
    from concourse.bass_utils import run_bass_kernel_spmd

    a = {k: np.asarray(v) for k, v in inputs.items()}
    f = np.float32

    def bc(v, n=P):
        return np.broadcast_to(v.reshape(1, -1), (n, v.size))

    def pad(v):
        out = np.zeros((P, v.shape[1]), f)
        out[:v.shape[0]] = v
        return out

    ch = np.arange(P)
    pos = np.arange(NP_)
    ref = ((np.arange(G8, dtype=f) + f(0.5)) * f(2.0 / G8) - f(1.0)).astype(f)
    heads = (ch[:, None] // DH == np.arange(H)[None, :]).astype(f)
    col0 = np.arange(H * NP_)
    E0 = (np.arange(P)[:, None] == (col0 // NP_)[None, :]).astype(f)
    col1 = np.arange(H * N)
    E1 = (ch[:, None] == (col1 // N * SEG + (col1 % N) // SEG)[None, :]).astype(f)
    quarter = (ch[:, None] // HI == np.arange(4)[None, :]).astype(f) / f(W_SCALE)

    vecs = np.stack([a["L0_conv_" + n] for n in ("ln_g", "ln_b", "bq", "bv", "dw_b", "mq_b", "mk_b")]
                    + [a["L0_conv_bq"]], axis=1)
    wv = a["L0_conv_wv"]
    down = a["L1_ffn_expert_down"][:E]
    up = a["L1_ffn_expert_up"][:E]
    downR = np.broadcast_to(down.reshape(HI, LO, C).transpose(2, 1, 0)[:, :, None, :], (C, LO, 4, HI))
    upR = np.broadcast_to(up.reshape(1, HI, LO * C), (4, HI, LO * C))
    k0, k1 = a["L1_ffn_keys0"], a["L1_ffn_keys1"]
    A = {"ident": np.eye(P, dtype=f), "wq": a["L0_conv_wq"], "lng": bc(a["L0_conv_ln_g"]),
         "lnb": bc(a["L0_conv_ln_b"]), "vecs": vecs, "pw": a["L0_conv_pw_w"].reshape(2, C)[::-1].T,
         "refs": pad(np.stack([ref[pos % G8], ref[pos // G8]], axis=1)), "iota": bc(np.arange(SIDE, dtype=f)),
         "hm": heads, "dw": a["L0_conv_dw_w"].reshape(C, KS * KS),
         "wv2": pad(wv.reshape(2, NP_, C).transpose(1, 0, 2).reshape(NP_, 2 * C)),
         "mq": a["L0_conv_mq_w"], "mk": a["L0_conv_mk_w"], "mv": a["L0_conv_mv_w"], "mo": a["L0_conv_mo_w"],
         "mlp": a["L0_conv_mlp_w"], "E0": E0}
    Bm = {"wqkv": a["L1_attn_w_qkv"].T, "wproj": a["L1_attn_w_proj"].T, "Wq": a["L1_ffn_Wq"].T,
          "flng": bc(a["L1_ffn_ln_g"]), "flnb": bc(a["L1_ffn_ln_b"]), "downR": downR.reshape(C, -1),
          "upR": upR.reshape(P, -1), "qmask": quarter, "keys": pad(np.concatenate([k0, k1, k0, k1], axis=1)),
          "E1": E1}
    rows = {"bq": a["L0_conv_bq"], "mvb": a["L0_conv_mv_b"], "mob": a["L0_conv_mo_b"], "mlpb": a["L0_conv_mlp_b"],
            "bproj": a["L1_attn_b_proj"], "fbq": a["L1_ffn_bq"]}
    arrays = {
        "x": np.ascontiguousarray(a["x"].reshape(B, NT, P, C).transpose(0, 2, 1, 3)),
        "wa": np.ascontiguousarray(np.concatenate([A[n] for n, _ in WEIGHTS_A], axis=1)),
        "wb": np.ascontiguousarray(np.concatenate([Bm[n] for n, _ in WEIGHTS_B], axis=1)),
        "rows": np.concatenate([rows[n] for n, _ in ROWS])[None, :],
    }
    nc = bacc.Bacc("TRN2", target_bir_lowering=False, num_devices=1)
    args = [nc.dram_tensor(n + "_dram", v.shape, mybir.dt.from_np(v.dtype), kind="ExternalInput").ap()
            for n, v in arrays.items()]
    out = nc.dram_tensor("out_dram", (B, P, NT, C), F32, kind="ExternalOutput").ap()
    build(nc, *args, out)
    r = run_bass_kernel_spmd(nc, [{n + "_dram": v for n, v in arrays.items()}], core_ids=[0])
    got = r.results[0]["out_dram"]
    return np.ascontiguousarray(got.transpose(0, 2, 1, 3)).reshape(B, SIDE, SIDE, C)
```

```python
from contextlib import ExitStack

import concourse.bass as bass
from concourse import mybir

ALU = mybir.AluOpType
ACT = mybir.ActivationFunctionType
X = mybir.AxisListType.X
F32 = mybir.dt.float32
F16 = mybir.dt.float16
BF16 = mybir.dt.bfloat16
U16 = mybir.dt.uint16

P = 128
B = 4
SIDE = 16
C = 128
NT = 2
N = NT * P
H = 8
DH = C // H
KS = 7
PADDED = SIDE + 6
G8 = 8
NP_ = G8 * G8
SEG = 16
TOP = 16
NK = 64
QD = 64
E = 128
LN_EPS = 1e-5
MARK = -3.0e38
LARGE = 3.0e38
HIDE = -1.0e30
LO = 4
HI = E // LO
CONV_DVE = 3
FOLDED = 13
POOL_HI = 3
W_SCALE = 2.0 ** 15

CELL_BLOCKS = [(0, 1, 16, 0), (1, 1, 8, 16), (2, 2, 5, 24), (4, 4, 3, 34), (8, 8, 1, 46)]
CELLS = 54
SLOT_SUMS = [
    (1, 1, 1, 53, -1, 8),
    (9, 9, 1, 43, -3, 4),
    (13, 13, 1, 29, -5, 2),
    (15, 15, 1, 16, -5, 1),
    (16, 18, 1, 44, -3, 4),
    (20, 22, 1, 30, -5, 2),
    (22, 27, 1, 36, -5, 2),
]
SLOT_COPIES = [(0, 0, 1, 1), (24, 17, 9, 2), (26, 32, 1, 1)]
SLOTS = 27
HC = 4
KC = HC * SLOTS
NCH = H // HC

FRONT_JOBS = {
    "A1a": ["qimg", "qT"], "A1b": ["qhT"],
    "A2d": ["offs"],
    "A3a": ["WT"], "A3b": ["interp"], "A3c": ["vT"],
    "A4": ["kh", "vh"],
    "F5a": ["S0_0", "S0_1"], "F5b": ["mT"], "F5c": ["P0_0", "P0_1"],
    "F6a": ["O0"], "F6b": ["aT"], "F6c": ["msa"],
    "F7a": ["zT"], "F7b": ["mlp"],
    "F8a": ["tT"], "F8b": ["k1", "q1"], "F8c": ["v1"],
    "F9a": ["route"],
    "F9b": ["S1_00", "S1_01", "S1_02", "S1_03"], "F9c": ["S1_10", "S1_11", "S1_12", "S1_13"],
    "F9d": ["bT"],
    "F10a": ["P1_0", "P1_1", "P1_2", "P1_3"], "F10b": ["P1_4", "P1_5", "P1_6", "P1_7"],
    "F11a": ["O1"], "F11b": ["a1T"], "F11c": ["proj"],
    "F12": ["fT"],
}
EXPERT_JOBS = {
    "NS": ["keys"],
    "N0a": ["Q0", "Q1"],
    "N0b": ["qsT0"], "N0c": ["S2_00", "S2_01"], "N0d": ["qsT1"], "N0e": ["S2_10", "S2_11"], "N0f": ["norm"],
    "N3a": ["wT", "eT"],
    "N4": ["I0", "I1"],
    "N5a": ["G0"], "N5b": ["G1"],
    "N6a": ["Y"], "N6b": ["YT"],
}
FRONT_BANKS = [0, 1, 2, 3]
EXPERT_BANKS = [4, 5, 6, 7]

ORDERS = {
    "tensor": """N6b- N0a F5b A1a F5c N0b F6a N0c F6b A1b N0d F6c N0e F7a F7b N0f F8a A2d F8b A3a NS F8c F9a F9b
        F9c A3b A3c F9d A4 F10a F10b F11a F11b F11c N3a F12 F5a+ N4 N5a N5b N6a""".split(),
    "scalar": """N6a- N0a F5b A1a F5c N0b N0c F6b N0d N0e F7a F7b A1b A2c F8a A2d F8b F8c F9a A3a A3b A3c A4
        F10a F10b N2c F11b N3a N4 F12""".split(),
    "vector": """N5b- A0a A0b F5a N6b- N0a F6a N1_0 F6c F7a A2c F7b F8a A3a F8b N1_1 F9a F9b NS N1_2 F9c F9d
        N1_3 N2a N2b N2c F11a F11c F12 N3a N3b N5a""".split(),
    "gpsimd": """N2c- F11c- N3b- A0a A0b N0a A2a NS A2b F6c F7b F8b N1_1 A4""".split(),
}


def schedule(engine):
    out = []
    for b in range(-1, B + 2):
        for name in ORDERS[engine]:
            s = name.rstrip("+-")
            image = b + {"A": 1, "F": 0, "N": -1}[s[0]] + name.count("+") - name.count("-")
            if s == "NS":
                image = 0 if b == -1 else B
            if 0 <= image < B:
                out.append((s, image))
    return out


def place_jobs():
    turn, count, out = {0: 0, 1: 0}, [0] * 8, {}
    for s, b in schedule("tensor"):
        ring = 0 if s in FRONT_JOBS else 1
        banks = (FRONT_BANKS, EXPERT_BANKS)[ring]
        for job in (FRONT_JOBS, EXPERT_JOBS)[ring].get(s, []):
            k = banks[turn[ring] % len(banks)]
            turn[ring] += 1
            count[k] += 1
            out[job, b] = (k, count[k])
    return out


WEIGHTS_A = [("ident", 128), ("wq", 128), ("lng", 128), ("lnb", 128), ("vecs", 8), ("pw", 2), ("refs", 2),
             ("iota", 16), ("hm", 8), ("dw", 49), ("wv2", 256), ("mq", 128), ("mk", 128), ("mv", 128),
             ("mo", 128), ("mlp", 128), ("E0", 512)]
WEIGHTS_B = [("wqk", 512), ("wv1", 128), ("wproj", 128), ("Wq", 512), ("fln", 2), ("downR", 512),
             ("upR", 512), ("qmask", 4), ("keys", 128), ("hm32", 4), ("Epat", N), ("pick", 3)]
ROWS = [("bq", 128), ("mvb", 128), ("mob", 128), ("mlpb", 128), ("bproj", 128), ("fbq", 512)]
VEC = {n: i for i, n in enumerate(["lng", "lnb", "bq", "bv", "dwb", "mqb", "mkb"])}


def offsets(parts):
    out, at = {}, 0
    for n, k in parts:
        out[n] = (at, k)
        at += k
    return out, at


def build(nc, x_in, wa_in, wb_in, rows_in, out):
    jobs = place_jobs()
    offA, NA = offsets(WEIGHTS_A)
    offB, NB = offsets(WEIGHTS_B)
    offR, NR = offsets(ROWS)

    ctx = ExitStack()
    with ctx:
        def sb(name, shape, dt=F32):
            return ctx.enter_context(nc.sbuf_tensor(name, [P] + list(shape), dt))

        def sem(name):
            return ctx.enter_context(nc.semaphore(name))

        wa = sb("wa", [NA])
        wb = sb("wb", [NB])
        bq_row = sb("bq_row", [C])
        KB = sb("KB", [2 * 2 * NK])
        upM = sb("upM", [4, LO, C])
        mhalf = sb("mhalf", [2 * NT * H])
        ones = sb("ones", [P])

        def A(n):
            at, k = offA[n]
            return wa[:, at:at + k]

        def Bw(n):
            at, k = offB[n]
            return wb[:, at:at + k]

        def vec(n):
            at = offA["vecs"][0] + VEC[n]
            return wa[:, at:at + 1]

        ident = A("ident")
        hm = A("hm")

        x_sb = sb("x_sb", [B, NT, C])
        stats = sb("stats", [4, NT, 6])
        mv = sb("mv", [4, NT, 2])
        veps = sb("veps", [4, NT])
        rstd = sb("rstd", [4, NT])
        hat = sb("hat", [4, NT, C])
        xln = sb("xln", [NT, C])
        qpad = sb("qpad", [PADDED, PADDED])
        taps = sb("taps", [KS * KS, NP_])
        conv = sb("conv", [NP_])
        qT = sb("qT", [N])
        qhT = sb("qhT", [2, N])
        osb = sb("osb", [NP_])
        tanh_ = sb("tanh_", [2])
        crd = sb("crd", [3, 2])
        hatw = sb("hatw", [3, 2, SIDE])
        Wp = sb("Wp", [SIDE, SIDE])
        WTs = sb("WTs", [NT, NP_])
        ips = sb("ips", [C])
        vT = sb("vT", [2, NP_])
        khT = sb("khT", [NP_])
        vBD0 = sb("vBD0", [2, 4, 2, DH + 1])
        kBD0 = sb("kBD0", [2, H, NP_])
        negM = sb("negM", [NT, H])
        negMT = sb("negMT", [N])
        rec = sb("rec", [2, NT * H])
        att = sb("att", [NT, C])
        attT = sb("attT", [N])
        z = sb("z", [NT, C])
        zT = sb("zT", [N])
        gl = sb("gl", [NT, C])
        xg = gl
        t0 = sb("t0", [NT, C])
        tlT = sb("tlT", [N])
        q1P = sb("q1P", [2, N])
        qB = sb("qB", [2, N])
        kE = sb("kE", [2, N])
        vA = sb("vA", [NT, H, DH + 1])
        cent = sb("cent", [2, SEG])
        centBD = sb("centBD", [H, SEG])
        kBD1 = sb("kBD1", [H, N])
        rts = sb("rts", [NT * H, SEG + 4])
        rtm = sb("rtm", [NT * H, SEG + 4])
        r8 = sb("r8", [NT * H, 8])
        segmax = sb("segmax", [NT * H, SEG])
        pen = sb("pen", [NT * H, SEG])
        sel = sb("sel", [NT * H, SEG])
        selM = sb("selM", [NT * H])
        bias = sb("bias", [NT * H, 2, SEG])
        late = sb("late", [H * 2 * N])
        PT1 = late[:, :].rearrange("p (h k n) -> p h k n", h=H, k=2)
        PT0 = late[:, 0:4 * N].rearrange("p (a n) -> p a n", a=4)
        t1 = sb("t1", [2, NT, C])
        fT = sb("fT", [2, N])
        onehot = sb("onehot", [HI * NCH * N], F16)
        OH = onehot[:, :].rearrange("p (n q v g) -> p n q v g", n=NCH * NT, q=4, v=HI)
        early = onehot[:, :].bitcast(F32)
        Q = NT * H * QD

        def early_part(i, n):
            return early[:, i * Q:i * Q + n]
        sq = early_part(0, Q).rearrange("p (t n) -> p t n", t=NT)
        qn = early_part(1, Q).rearrange("p (t n) -> p t n", t=NT)
        sqT = early_part(2, Q).rearrange("p (t c n) -> p t c n", t=NT, c=4)
        qsT = early_part(3, Q).rearrange("p (t c n) -> p t c n", t=NT, c=4)
        S = early_part(4, 2 * Q).rearrange("p (t g e) -> p t g e", t=NT, g=2 * H)
        Sx = early_part(6, 2 * Q).rearrange("p (t g e) -> p t g e", t=NT, g=2 * H)
        ssq = sb("ssq", [NT, 2, H])
        qrstd = sb("qrstd", [NT, H])
        nrm = sb("nrm", [NT * 2 * H])
        inv = sb("inv", [NT * 2 * H])
        vraw = sb("vraw", [NT * H, 2, TOP])
        v16 = sb("v16", [NT * H, 2, TOP])
        i16 = sb("i16", [NT * H, 2, TOP], U16)
        act_store = sb("act_store", [2 * NT * H * 2 * TOP])
        act = act_store[:, :].rearrange("p (t g q l) -> p t g q l", t=NT, g=32, q=4)
        if_, ab = (act_store[:, i * NT * H * 2 * TOP:(i + 1) * NT * H * 2 * TOP].rearrange(
            "p (g a k) -> p g a k", g=NT * H, a=2) for i in range(2))
        dv = ab
        cands = sb("cands", [2 * NT * H * CELLS])
        cand, candx = (cands[:, i * NT * H * CELLS:(i + 1) * NT * H * CELLS].rearrange(
            "p (g c) -> p g c", g=NT * H) for i in range(2))
        candm = cand
        lom = cands[:, 0:LO * NCH * N // 2].bitcast(F16).rearrange("p (l n) -> p l n", l=LO)
        c8 = sb("c8", [NT * H, 2, 8])
        weights = sb("weights", [LO * NCH * N])
        we = weights[:, 0:2 * NT * H * CELLS].rearrange("p (a g c) -> p a g c", a=2, g=NT * H)
        R = weights[:, :].bitcast(F16).rearrange("p (s l n) -> p s l n", s=2, l=LO)
        masked = sb("masked", [2 * NT * H * CELLS])
        prod = masked[:, 0:NT * 32 * 4 * LO].rearrange("p (t g e) -> p t g e", t=NT, g=32)
        wem = masked[:, 0:2 * NT * H * CELLS].rearrange("p (a g c) -> p a g c", a=2, g=NT * H)
        zs = sb("zs", [3, NT * H])
        slots = sb("slots", [2, NT * H, SLOTS])
        wn = sb("wn", [NT * H, SLOTS])
        W2 = sb("W2", [2, NCH * N], F16)
        eT = sb("eT", [3, NCH * N], U16)
        YTs = W2[:, :, :].rearrange("p s n -> p (s n)")[:, 0:2 * N].bitcast(F32)
        outs = eT[:, 0, :].bitcast(F32).rearrange("p (t c) -> p t c", t=NT)
        kss = sb("kss", [3, 4])
        wmean = sb("wmean", [2, H])
        WqC = Bw("Wq")
        rrest = early[:, 0:2 * NR].rearrange("p (i n) -> p i n", i=2)
        rparts = onehot[:, 4 * NR:7 * NR].bitcast(BF16).rearrange("p (i n) -> p i n", i=3)
        ksq = early[:, 4 * NR:4 * NR + P]
        kn = early[:, 4 * NR + P:4 * NR + 2 * P]
        rows = early[:, 4 * NR + 2 * P:5 * NR + 2 * P]
        rows3 = sb("rows3", [NR], BF16)
        ones3 = sb("ones3", [P], BF16)
        ident16 = sb("ident16", [P], BF16)
        Epat16 = sb("Epat16", [N], BF16)

        def row3(n):
            at, k = offR[n]
            return rows3[0:3, at:at + k]

        psum = [ctx.enter_context(nc.psum_tensor(f"bank{k}", [P, 512], F32)) for k in range(8)]

        bank_full = [sem(f"bank_full{k}") for k in range(8)]
        bank_free = [sem(f"bank_free{k}") for k in range(8)]
        x_loaded = [sem(f"x_loaded{b}") for b in range(B)]
        wa_loaded = sem("wa_loaded")
        wb_loaded = sem("wb_loaded")
        bq_loaded = sem("bq_loaded")
        rows_loaded = sem("rows_loaded")
        preset = sem("preset")
        taps_pool_ready = sem("taps_pool_ready")
        conv_ready = sem("conv_ready")
        osb_ready = sem("osb_ready")
        var_ready = [sem(f"var_ready{k}") for k in range(4)]
        rstd_ready = [sem(f"rstd_ready{k}") for k in range(4)]
        hat_ready = [sem(f"hat_ready{k}") for k in range(4)]
        xln_ready = sem("xln_ready")
        hatw_ready = sem("hatw_ready")
        kbd0_ready = sem("kbd0_ready")
        negm_ready = sem("negm_ready")
        gl_ready = sem("gl_ready")
        t0_ready = sem("t0_ready")
        centbd_ready = sem("centbd_ready")
        kbd1_ready = sem("kbd1_ready")
        bias_ready = sem("bias_ready")
        kss_ready = sem("kss_ready")
        kinv_ready = sem("kinv_ready")
        kn_ready = sem("kn_ready")
        KB_ready = sem("KB_ready")
        WqC_ready = sem("WqC_ready")
        upM_ready = sem("upM_ready")
        sq_ready = sem("sq_ready")
        qvar_ready = sem("qvar_ready")
        qrstd_ready = sem("qrstd_ready")
        sqT_ready = sem("sqT_ready")
        nrm_ready = sem("nrm_ready")
        inv_ready = sem("inv_ready")
        rows3_ready = sem("rows3_ready")
        v16_ready = sem("v16_ready")
        i16_ready = sem("i16_ready")
        dv_ready = sem("dv_ready")
        ab_ready = sem("ab_ready")
        if_ready = sem("if_ready")
        we_ready = sem("we_ready")
        wem_ready = sem("wem_ready")
        slots_ready = sem("slots_ready")
        eT_ready = sem("eT_ready")
        onehot_dve_ready = sem("onehot_dve_ready")
        onehot_pool_ready = sem("onehot_pool_ready")
        act_ready = sem("act_ready")
        out_ready = sem("out_ready")
        out_stored = sem("out_stored")
        dve_chain = sem("dve_chain")
        act_chain = sem("act_chain")
        pool_chain = sem("pool_chain")

        def full(eng, job, b):
            k, n = jobs[job, b]
            eng.wait_ge(bank_full[k], n)
            return psum[k]

        def freed(ins, job, b):
            ins.then_inc(bank_free[jobs[job, b][0]], 1)

        def read_out(eng, job, b):
            k, n = jobs[job, b]
            eng.wait_ge(bank_free[k], n)

        def chained(eng, semaphore):
            count = [0]

            def link(ins):
                count[0] += 1
                ins.then_inc(semaphore, 1)
                eng.wait_ge(semaphore, count[0])
            return link

        def sampling_free(eng, b):
            if b >= 1:
                read_out(eng, "kh", b - 1)
                read_out(eng, "vh", b - 1)
            if b >= 2:
                read_out(eng, "O0", b - 2)

        def front_free(eng, b):
            if b >= 1:
                read_out(eng, "fT", b - 1)

        def stored(eng, b, back):
            if b >= back:
                eng.wait_ge(out_stored, 16 * (b - back + 1))

        def conv_rows(eng, first, last):
            dw = A("dw").rearrange("p (a b) -> p a b", a=KS)
            tv = taps[:, :, :].rearrange("p (a b) (y x) -> p y x a b", a=KS, y=G8)
            for ky in range(first, last):
                for kx in range(0, KS, 2):
                    n = min(2, KS - kx)
                    q = qpad[:, ky:ky + 15:2, kx:kx + 16].rearrange("p y (x r) -> p y x r", r=2)[:, :, :, 0:n]
                    ins = eng.tensor_tensor(tv[:, :, :, ky, kx:kx + n], q,
                                            dw[:, ky, kx:kx + n].unsqueeze(1).unsqueeze(1).broadcast_to(
                                                [P, G8, G8, n]), ALU.mult)
            return ins

        def hi_view(e):
            return e[0:KC, 2, :].rearrange("p (n q g) -> p n q g", n=NCH * NT, q=4)

        block = ctx.enter_context(nc.Block())

        @block.sync
        def _(sp):
            sp.dma_start(x_sb[:, 0, :, :], x_in[0]).then_inc(x_loaded[0], 16)
            sp.dma_start(wa[:, :], wa_in).then_inc(wa_loaded, 16)
            sp.dma_start(bq_row[0:1, :], rows_in[0:1, 0:C]).then_inc(bq_loaded, 16)
            for b in range(1, B):
                sp.dma_start(x_sb[:, b, :, :], x_in[b]).then_inc(x_loaded[b], 16)
            sp.dma_start(wb[:, :], wb_in).then_inc(wb_loaded, 16)
            sp.dma_start(rows[0:3, :], rows_in).then_inc(rows_loaded, 16)
            for b in range(B):
                sp.wait_ge(out_ready, b + 1)
                sp.dma_start(out[b], outs[:, :, :]).then_inc(out_stored, 16)
            sp.wait_ge(out_stored, 16 * B)

        @block.tensor
        def _(pe):
            def take(job, b):
                k, n = jobs[job, b]
                if n > 1:
                    pe.wait_ge(bank_free[k], n - 1)
                return psum[k]

            def done(ins, job, b):
                ins.then_inc(bank_full[jobs[job, b][0]], 1)

            def transposes(job, b, pairs):
                o = take(job, b)
                for at, src in pairs:
                    k, m = src.shape
                    last = nc.tensor.transpose(o[0:m, at:at + k], src, ident[0:k, 0:k])
                done(last, job, b)

            mm = nc.tensor.matmul

            def A1a(b):
                p = b % 2
                if b == 0:
                    pe.wait_ge(wa_loaded, 16)
                    pe.wait_ge(bq_loaded, 16)
                    pe.wait_ge(preset, 1)
                pe.wait_ge(xln_ready, b + 1)
                o = take("qimg", b)
                for s in range(NT):
                    c = slice(s * P, s * P + P)
                    mm(o[:, c], xln[:, s, :], A("wq"), start=True, stop=False)
                    last = mm(o[:, c], ones[0:1, :], bq_row[0:1, :], start=False, stop=True)
                done(last, "qimg", b)
                o = take("qT", b)
                last = mm(o[:, 0:N], A("wq"), xln[:, :, :], start=True, stop=True)
                done(last, "qT", b)

            def A1b(b):
                read_out(pe, "qT", b)
                o = take("qhT", b)
                done(mm(o[:, 0:N], A("mq"), qT[:, :], start=True, stop=True), "qhT", b)

            def A2d(b):
                pe.wait_ge(osb_ready, b + 1)
                o = take("offs", b)
                done(mm(o[0:NP_, 0:2], osb[:, :], A("pw"), start=True, stop=True), "offs", b)

            def A3a(b):
                p = b % 2
                pe.wait_ge(hatw_ready, b + 1)
                Wf = Wp[0:NP_, :, :].rearrange("p a b -> p (a b)")
                transposes("WT", b, [(s * NP_, Wf[:, s * P:s * P + P]) for s in range(NT)])

            def A3b(b):
                read_out(pe, "WT", b)
                o = take("interp", b)
                for s in range(NT):
                    last = mm(o[0:NP_, 0:C], WTs[:, s, :], x_sb[:, b, s, :], start=(s == 0), stop=(s == NT - 1))
                done(last, "interp", b)

            def A3c(b):
                read_out(pe, "interp", b)
                o = take("vT", b)
                wv2 = A("wv2").rearrange("p (u n) -> p u n", u=2)
                for u in range(2):
                    last = mm(o[:, 0:NP_], wv2[0:NP_, u, :], ips[0:NP_, u:C:2], start=(u == 0), stop=(u == 1))
                done(last, "vT", b)

            def A4(b):
                if b == 0:
                    pe.wait_ge(rows3_ready, 1)
                    pe.wait_ge(wb_loaded, 16)
                read_out(pe, "vT", b)
                o = take("kh", b)
                done(mm(o[:, 0:NP_], A("mk"), vT[:, 0, :], start=True, stop=True), "kh", b)
                o = take("vh", b)
                mm(o[:, 0:C], vT[:, :, :], A("mv"), start=True, stop=False)
                done(mm(o[:, 0:C], ones3[0:3, :], row3("mvb"), start=False, stop=True), "vh", b)

            def F5a(b):
                p = b % 2
                read_out(pe, "qhT", b)
                pe.wait_ge(kbd0_ready, b + 1)
                for t in range(NT):
                    o = take(f"S0_{t}", b)
                    done(mm(o[:, :], qhT[:, b % 2, t * P:t * P + P], kBD0[:, b % 2, :, :], start=True, stop=True),
                         f"S0_{t}", b)

            def F5b(b):
                pe.wait_ge(negm_ready, b + 1)
                transposes("mT", b, [(t * P, negM[:, t, :]) for t in range(NT)])

            def F5c(b):
                read_out(pe, "mT", b)
                E0 = A("E0")
                for j in range(2):
                    o = take(f"P0_{j}", b)
                    for i in range(2):
                        hp = 2 * j + i
                        mm(o[:, i * N:i * N + N], kBD0[:, b % 2, 2 * hp:2 * hp + 2, :], qhT[:, b % 2, :],
                           start=True, stop=False)
                        last = mm(o[:, i * N:i * N + N], E0[0:H, hp * P:hp * P + P], negMT[0:H, :],
                                  start=False, stop=True)
                    done(last, f"P0_{j}", b)

            def F6a(b):
                read_out(pe, "P0_0", b)
                read_out(pe, "P0_1", b)
                read_out(pe, "vh", b)
                o = take("O0", b)
                for t in range(NT):
                    for hp in range(4):
                        at = (t * H + 2 * hp) * (DH + 1)
                        last = mm(o[:, at:at + 2 * (DH + 1)], PT0[:, hp, t * P:t * P + P], vBD0[:, b % 2, hp, :, :],
                                  start=True, stop=True)
                done(last, "O0", b)

            def F6b(b):
                read_out(pe, "O0", b)
                transposes("aT", b, [(t * P, att[:, t, :]) for t in range(NT)])

            def F6c(b):
                read_out(pe, "aT", b)
                o = take("msa", b)
                for t in range(NT):
                    c = slice(t * P, t * P + P)
                    mm(o[:, c], attT[:, c], A("mo"), start=True, stop=False)
                    last = mm(o[:, c], ones3[0:3, :], row3("mob"), start=False, stop=True)
                done(last, "msa", b)

            def F7a(b):
                p = b % 2
                pe.wait_ge(hat_ready[1], b + 1)
                transposes("zT", b, [(t * P, hat[:, 1, t, :]) for t in range(NT)])

            def F7b(b):
                read_out(pe, "zT", b)
                o = take("mlp", b)
                for t in range(NT):
                    c = slice(t * P, t * P + P)
                    mm(o[:, c], zT[:, c], A("mlp"), start=True, stop=False)
                    last = mm(o[:, c], ones3[0:3, :], row3("mlpb"), start=False, stop=True)
                done(last, "mlp", b)

            def F8a(b):
                p = b % 2
                pe.wait_ge(hat_ready[2], b + 1)
                transposes("tT", b, [(t * P, hat[:, 2, t, :]) for t in range(NT)])

            def F8b(b):
                if b == 0:
                    pe.wait_ge(upM_ready, 1)
                read_out(pe, "tT", b)
                wqk = Bw("wqk").rearrange("p (i j m) -> p i j m", i=2, j=2)
                for i, job in ((1, "k1"), (0, "q1")):
                    o = take(job, b)
                    for j in range(2):
                        c = slice(j * N, j * N + N)
                        last = mm(o[:, c], wqk[:, i, j, :], tlT[:, :], start=True, stop=(i == 0))
                        if i == 1:
                            last = mm(o[:, c], ident16[:, :], Epat16[:, :], start=False, stop=True)
                    done(last, job, b)

            def F8c(b):
                o = take("v1", b)
                for t in range(NT):
                    c = slice(t * P, t * P + P)
                    last = mm(o[:, c], tlT[:, c], Bw("wv1"), start=True, stop=True)
                done(last, "v1", b)

            def F9a(b):
                read_out(pe, "q1", b)
                pe.wait_ge(centbd_ready, b + 1)
                o = take("route", b)
                for t in range(NT):
                    for j in range(2):
                        last = mm(o[:, t * P + j * 64:t * P + j * 64 + 64], q1P[:, j, t * P:t * P + P],
                                  centBD[:, 4 * j:4 * j + 4, :], start=True, stop=True)
                done(last, "route", b)

            def segment_scores(b, t):
                for i in range(4):
                    job = f"S1_{t}{i}"
                    o = take(job, b)
                    done(mm(o[:, :], q1P[:, i // 2, t * P:t * P + P], kBD1[:, 2 * i:2 * i + 2, :],
                            start=True, stop=True), job, b)

            def F9b(b):
                pe.wait_ge(kbd1_ready, b + 1)
                segment_scores(b, 0)

            def F9c(b):
                segment_scores(b, 1)

            def F9d(b):
                pe.wait_ge(bias_ready, b + 1)
                bv = bias[:, :, :, :].rearrange("p (t j h) a s -> p t j (h a s)", t=NT, j=2)
                transposes("bT", b, [(j * N + t * P, bv[:, t, j, :]) for j in range(2) for t in range(NT)])

            def F10a(b):
                read_out(pe, "bT", b)
                weights_of(b, range(0, H // 2))

            def F10b(b):
                weights_of(b, range(H // 2, H))

            def weights_of(b, heads):
                for h in heads:
                    job = f"P1_{h}"
                    o = take(job, b)
                    for kc in range(NT):
                        last = mm(o[:, kc * N:kc * N + N], kBD1[:, h, kc * P:kc * P + P], qB[:, h // 4, :],
                                  start=True, stop=True)
                    done(last, job, b)

            def F11a(b):
                read_out(pe, "v1", b)
                o = take("O1", b)
                for h in range(H):
                    read_out(pe, f"P1_{h}", b)
                    for t in range(NT):
                        at = (t * H + h) * (DH + 1)
                        for kc in range(NT):
                            last = mm(o[:, at:at + DH + 1], PT1[:, h, kc, t * P:t * P + P], vA[:, kc, h, :],
                                      start=(kc == 0), stop=(kc == NT - 1))
                done(last, "O1", b)

            def F11b(b):
                read_out(pe, "O1", b)
                transposes("a1T", b, [(t * P, att[:, t, :]) for t in range(NT)])

            def F11c(b):
                read_out(pe, "a1T", b)
                o = take("proj", b)
                for t in range(NT):
                    c = slice(t * P, t * P + P)
                    mm(o[:, c], attT[:, c], Bw("wproj"), start=True, stop=False)
                    last = mm(o[:, c], ones3[0:3, :], row3("bproj"), start=False, stop=True)
                done(last, "proj", b)

            def F12(b):
                pe.wait_ge(hat_ready[3], b + 1)
                transposes("fT", b, [(t * P, hat[:, 3, t, :]) for t in range(NT)])

            def NS(b):
                pe.wait_ge(kn_ready, 1)
                transposes("keys", b, [(0, kn[0:NK, :])])

            def N0a(b):
                p = b % 2
                if b == 0:
                    pe.wait_ge(WqC_ready, 1)
                read_out(pe, "fT", b)
                for t in range(NT):
                    o = take(f"Q{t}", b)
                    mm(o[:, :], fT[:, p, t * P:t * P + P], WqC[:, :], start=True, stop=False)
                    done(mm(o[:, :], ones3[0:3, :], row3("fbq"), start=False, stop=True), f"Q{t}", b)

            def query_transposes(b, t):
                read_out(pe, f"Q{t}", b)
                transposes(f"qsT{t}", b, [(c * P, qn[:, t, c * P:c * P + P]) for c in range(4)])

            def key_scores(b, t):
                read_out(pe, f"qsT{t}", b)
                for j in range(2):
                    o = take(f"S2_{t}{j}", b)
                    for i in range(2):
                        last = mm(o[:, i * 256:i * 256 + 256], qsT[:, t, 2 * j + i, :], KB[:, :],
                                  start=True, stop=True)
                    done(last, f"S2_{t}{j}", b)

            def N0b(b):
                query_transposes(b, 0)

            def N0c(b):
                if b == 0:
                    pe.wait_ge(KB_ready, 1)
                key_scores(b, 0)

            def N0d(b):
                query_transposes(b, 1)

            def N0e(b):
                key_scores(b, 1)

            def N0f(b):
                pe.wait_ge(sqT_ready, NT * (b + 1))
                o = take("norm", b)
                for t in range(NT):
                    for c in range(4):
                        at = t * 2 * H + 4 * c
                        last = mm(o[:, at:at + 4], sqT[:, t, c, :], Bw("hm32"), start=True, stop=True)
                done(last, "norm", b)

            def N3a(b):
                pe.wait_ge(slots_ready, b + 1)
                for job, src in (("wT", wn[:, :, :]), ("eT", slots[:, 1, :, :])):
                    transposes(job, b, [((c * NT + t) * P,
                                         src[:, t * H + c * HC:t * H + (c + 1) * HC, :].rearrange("p h s -> p (h s)"))
                                        for c in range(NCH) for t in range(NT)])

            def N4(b):
                p = b % 2
                downR = Bw("downR").rearrange("p (l m) -> p l m", l=LO)
                for j in range(2):
                    o = take(f"I{j}", b)
                    for i in range(2):
                        last = mm(o[:, i * N:i * N + N], downR[:, 2 * j + i, :], fT[:, p, :], start=True, stop=True)
                    done(last, f"I{j}", b)

            def N5a(b):
                pe.wait_ge(onehot_dve_ready, b + 1)
                pe.wait_ge(onehot_pool_ready, b + 1)
                scatter(b, 0)

            def N5b(b):
                scatter(b, 1)

            def scatter(b, t):
                OHv = OH[0:KC, :, :, :, :].rearrange("p n q v g -> p n g (q v)")
                Rv = R[0:KC, :, :, :].rearrange("p s l (c t q g) -> p c t g s q l", c=NCH, t=NT, g=32)
                o = take(f"G{t}", b)
                for g in range(32):
                    for c in range(NCH):
                        for s in range(2):
                            last = mm(o[:, g * 16:g * 16 + 16], OHv[:, c * NT + t, g], Rv[:, c, t, g, s],
                                      start=(c == 0 and s == 0), stop=(c == NCH - 1 and s == 1))
                done(last, f"G{t}", b)

            def N6a(b):
                if b == 0:
                    pe.wait_ge(upM_ready, 1)
                for t in range(NT):
                    read_out(pe, f"G{t}", b)
                o = take("Y", b)
                ov = o[:, 0:N].rearrange("p (t q g) -> p t q g", t=NT, q=4)
                for q in range(4):
                    for lo in range(LO):
                        last = mm(ov[:, :, q, :], upM[:, q, lo, :], prod[:, :, :, q * LO + lo],
                                  start=(lo == 0), stop=(lo == LO - 1))
                done(last, "Y", b)

            def N6b(b):
                read_out(pe, "Y", b)
                transposes("YT", b, [(t * P, YTs[:, t * P:t * P + P]) for t in range(NT)])

            do = {"A1a": A1a, "A1b": A1b, "A2d": A2d, "A3a": A3a, "A3b": A3b, "A3c": A3c, "A4": A4, "F5a": F5a,
                  "F5b": F5b, "F5c": F5c, "F6a": F6a, "F6b": F6b, "F6c": F6c, "F7a": F7a, "F7b": F7b, "F8a":
                  F8a, "F8b": F8b, "F8c": F8c, "F9a": F9a, "F9b": F9b, "F9c": F9c, "F9d": F9d, "F10a": F10a,
                  "F10b": F10b, "F11a": F11a, "F11b": F11b, "F11c": F11c, "F12": F12, "NS": NS, "N0a": N0a,
                  "N0b": N0b, "N0c": N0c, "N0d": N0d, "N0e": N0e, "N0f": N0f, "N3a": N3a, "N4": N4, "N5a": N5a,
                  "N5b": N5b, "N6a": N6a, "N6b": N6b}
            for s, b in schedule("tensor"):
                if s in do:
                    do[s](b)

        @block.scalar
        def _(ac):
            fn = nc.scalar.activation
            link = chained(ac, act_chain)

            def A1a(b):
                sampling_free(ac, b)
                if b == 0:
                    ac.wait_ge(wa_loaded, 16)
                    ac.wait_ge(preset, 1)
                o = full(ac, "qimg", b)
                inner = qpad[:, 3:3 + SIDE, 3:3 + SIDE]
                freed(fn(inner, o[:, 0:N].rearrange("p (a b) -> p a b", b=SIDE), ACT.Identity), "qimg", b)
                o = full(ac, "qT", b)
                freed(fn(qT[:, :].rearrange("p (c s) -> p s c", s=2),
                         o[:, 0:N].rearrange("p (s c) -> p s c", s=2), ACT.Identity, bias=vec("bq")), "qT", b)

            def A1b(b):
                o = full(ac, "qhT", b)
                freed(fn(qhT[:, b % 2, :], o[:, 0:N], ACT.Identity, bias=vec("mqb")), "qhT", b)

            def A2c(b):
                p = b % 2
                ac.wait_ge(conv_ready, b + 1)
                fn(osb[:, :], conv[:, :], ACT.Gelu, bias=vec("dwb")).then_inc(osb_ready, 1)

            def A2d(b):
                o = full(ac, "offs", b)
                freed(fn(tanh_[0:NP_, :], o[0:NP_, 0:2], ACT.Tanh), "offs", b)

            def A3a(b):
                p = b % 2
                o = full(ac, "WT", b)
                freed(fn(WTs[:, :, :], o[:, 0:NT * NP_].rearrange("p (s n) -> p s n", s=NT), ACT.Identity), "WT", b)

            def A3b(b):
                o = full(ac, "interp", b)
                freed(fn(ips[0:NP_, :], o[0:NP_, 0:C], ACT.Identity), "interp", b)

            def A3c(b):
                o = full(ac, "vT", b)
                freed(fn(vT[:, :, :], o[:, 0:NP_].unsqueeze(1).broadcast_to([P, 2, NP_]), ACT.Identity,
                         bias=vec("bv")), "vT", b)

            def A4(b):
                p = b % 2
                o = full(ac, "kh", b)
                freed(fn(khT[:, :], o[:, 0:NP_], ACT.Identity, bias=vec("mkb")), "kh", b)
                o = full(ac, "vh", b)
                for r in range(2):
                    q = slice(NP_ * r, NP_ * r + NP_)
                    last = fn(vBD0[q, b % 2, :, r, 0:DH],
                              o[q, 0:C].rearrange("p (a r d) -> p a r d", a=4, r=2)[:, :, r, :], ACT.Identity)
                freed(last, "vh", b)

            def F5b(b):
                front_free(ac, b)
                o = full(ac, "mT", b)
                freed(fn(negMT[0:H, :], o[0:H, 0:N], ACT.Identity), "mT", b)

            def F5c(b):
                for j in range(2):
                    o = full(ac, f"P0_{j}", b)
                    freed(fn(PT0[:, 2 * j:2 * j + 2, :], o[:, :].rearrange("p (i n) -> p i n", i=2), ACT.Exp),
                          f"P0_{j}", b)

            def F6b(b):
                p = b % 2
                o = full(ac, "aT", b)
                freed(fn(attT[:, :], o[:, 0:N], ACT.Identity), "aT", b)

            def F7a(b):
                p = b % 2
                o = full(ac, "zT", b)
                freed(fn(zT[:, :], o[:, 0:N], ACT.Identity, bias=vec("lnb"), scale=vec("lng")), "zT", b)

            def F7b(b):
                o = full(ac, "mlp", b)
                freed(fn(gl[:, :, :], o[:, 0:N].rearrange("p (t c) -> p t c", t=NT), ACT.Gelu), "mlp", b)

            def F8a(b):
                p = b % 2
                o = full(ac, "tT", b)
                freed(fn(tlT[:, :], o[:, 0:N], ACT.Identity), "tT", b)

            def F8b(b):
                o = full(ac, "k1", b)
                freed(fn(kE[:, :, :], o[:, :].rearrange("p (j n) -> p j n", j=2), ACT.Identity), "k1", b)
                o = full(ac, "q1", b)
                freed(fn(q1P[:, :, :], o[:, :].rearrange("p (j n) -> p j n", j=2), ACT.Identity), "q1", b)

            def F8c(b):
                o = full(ac, "v1", b)
                freed(fn(vA[:, :, :, 0:DH], o[:, 0:N].rearrange("p (t h d) -> p t h d", t=NT, h=H), ACT.Identity),
                      "v1", b)

            def F9a(b):
                o = full(ac, "route", b)
                freed(fn(rts[:, :, 0:SEG], o[:, 0:N].rearrange("p (g s) -> p g s", s=SEG), ACT.Identity),
                      "route", b)

            def F10a(b):
                weights_of(b, range(0, H // 2))

            def F10b(b):
                weights_of(b, range(H // 2, H))

            def weights_of(b, heads):
                for h in heads:
                    o = full(ac, f"P1_{h}", b)
                    freed(fn(PT1[:, h, :, :], o[:, :].rearrange("p (k n) -> p k n", k=NT), ACT.Exp,
                             scale=DH ** -0.5), f"P1_{h}", b)

            def F11b(b):
                o = full(ac, "a1T", b)
                freed(fn(attT[:, :], o[:, 0:N], ACT.Identity), "a1T", b)

            def F12(b):
                stored(ac, b, 2)
                o = full(ac, "fT", b)
                freed(fn(fT[:, b % 2, :], o[:, 0:N], ACT.Identity), "fT", b)

            def N0a(b):
                for t in range(NT):
                    o = full(ac, f"Q{t}", b)
                    fn(sq[:, t, :], o[:, :], ACT.Square).then_inc(sq_ready, 1)

            def queries(b, t):
                o = full(ac, f"qsT{t}", b)
                freed(fn(qsT[:, t, :, :], o[:, :].rearrange("p (c n) -> p c n", c=4), ACT.Identity,
                         scale=Bw("fln")[:, 0:1], bias=Bw("fln")[:, 1:2]), f"qsT{t}", b)
                read_out(ac, f"qsT{t}", b)
                fn(sqT[:, t, :, :], qsT[:, t, :, :], ACT.Square).then_inc(sqT_ready, 1)

            def key_scores(b, t):
                for j in range(2):
                    o = full(ac, f"S2_{t}{j}", b)
                    freed(fn(S[:, t, 8 * j:8 * j + 8, :], o[:, :].rearrange("p (l e) -> p l e", e=NK),
                             ACT.Identity), f"S2_{t}{j}", b)

            def N0b(b):
                queries(b, 0)

            def N0c(b):
                key_scores(b, 0)

            def N0d(b):
                queries(b, 1)

            def N0e(b):
                key_scores(b, 1)

            def N2c(b):
                p = b % 2
                if b >= 1:
                    read_out(ac, "G1", b - 1)
                ac.wait_ge(i16_ready, b + 1)
                fn(if_[:, :, :, :], i16[:, :, :, :], ACT.Copy).then_inc(if_ready, 1)
                ac.wait_ge(dv_ready, b + 1)
                fn(ab[:, :, :, :], dv[:, :, :, :], ACT.Exp).then_inc(ab_ready, 1)

            def N3a(b):
                if b >= 1:
                    ac.wait_ge(onehot_dve_ready, b)
                    ac.wait_ge(onehot_pool_ready, b)
                    full(ac, "YT", b - 1)
                    stored(ac, b, 1)
                o = full(ac, "wT", b)
                link(fn(W2[0:KC, 0, :], o[0:KC, :], ACT.Copy))
                o = full(ac, "eT", b)
                freed(fn(eT[0:KC, 0, :], o[0:KC, :], ACT.Copy), "eT", b)

            def N4(b):
                if b >= 1:
                    read_out(ac, "G1", b - 1)
                for j in range(2):
                    o = full(ac, f"I{j}", b)
                    for i in range(2):
                        for t in range(NT):
                            src = o[:, i * N + t * P:i * N + t * P + P].rearrange("p (q g) -> p g q", q=4)
                            last = fn(act[:, t, :, :, 2 * j + i], src, ACT.Gelu)
                    freed(last, f"I{j}", b)

            def N6a(b):
                o = full(ac, "Y", b)
                freed(fn(YTs[:, :], o[:, 0:N], ACT.Identity), "Y", b)

            do = {"A1a": A1a, "A1b": A1b, "A2c": A2c, "A2d": A2d, "A3a": A3a, "A3b": A3b, "A3c": A3c, "A4": A4,
                  "F5b": F5b, "F5c": F5c, "F6b": F6b, "F7a": F7a, "F7b": F7b, "F8a": F8a, "F8b": F8b, "F8c":
                  F8c, "F9a": F9a, "F10a": F10a, "F10b": F10b, "F11b": F11b, "F12": F12, "N0a": N0a, "N0b": N0b,
                  "N0c": N0c, "N0d": N0d, "N0e": N0e, "N2c": N2c, "N3a": N3a, "N4": N4, "N6a": N6a}
            for s, b in schedule("scalar"):
                if s in do:
                    do[s](b)

        @block.vector
        def _(dve):
            v = nc.vector
            link = chained(dve, dve_chain)

            def statistics(k, src):
                for t in range(NT):
                    last = v.bn_stats(stats[:, k, t, :], src[:, t, :])
                link(last)
                for t in range(NT):
                    last = v.bn_aggr(mv[:, k, t, :], stats[:, k, t, :])
                link(last)
                v.tensor_scalar(veps[:, k, :], mv[:, k, :, 1], LN_EPS, None, ALU.add).then_inc(var_ready[k], 1)

            def normalized(k, src, b):
                dve.wait_ge(rstd_ready[k], b + 1)
                for t in range(NT):
                    last = v.tensor_scalar(hat[:, k, t, :], src[:, t, :], mv[:, k, t, 0:1],
                                           rstd[:, k, t:t + 1], ALU.subtract, ALU.mult)
                last.then_inc(hat_ready[k], 1)

            def A0a(b):
                sampling_free(dve, b)
                dve.wait_ge(x_loaded[b], 16)
                statistics(0, x_sb[:, b, :, :])

            def A0b(b):
                normalized(0, x_sb[:, b, :, :], b)

            def A2c(b):
                if b == 0:
                    dve.wait_ge(wa_loaded, 16)
                    read_out(dve, "qimg", b)
                    link(conv_rows(v, 0, CONV_DVE))
                dve.wait_ge(taps_pool_ready, b + 1)
                n = KS * KS if b == 0 else FOLDED
                v.tensor_reduce(conv[:, :], taps[:, 0:n, :].rearrange("p k n -> p n k"), X,
                                ALU.add).then_inc(conv_ready, 1)

            def A3a(b):
                n = slice(0, NP_)
                read_out(dve, "offs", b)
                link(v.tensor_tensor(crd[n, 0, :], tanh_[n, :], A("refs")[n, :], ALU.add))
                link(v.tensor_scalar(crd[n, 1, :], crd[n, 0, :], 1.0, 4.0, ALU.add, ALU.mult))
                link(v.tensor_scalar(crd[n, 2, :], crd[n, 1, :], 1.0, 0.5 * (SIDE - 1), ALU.add, ALU.mult))
                link(v.tensor_tensor(hatw[n, 0, :, :], A("iota")[n, :].unsqueeze(1).broadcast_to([NP_, 2, SIDE]),
                                     crd[n, 2, :].unsqueeze(2).broadcast_to([NP_, 2, SIDE]), ALU.subtract))
                link(v.scalar_tensor_tensor(hatw[n, 1, :, :], hatw[n, 0, :, :], -1.0, hatw[n, 0, :, :],
                                            ALU.mult, ALU.min))
                link(v.tensor_scalar(hatw[n, 2, :, :], hatw[n, 1, :, :], 1.0, 0.0, ALU.add, ALU.max))
                v.tensor_tensor(Wp[n, :, :], hatw[n, 2, 1, :].unsqueeze(2).broadcast_to([NP_, SIDE, SIDE]),
                                hatw[n, 2, 0, :].unsqueeze(1).broadcast_to([NP_, SIDE, SIDE]),
                                ALU.mult).then_inc(hatw_ready, 1)

            def F5a(b):
                front_free(dve, b)
                for t in range(NT):
                    o = full(dve, f"S0_{t}", b)
                    freed(v.tensor_reduce(negM[:, t, :], o[:, :].rearrange("p (h k) -> p h k", h=H), X, ALU.max,
                                          negate=True), f"S0_{t}", b)
                for t in range(NT):
                    read_out(dve, f"S0_{t}", b)
                v.engine_nop().then_inc(negm_ready, 1)

            def normalize(job, k, b):
                p = b % 2
                o = full(dve, job, b)
                ov = o[:, 0:NT * H * (DH + 1)].rearrange("p (g d) -> p g d", d=DH + 1)
                link(v.reciprocal(rec[:, k, :], ov[:, :, DH]))
                freed(v.tensor_tensor(att[:, :, :].rearrange("p t (h d) -> p (t h) d", d=DH), ov[:, :, 0:DH],
                                      rec[:, k, :].unsqueeze(2).broadcast_to([P, NT * H, DH]), ALU.mult), job, b)

            def F6a(b):
                normalize("O0", 0, b)

            def F6c(b):
                o = full(dve, "msa", b)
                freed(v.tensor_tensor(z[:, :, :], o[:, 0:N].rearrange("p (t c) -> p t c", t=NT),
                                      x_sb[:, b, :, :], ALU.add), "msa", b)
                read_out(dve, "msa", b)
                statistics(1, z[:, :, :])

            def F7a(b):
                normalized(1, z[:, :, :], b)

            def F7b(b):
                p = b % 2
                read_out(dve, "mlp", b)
                v.tensor_tensor(t0[:, :, :], gl[:, :, :], z[:, :, :], ALU.add).then_inc(t0_ready, 1)
                dve.wait_ge(t0_ready, b + 1)
                statistics(2, t0[:, :, :])

            def F8a(b):
                normalized(2, t0[:, :, :], b)

            def F8b(b):
                read_out(dve, "k1", b)
                link(v.tensor_reduce(cent[:, :, :], kE[:, :, :].rearrange("p j (s n) -> p j s n", n=SEG), X, ALU.add))
                v.tensor_tensor(centBD[:, :, :].rearrange("p (j h) s -> p j h s", j=2),
                                cent[:, :, :].unsqueeze(2).broadcast_to([P, 2, 4, SEG]),
                                Bw("hm32").unsqueeze(1).unsqueeze(3).broadcast_to([P, 2, 4, SEG]),
                                ALU.mult).then_inc(centbd_ready, 1)

            def F9a(b):
                read_out(dve, "route", b)
                for g in range(NT * H):
                    last = v.max(r8[:, g, :], rts[:, g, :])
                link(last)
                for g in range(NT * H):
                    last = v.match_replace(rtm[:, g, :], r8[:, g, :], rts[:, g, :], MARK)
                link(last)
                link(v.tensor_scalar(pen[:, :, :], rtm[:, :, 0:SEG], 0.5 * MARK, HIDE, ALU.is_gt, ALU.mult))

            def segment_maxima(b, t):
                for i in range(4):
                    job = f"S1_{t}{i}"
                    o = full(dve, job, b)
                    freed(v.tensor_reduce(segmax[:, t * H + 2 * i:t * H + 2 * i + 2, :],
                                          o[:, :].rearrange("p (g n) -> p g n", n=SEG), X, ALU.max), job, b)

            def F9b(b):
                segment_maxima(b, 0)

            def F9c(b):
                segment_maxima(b, 1)
                for i in range(4):
                    read_out(dve, f"S1_1{i}", b)
                link(v.tensor_tensor(sel[:, :, :], segmax[:, :, :], pen[:, :, :], ALU.add))
                link(v.tensor_reduce(selM[:, :], sel[:, :, :], X, ALU.max))
                v.tensor_tensor(bias[:, :, 1, :], pen[:, :, :],
                                selM[:, :].unsqueeze(2).broadcast_to([P, NT * H, SEG]),
                                ALU.subtract).then_inc(bias_ready, 1)

            def F9d(b):
                o = full(dve, "bT", b)
                freed(v.tensor_tensor(qB[:, :, :], o[:, :].rearrange("p (j n) -> p j n", j=2), q1P[:, :, :], ALU.add),
                      "bT", b)

            def F11a(b):
                normalize("O1", 1, b)

            def F11c(b):
                p = b % 2
                stored(dve, b, 2)
                o = full(dve, "proj", b)
                freed(v.tensor_tensor(t1[:, p, :, :], o[:, 0:N].rearrange("p (t c) -> p t c", t=NT),
                                      t0[:, :, :], ALU.add), "proj", b)
                read_out(dve, "proj", b)
                statistics(3, t1[:, p, :, :])

            def F12(b):
                normalized(3, t1[:, b % 2, :, :], b)

            def NS(b):
                k = slice(0, NK)
                dve.wait_ge(wb_loaded, 16)
                dve.wait_ge(rows_loaded, 16)
                keys = Bw("keys")
                link(v.tensor_tensor(ksq[k, :], keys[k, :], keys[k, :], ALU.mult))
                link(v.tensor_reduce(kss[k, 0, :], ksq[k, :].rearrange("p (a d) -> p a d", a=4), X, ALU.add))
                v.tensor_scalar(kss[k, 1, :], kss[k, 0, :], 1e-24, None, ALU.max).then_inc(kss_ready, 1)
                dve.wait_ge(kinv_ready, 1)
                v.tensor_tensor(kn[k, :].rearrange("p (a d) -> p a d", a=4),
                                keys[k, :].rearrange("p (a d) -> p a d", a=4),
                                kss[k, 2, :].unsqueeze(2).broadcast_to([NK, 4, 32]), ALU.mult).then_inc(kn_ready, 1)
                for i, (src, n) in enumerate(((Bw("Wq"), P), (rows[0:3, offR["fbq"][0]:NR], 3))):
                    sv = src.rearrange("p (h q) -> p h q", h=H)
                    link(v.tensor_reduce(wmean[0:n, i, :], sv, X, ALU.add))
                    last = v.scalar_tensor_tensor(sv, wmean[0:n, i, :].unsqueeze(2).broadcast_to([n, H, QD]),
                                                  -1.0 / QD, sv, ALU.mult, ALU.add)
                    if i == 0:
                        last.then_inc(WqC_ready, 1)
                    else:
                        link(last)
                r, pick = slice(0, 3), Bw("pick")
                link(v.tensor_copy(rparts[r, 0, :], rows[r, :]))
                link(v.tensor_tensor(rrest[r, 0, :], rows[r, :], rparts[r, 0, :], ALU.subtract))
                link(v.tensor_copy(rparts[r, 1, :], rrest[r, 0, :]))
                link(v.tensor_tensor(rparts[r, 2, :], rrest[r, 0, :], rparts[r, 1, :], ALU.subtract))
                link(v.tensor_scalar(rrest[r, 1, :], rparts[r, 0, :], pick[r, 0:1], None, ALU.mult))
                link(v.scalar_tensor_tensor(rrest[r, 0, :], rparts[r, 1, :], pick[r, 1:2], rrest[r, 1, :],
                                            ALU.mult, ALU.add))
                v.scalar_tensor_tensor(rows3[r, :], rparts[r, 2, :], pick[r, 2:3], rrest[r, 0, :],
                                       ALU.mult, ALU.add).then_inc(rows3_ready, 1)
                link(v.memset(KB[:, :], 0.0))
                o = full(dve, "keys", b)
                for i in range(4):
                    q = slice(32 * i, 32 * i + 32)
                    last = v.tensor_copy(KB[q, NK * i:NK * i + NK], o[q, 0:NK])
                freed(last, "keys", b)
                read_out(dve, "keys", b)
                v.engine_nop().then_inc(KB_ready, 1)

            def N0a(b):
                for t in range(NT):
                    dve.wait_ge(sq_ready, NT * b + t + 1)
                    link(v.tensor_reduce(ssq[:, t, 0, :], sq[:, t, :].rearrange("p (h q) -> p h q", h=H), X, ALU.add))
                    v.tensor_scalar(ssq[:, t, 1, :], ssq[:, t, 0, :], 1.0 / QD, LN_EPS, ALU.mult,
                                    ALU.add).then_inc(qvar_ready, 1)
                for t in range(NT):
                    dve.wait_ge(qrstd_ready, NT * b + t + 1)
                    o = full(dve, f"Q{t}", b)
                    freed(v.tensor_tensor(qn[:, t, :].rearrange("p (h q) -> p h q", h=H),
                                          o[:, :].rearrange("p (h q) -> p h q", h=H),
                                          qrstd[:, t, :].unsqueeze(2).broadcast_to([P, H, QD]), ALU.mult),
                          f"Q{t}", b)

            def top_keys(b, i):
                t, half = i // 2, i % 2
                lists = slice(8 * half, 8 * half + 8)
                vt = vraw[:, t * H:t * H + H, :, :].rearrange("p h a k -> p (h a) k")[:, lists, :]
                it = i16[:, t * H:t * H + H, :, :].rearrange("p h a k -> p (h a) k")[:, lists, :]
                sv, sx = S[:, t, lists, :], Sx[:, t, lists, :]
                read_out(dve, f"S2_{t}{half}", b)
                for g in range(8):
                    last = v.max(vt[:, g, 0:8], sv[:, g, :])
                link(last)
                for g in range(8):
                    last = v.match_replace(sx[:, g, :], vt[:, g, 0:8], sv[:, g, :], MARK)
                link(last)
                for g in range(8):
                    last = v.max(vt[:, g, 8:16], sx[:, g, :])
                link(last)
                for g in range(8):
                    v.max_index(it[:, g, 0:8], vt[:, g, 0:8], sv[:, g, :])
                    last = v.max_index(it[:, g, 8:16], vt[:, g, 8:16], sx[:, g, :])
                return last

            def N1_0(b):
                top_keys(b, 0)

            def N1_1(b):
                o = full(dve, "norm", b)
                freed(v.tensor_scalar(nrm[:, :], o[:, 0:NT * 2 * H], 1e-24, None, ALU.max), "norm", b)
                top_keys(b, 1)

            def N1_2(b):
                top_keys(b, 2)

            def N1_3(b):
                top_keys(b, 3).then_inc(i16_ready, 1)

            def N2a(b):
                dve.wait_ge(inv_ready, b + 1)
                dve.wait_ge(i16_ready, b + 1)
                v.tensor_tensor(v16[:, :, :, :].rearrange("p g a k -> p (g a) k"),
                                vraw[:, :, :, :].rearrange("p g a k -> p (g a) k"),
                                inv[:, :].unsqueeze(2).broadcast_to([P, NT * 2 * H, TOP]),
                                ALU.mult).then_inc(v16_ready, 1)
                dve.wait_ge(v16_ready, b + 1)
                for i0, r, c, at in CELL_BLOCKS:
                    last = v.tensor_tensor(cand[:, :, at:at + r * c].rearrange("p g (r c) -> p g r c", r=r),
                                           v16[:, :, 0, i0:i0 + r].unsqueeze(3).broadcast_to([P, NT * H, r, c]),
                                           v16[:, :, 1, 0:c].unsqueeze(2).broadcast_to([P, NT * H, r, c]), ALU.add)
                link(last)
                for g in range(NT * H):
                    last = v.max(c8[:, g, 0, :], cand[:, g, :])
                link(last)
                for g in range(NT * H):
                    last = v.match_replace(candx[:, g, :], c8[:, g, 0, :], cand[:, g, :], MARK)
                link(last)

            def N2b(b):
                for g in range(NT * H):
                    last = v.max(c8[:, g, 1, :], candx[:, g, :])
                link(last)
                for g in range(NT * H):
                    last = v.match_replace(candm[:, g, :], c8[:, g, 1, :], candx[:, g, :], MARK)
                link(last)

            def N2c(b):
                dve.wait_ge(we_ready, b + 1)
                n = NT * H * CELLS
                if b >= 1:
                    dve.wait_ge(slots_ready, b)
                link(v.scalar_tensor_tensor(
                    wem[:, :, :, :].rearrange("p a g c -> p a (g c)"),
                    candm[:, :, :].rearrange("p g c -> p (g c)").unsqueeze(1).broadcast_to([P, 2, n]), MARK,
                    we[:, :, :, :].rearrange("p a g c -> p a (g c)"), ALU.is_equal, ALU.mult))
                link(v.tensor_reduce(zs[:, 0, :], wem[:, 0, :, :], X, ALU.add))
                link(v.reciprocal(zs[:, 1, :], zs[:, 0, :]))
                v.tensor_scalar(zs[:, 2, :], zs[:, 1, :], W_SCALE, None, ALU.mult).then_inc(wem_ready, 1)

            def N3a(b):
                if b >= 1:
                    full(dve, "G1", b - 1)
                read_out(dve, "eT", b)
                v.tensor_scalar(eT[0:KC, 1, :], eT[0:KC, 0, :], LO - 1, None, ALU.bitwise_and)
                v.tensor_scalar(eT[0:KC, 2, :], eT[0:KC, 0, :], E - LO, None,
                                ALU.bitwise_and).then_inc(eT_ready, 1)
                o = full(dve, "wT", b)
                dve.wait_ge(act_chain, b + 1)
                freed(v.tensor_tensor(W2[0:KC, 1, :], o[0:KC, :], W2[0:KC, 0, :], ALU.subtract), "wT", b)
                dve.wait_ge(eT_ready, b + 1)
                for lo in range(LO):
                    last = v.tensor_scalar(lom[0:KC, lo, :], eT[0:KC, 1, :], float(lo), None, ALU.is_equal)
                link(last)
                read_out(dve, "wT", b)
                for lo in range(LO):
                    v.tensor_tensor(R[0:KC, :, lo, :], W2[0:KC, :, :],
                                    lom[0:KC, lo, :].unsqueeze(1).broadcast_to([KC, 2, NCH * N]), ALU.mult)

            def N3b(b):
                for hi in range(POOL_HI, HI):
                    last = v.tensor_scalar(OH[0:KC, :, :, hi, :], hi_view(eT), float(LO * hi), None, ALU.is_equal)
                last.then_inc(onehot_dve_ready, 1)

            def products(b, t):
                o = full(dve, f"G{t}", b)
                freed(v.tensor_tensor(
                    prod[:, t, :, :], o[:, :].rearrange("p (g e) -> p g e", g=32),
                    act[:, t, :, :, :].rearrange("p g q l -> p g (q l)"), ALU.mult), f"G{t}", b)

            def N5a(b):
                read_out(dve, "I0", b)
                read_out(dve, "I1", b)
                if b >= 1:
                    full(dve, "Y", b - 1)
                products(b, 0)

            def N5b(b):
                products(b, 1)

            def N6b(b):
                p = b % 2
                stored(dve, b, 1)
                o = full(dve, "YT", b)
                ins = v.tensor_tensor(outs[:, :, :], o[:, 0:N].rearrange("p (t c) -> p t c", t=NT),
                                      t1[:, p, :, :], ALU.add)
                freed(ins, "YT", b)
                read_out(dve, "YT", b)
                v.engine_nop().then_inc(out_ready, 1)

            do = {"A0a": A0a, "A0b": A0b, "A2c": A2c, "A3a": A3a, "F5a": F5a, "F6a": F6a, "F6c": F6c,
                  "F7a": F7a, "F7b": F7b, "F8a": F8a, "F8b": F8b, "F9a": F9a, "F9b": F9b, "F9c": F9c, "F9d":
                  F9d, "F11a": F11a, "F11c": F11c, "F12": F12, "NS": NS, "N0a": N0a, "N1_0": N1_0, "N1_1": N1_1,
                  "N1_2": N1_2, "N1_3": N1_3, "N2a": N2a, "N2b": N2b, "N2c": N2c, "N3a": N3a, "N3b": N3b, "N5a":
                  N5a, "N5b": N5b, "N6b": N6b}
            for s, b in schedule("vector"):
                if s in do:
                    do[s](b)

        @block.gpsimd
        def _(pool):
            g_ = nc.gpsimd
            link = chained(pool, pool_chain)

            g_.memset(mhalf[:, :], -0.5)
            g_.memset(ones[:, :], 1.0)
            g_.memset(qpad[:, :, :], 0.0)
            g_.memset(rts[:, :, :], LARGE)
            g_.memset(bias[:, :, :, :], 0.0)
            g_.memset(ones3[:, :], 1.0)
            link(g_.memset(vBD0[:, :, :, :, :], 0.0))
            for r in range(2):
                link(g_.memset(vBD0[NP_ * r:NP_ * r + NP_, :, :, r, DH:DH + 1], 1.0))
            g_.memset(vA[:, :, :, DH:DH + 1], 1.0).then_inc(preset, 1)
            pool.wait_ge(preset, 1)

            def inverse_root(k, b):
                p = b % 2
                pool.wait_ge(var_ready[k], b + 1)
                g_.tensor_tensor(rstd[:, k, :], veps[:, k, :], mhalf[:, 0:NT], ALU.pow)\
                    .then_inc(rstd_ready[k], 1)

            def A0a(b):
                sampling_free(pool, b)
                inverse_root(0, b)

            def A0b(b):
                if b == 0:
                    pool.wait_ge(wa_loaded, 16)
                pool.wait_ge(hat_ready[0], b + 1)
                link(g_.tensor_tensor(xg[:, :, :], hat[:, 0, :, :],
                                      A("lng").unsqueeze(1).broadcast_to([P, NT, C]), ALU.mult))
                g_.tensor_tensor(xln[:, :, :], xg[:, :, :],
                                 A("lnb").unsqueeze(1).broadcast_to([P, NT, C]), ALU.add).then_inc(xln_ready, 1)

            def A2a(b):
                if b == 0:
                    pool.wait_ge(wa_loaded, 16)
                read_out(pool, "qimg", b)
                if b == 0:
                    conv_rows(g_, CONV_DVE, KS).then_inc(taps_pool_ready, 1)
                else:
                    pool.wait_ge(conv_ready, b)
                    link(conv_rows(g_, 0, KS))

            def A2b(b):
                if b >= 1:
                    n = 2 * (FOLDED - 1)
                    link(g_.tensor_tensor(taps[:, 1:1 + n, :], taps[:, 1:1 + n, :], taps[:, 1 + n:1 + 2 * n, :],
                                          ALU.add))
                    n = FOLDED - 1
                    g_.tensor_tensor(taps[:, 1:1 + n, :], taps[:, 1:1 + n, :], taps[:, 1 + n:1 + 2 * n, :],
                                     ALU.add).then_inc(taps_pool_ready, 1)

            def A4(b):
                read_out(pool, "kh", b)
                g_.tensor_tensor(kBD0[:, b % 2, :, :], khT[:, :].unsqueeze(1).broadcast_to([P, H, NP_]),
                                hm.unsqueeze(2).broadcast_to([P, H, NP_]), ALU.mult).then_inc(kbd0_ready, 1)

            def F6c(b):
                inverse_root(1, b)

            def F7b(b):
                inverse_root(2, b)

            def F8b(b):
                front_free(pool, b)
                read_out(pool, "k1", b)
                g_.tensor_tensor(kBD1[:, :, :].rearrange("p (j h) n -> p j h n", j=2),
                                 kE[:, :, :].unsqueeze(2).broadcast_to([P, 2, 4, N]),
                                 Bw("hm32").unsqueeze(1).unsqueeze(3).broadcast_to([P, 2, 4, N]),
                                 ALU.mult).then_inc(kbd1_ready, 1)

            def F11c(b):
                inverse_root(3, b)

            def NS(b):
                k = slice(0, NK)
                pool.wait_ge(kss_ready, 1)
                g_.tensor_tensor(kss[k, 2, :], kss[k, 1, :], mhalf[k, 0:4], ALU.pow).then_inc(kinv_ready, 1)
                pool.wait_ge(wb_loaded, 16)
                g_.tensor_copy(ident16[:, :], ident)
                g_.tensor_copy(Epat16[:, :], Bw("Epat"))
                qm = Bw("qmask")
                for q in range(4):
                    last = g_.tensor_scalar(upM[:, q, :, :].rearrange("p l c -> p (l c)"), Bw("upR"), qm[:, q:q + 1],
                                            None, ALU.mult)
                last.then_inc(upM_ready, 1)

            def N0a(b):
                for t in range(NT):
                    pool.wait_ge(qvar_ready, NT * b + t + 1)
                    g_.tensor_tensor(qrstd[:, t, :], ssq[:, t, 1, :], mhalf[:, 0:H], ALU.pow).then_inc(qrstd_ready, 1)

            def N1_1(b):
                read_out(pool, "norm", b)
                g_.tensor_tensor(inv[:, :], nrm[:, :], mhalf[:, :], ALU.pow).then_inc(inv_ready, 1)

            def N2c(b):
                p = b % 2
                pool.wait_ge(v16_ready, b + 1)
                if b >= 1:
                    full(pool, "G1", b - 1)
                    read_out(pool, "G1", b - 1)
                vv = v16[:, :, :, :].rearrange("p g a k -> p (g a) k")
                g_.tensor_tensor(dv[:, :, :, :].rearrange("p g a k -> p (g a) k"), vv,
                                 vv[:, :, 0:1].broadcast_to([P, 2 * NT * H, TOP]), ALU.subtract).then_inc(dv_ready, 1)
                for s, (src, ready, op) in enumerate(((ab, ab_ready, ALU.mult), (if_, if_ready, ALU.add))):
                    pool.wait_ge(ready, b + 1)
                    for i0, r, c, at in CELL_BLOCKS:
                        last = g_.tensor_tensor(
                            we[:, s, :, at:at + r * c].rearrange("p g (r c) -> p g r c", r=r),
                            src[:, :, 0, i0:i0 + r].unsqueeze(3).broadcast_to([P, NT * H, r, c]),
                            src[:, :, 1, 0:c].unsqueeze(2).broadcast_to([P, NT * H, r, c]), op)
                last.then_inc(we_ready, 1)
                if b >= 1:
                    read_out(pool, "eT", b - 1)
                    read_out(pool, "wT", b - 1)
                pool.wait_ge(wem_ready, b + 1)
                src = wem[:, :, :, :].rearrange("p a g c -> p (a g) c")
                dst = slots[:, :, :, :].rearrange("p a g c -> p (a g) c")
                for at, c, step, n in SLOT_COPIES:
                    g_.tensor_copy(dst[:, :, at:at + n], src[:, :, c:c + step * (n - 1) + 1:step])
                for at, c, step, c2, step2, n in SLOT_SUMS:
                    end = c2 + step2 * (n - 1) - 1
                    last = g_.tensor_tensor(dst[:, :, at:at + n], src[:, :, c:c + n], src[:, :, c2:end:step2], ALU.add)
                link(last)
                g_.tensor_tensor(wn[:, :, :], slots[:, 0, :, :],
                                 zs[:, 2, :].unsqueeze(2).broadcast_to([P, NT * H, SLOTS]), ALU.mult)\
                    .then_inc(slots_ready, 1)

            def N3b(b):
                if b >= 1:
                    full(pool, "G1", b - 1)
                pool.wait_ge(eT_ready, b + 1)
                for hi in range(0, POOL_HI):
                    last = g_.tensor_scalar(OH[0:KC, :, :, hi, :], hi_view(eT), float(LO * hi), None, ALU.is_equal)
                last.then_inc(onehot_pool_ready, 1)

            do = {"A0a": A0a, "A0b": A0b, "A2a": A2a, "A2b": A2b, "A4": A4, "F6c": F6c, "F7b": F7b, "F8b": F8b, "F11c": F11c, "NS":
                  NS, "N0a": N0a, "N1_1": N1_1, "N2c": N2c, "N3b": N3b}
            for s, b in schedule("gpsimd"):
                if s in do:
                    do[s](b)


def kernel(**inputs):
    import numpy as np
    import concourse.bacc as bacc
    from concourse.bass_utils import run_bass_kernel_spmd

    a = {k: np.asarray(v) for k, v in inputs.items()}
    f = np.float32

    def bc(v, n=P):
        return np.broadcast_to(v.reshape(1, -1), (n, v.size))

    def pad(v):
        out = np.zeros((P, v.shape[1]), f)
        out[:v.shape[0]] = v
        return out

    ch = np.arange(P)
    pos = np.arange(NP_)
    ref = ((np.arange(G8, dtype=f) + f(0.5)) * f(2.0 / G8) - f(1.0)).astype(f)
    heads = (ch[:, None] // DH == np.arange(H)[None, :]).astype(f)
    col0 = np.arange(H * NP_)
    E0 = (np.arange(P)[:, None] == (col0 // NP_)[None, :]).astype(f)
    Epat = (ch[:, None] % 32 - DH == np.arange(N)[None, :] // SEG).astype(f)
    blocks = (ch[:, None] // 32 == np.arange(4)[None, :]).astype(f)
    pick = (ch[:, None] == np.arange(3)[None, :]).astype(f)
    quarter = (ch[:, None] // HI == np.arange(4)[None, :]).astype(f) / f(W_SCALE)

    vecs = np.stack([a["L0_conv_" + n] for n in ("ln_g", "ln_b", "bq", "bv", "dw_b", "mq_b", "mk_b")]
                    + [a["L0_conv_bq"]], axis=1)
    wv = a["L0_conv_wv"]
    down = a["L1_ffn_expert_down"][:E]
    up = a["L1_ffn_expert_up"][:E]
    downR = np.broadcast_to(down.reshape(HI, LO, C).transpose(2, 1, 0)[:, :, None, :], (C, LO, 4, HI))
    upR = np.broadcast_to(up.reshape(1, HI, LO * C), (4, HI, LO * C))
    k0, k1 = a["L1_ffn_keys0"], a["L1_ffn_keys1"]
    A = {"ident": np.eye(P, dtype=f), "wq": a["L0_conv_wq"], "lng": bc(a["L0_conv_ln_g"]),
         "lnb": bc(a["L0_conv_ln_b"]), "vecs": vecs, "pw": a["L0_conv_pw_w"].reshape(2, C)[::-1].T,
         "refs": pad(np.stack([ref[pos % G8], ref[pos // G8]], axis=1)), "iota": bc(np.arange(SIDE, dtype=f)),
         "hm": heads, "dw": a["L0_conv_dw_w"].reshape(C, KS * KS),
         "wv2": pad(wv.reshape(2, NP_, C).transpose(1, 0, 2).reshape(NP_, 2 * C)),
         "mq": a["L0_conv_mq_w"], "mk": a["L0_conv_mk_w"], "mv": a["L0_conv_mv_w"], "mo": a["L0_conv_mo_w"],
         "mlp": a["L0_conv_mlp_w"], "E0": E0}
    wqk = np.zeros((C, 2, H, 32), f)
    wqk[:, :, :, :DH] = a["L1_attn_w_qkv"].T[:, :2 * C].reshape(C, 2, H, DH)
    Bm = {"wqk": wqk.reshape(C, 4 * P), "wv1": a["L1_attn_w_qkv"].T[:, 2 * C:], "wproj": a["L1_attn_w_proj"].T, "Wq": a["L1_ffn_Wq"].T,
          "fln": np.tile(np.stack([a["L1_ffn_ln_g"], a["L1_ffn_ln_b"]], axis=1), (2, 1)), "downR": downR.reshape(C, -1),
          "upR": upR.reshape(P, -1), "qmask": quarter, "keys": pad(np.concatenate([k0, k1, k0, k1], axis=1)),
          "hm32": blocks, "Epat": Epat, "pick": pick}
    rows = {"bq": a["L0_conv_bq"], "mvb": a["L0_conv_mv_b"], "mob": a["L0_conv_mo_b"], "mlpb": a["L0_conv_mlp_b"],
            "bproj": a["L1_attn_b_proj"], "fbq": a["L1_ffn_bq"]}
    arrays = {
        "x": np.ascontiguousarray(a["x"].reshape(B, NT, P, C).transpose(0, 2, 1, 3)),
        "wa": np.ascontiguousarray(np.concatenate([A[n] for n, _ in WEIGHTS_A], axis=1)),
        "wb": np.ascontiguousarray(np.concatenate([Bm[n] for n, _ in WEIGHTS_B], axis=1)),
        "rows": np.ascontiguousarray(bc(np.concatenate([rows[n] for n, _ in ROWS]), 3)),
    }
    nc = bacc.Bacc("TRN2", target_bir_lowering=False, num_devices=1)
    args = [nc.dram_tensor(n + "_dram", v.shape, mybir.dt.from_np(v.dtype), kind="ExternalInput").ap()
            for n, v in arrays.items()]
    out = nc.dram_tensor("out_dram", (B, P, NT, C), F32, kind="ExternalOutput").ap()
    build(nc, *args, out)
    r = run_bass_kernel_spmd(nc, [{n + "_dram": v for n, v in arrays.items()}], core_ids=[0])
    got = r.results[0]["out_dram"]
    return np.ascontiguousarray(got.transpose(0, 2, 1, 3)).reshape(B, SIDE, SIDE, C)
```

```python
from contextlib import ExitStack

import concourse.bass as bass
from concourse import mybir

ALU = mybir.AluOpType
ACT = mybir.ActivationFunctionType
X = mybir.AxisListType.X
F32 = mybir.dt.float32
F16 = mybir.dt.float16
BF16 = mybir.dt.bfloat16
U16 = mybir.dt.uint16

P = 128
B = 4
SIDE = 16
C = 128
NT = 2
N = NT * P
H = 8
DH = C // H
KS = 7
PADDED = SIDE + 6
G8 = 8
NP_ = G8 * G8
SEG = 16
TOP = 16
NK = 64
QD = 64
E = 128
LN_EPS = 1e-5
MARK = -3.0e38
LARGE = 3.0e38
HIDE = -1.0e30
LO = 4
HI = E // LO
CONV_DVE = 4
FOLDED = 4
POOL_HI = 4
W_SCALE = 2.0 ** 15

CELL_BLOCKS = [(0, 1, 16, 0), (1, 1, 8, 16), (2, 2, 5, 24), (4, 4, 3, 34), (8, 8, 1, 46)]
CELLS = 54
SLOT_SUMS = [
    (1, 1, 1, 53, -1, 8),
    (9, 9, 1, 43, -3, 4),
    (13, 13, 1, 29, -5, 2),
    (15, 15, 1, 16, -5, 1),
    (16, 18, 1, 44, -3, 4),
    (20, 22, 1, 30, -5, 2),
    (22, 27, 1, 36, -5, 2),
]
SLOT_COPIES = [(0, 0, 1, 1), (24, 17, 9, 2), (26, 32, 1, 1)]
SLOTS = 27
HC = 4
KC = HC * SLOTS
NCH = H // HC

FRONT_JOBS = {
    "A1a": ["qimg", "qT"], "A1b": ["qhT"],
    "A2d": ["offs"],
    "A3a": ["WT"], "A3b": ["interp"], "A3c": ["vT"],
    "A4": ["kh", "vh"],
    "F5a": ["S0_0", "S0_1"], "F5b": ["mT"], "F5c": ["P0_0", "P0_1"],
    "F6a": ["O0"], "F6b": ["aT"], "F6c": ["msa"],
    "F7a": ["zT"], "F7b": ["mlp"],
    "F8a": ["tT"], "F8b": ["k1", "q1"], "F8c": ["v1"],
    "F9a": ["route"],
    "F9b": ["S1_00", "S1_01", "S1_02", "S1_03"], "F9c": ["S1_10", "S1_11", "S1_12", "S1_13"],
    "F9d": ["bT"],
    "F10a": ["P1_0", "P1_1", "P1_2", "P1_3"], "F10b": ["P1_4", "P1_5", "P1_6", "P1_7"],
    "F11a": ["O1"], "F11b": ["a1T"], "F11c": ["proj"],
    "F12": ["fT"],
}
EXPERT_JOBS = {
    "NS": ["keys"],
    "N0a": ["Q0"], "N0h": ["Q1"],
    "N0b": ["qsT0"], "N0c": ["S2_00", "S2_01"], "N0d": ["qsT1"], "N0e": ["S2_10", "S2_11"], "N0f": ["norm0"], "N0g": ["norm1"],
    "N3a": ["wT", "eT"],
    "N4": ["I"],
    "N5a": ["G0"], "N5b": ["G1"],
    "N6a": ["Y"], "N6b": ["YT"],
}
FRONT_BANKS = [0, 1, 2, 3]
EXPERT_BANKS = [4, 5, 6, 7]

ORDERS = {
    "tensor": """F11b- F11c- F5b N3a- A1a F12- N4- F5c N0a N0h F6a N5a- F6b N0b N5b- F6c N0c N0f N0d F7a A1b F7b
        N6a- N6b- F8a A2d F8b A3a F8c F9a A3b F9b NS F9c N0e A3c F9d N0g A4 F10a F10b F11a F5a+""".split(),
    "scalar": """F10b- A0b N2q- F11b- F5b N3a- F12- A1a N4- F5c N0a N0h F6b N0b N0c F7a F7b A1b A2c N6a- F8a A2d
        F8b A3a F8c F9a N0d A3b N2p A3c N0e A4 F10a""".split(),
    "vector": """N0g- N1_2- N1_3- A0a N2d- NB+ N2e- N2f- F11a- F5a F11c- N3a- N3b- N0a N0h F6a N0b N0d N5a- F6c
        N5b- N0f N1_0 F7b A2c N1_1 A3a N6b- F8b N2a F9a F9b NS N2b F9c N2c F9d""".split(),
    "gpsimd": """N0f- A3a- F8b- N2a- N2c- A4- N0g- A0a N2d- A0b N2f- F11c- N3b- A2a N0a N0h A2a2 F6c A2b NS A2b2
        F7b""".split(),
}


def schedule(engine):
    out = []
    for b in range(-1, B + 2):
        for name in ORDERS[engine]:
            s = name.rstrip("+-")
            image = b + {"A": 1, "F": 0, "N": -1}[s[0]] + name.count("+") - name.count("-")
            if s in ("NS", "NB"):
                image = 0 if b == -1 else B
            if 0 <= image < B:
                out.append((s, image))
    return out


def place_jobs():
    turn, count, out = {0: 0, 1: 0}, [0] * 8, {}
    for s, b in schedule("tensor"):
        ring = 0 if s in FRONT_JOBS else 1
        banks = (FRONT_BANKS, EXPERT_BANKS)[ring]
        for job in (FRONT_JOBS, EXPERT_JOBS)[ring].get(s, []):
            k = banks[turn[ring] % len(banks)]
            turn[ring] += 1
            count[k] += 1
            out[job, b] = (k, count[k])
    return out


WEIGHTS_A = [("ident", 128), ("wq", 128), ("lng", 128), ("lnb", 128), ("vecs", 8), ("pw", 2), ("less", 2), ("refs", 2),
             ("iota", 16), ("hm", 8), ("dw", 49), ("wv2", 256), ("mq", 128), ("mk", 128), ("mv", 128),
             ("mo", 128), ("mlp", 128), ("E0", 512)]
WEIGHTS_B = [("wqk", 512), ("wv1", 128), ("wproj", 128), ("Wq", 512), ("fln", 2), ("down", E), ("hm32", 4)]
WEIGHTS_S = [("upR", 512), ("keys", 128), ("Epat", N)]
ROWS = [("bq", 128), ("mvb", 128), ("mob", 128), ("mlpb", 128), ("bproj", 128), ("fbq", 512)]
VEC = {n: i for i, n in enumerate(["lng", "lnb", "bq", "bv", "dwb", "mqb", "mkb"])}


def offsets(parts):
    out, at = {}, 0
    for n, k in parts:
        out[n] = (at, k)
        at += k
    return out, at


def build(nc, x_in, wa_in, wb_in, ws_in, rows_in, out):
    jobs = place_jobs()
    offA, NA = offsets(WEIGHTS_A)
    offB, NB = offsets(WEIGHTS_B)
    offS, NS_ = offsets(WEIGHTS_S)
    offR, NR = offsets(ROWS)

    ctx = ExitStack()
    with ctx:
        def sb(name, shape, dt=F32):
            return ctx.enter_context(nc.sbuf_tensor(name, [P] + list(shape), dt))

        def sem(name):
            return ctx.enter_context(nc.semaphore(name))

        wa = sb("wa", [NA])
        wb = sb("wb", [NB])
        bq_row = sb("bq_row", [C])
        KB = sb("KB", [2 * 2 * NK])
        up = sb("up", [LO, C])
        mhalf = sb("mhalf", [2 * NT * H])
        ones = sb("ones", [P])

        def A(n):
            at, k = offA[n]
            return wa[:, at:at + k]

        def Bw(n):
            at, k = offB[n]
            return wb[:, at:at + k]

        def Sw(n):
            at, k = offS[n]
            return ws[:, at:at + k]

        def vec(n):
            at = offA["vecs"][0] + VEC[n]
            return wa[:, at:at + 1]

        ident = A("ident")
        hm = A("hm")

        x_sb = sb("x_sb", [B, NT, C])
        stats = sb("stats", [4, NT, 6])
        mv = sb("mv", [4, NT, 2])
        veps = sb("veps", [4, NT])
        rstd = sb("rstd", [4, NT])
        negmean = sb("negmean", [4, NT])
        shift = sb("shift", [4, NT])
        hat = sb("hat", [4, NT, C])
        xln = sb("xln", [NT, C])
        qpad = sb("qpad", [PADDED, PADDED])
        taps = sb("taps", [KS * KS, NP_])
        conv = sb("conv", [NP_])
        qT = sb("qT", [N])
        qhT = sb("qhT", [2, N])
        osb = sb("osb", [NP_])
        tanh_ = sb("tanh_", [2])
        crd = sb("crd", [3, 2])
        hatw = sb("hatw", [3, 2, SIDE])
        Wp = sb("Wp", [SIDE, SIDE])
        WTs = sb("WTs", [NT, NP_])
        ips = sb("ips", [C])
        vT = sb("vT", [2, NP_])
        khT = sb("khT", [NP_])
        vBD0 = sb("vBD0", [2, 4, 2, DH + 1])
        kBD0 = sb("kBD0", [2, H, NP_])
        negM = sb("negM", [NT, H])
        negB = sb("negB", [3, NT * H], BF16)
        negR = sb("negR", [NT * H])
        negP = sb("negP", [NT, 3, H])
        negMT = sb("negMT", [N], BF16)
        E0 = sb("E0", [H * NP_], BF16)
        rec = sb("rec", [2, NT * H])
        att = sb("att", [2, NT, C])
        attT = sb("attT", [2, N])
        z = sb("z", [NT, C])
        zT = sb("zT", [N])
        gl = sb("gl", [NT, C])
        t0 = sb("t0", [2, NT, C])
        tlT = sb("tlT", [N])
        q1P = sb("q1P", [2, N])
        qB = sb("qB", [2, N])
        kE = sb("kE", [2, N])
        vA = sb("vA", [NT, H, DH + 1])
        cent = sb("cent", [2, SEG])
        centBD = sb("centBD", [H, SEG])
        kBD1 = sb("kBD1", [H, N])
        rts = sb("rts", [NT * H, SEG + 4])
        rtm = sb("rtm", [NT * H, SEG + 4])
        r8 = sb("r8", [NT * H, 8])
        segmax = sb("segmax", [NT * H, SEG])
        pen = sb("pen", [NT * H, SEG])
        sel = sb("sel", [NT * H, SEG])
        selM = sb("selM", [NT * H])
        bias = sb("bias", [NT * H, 2, SEG])
        PT1 = sb("PT1", [H, 2, N])
        PT0 = sb("PT0", [4, N])
        t1 = sb("t1", [2, NT, C])
        fT = sb("fT", [2, N])
        onehot = sb("onehot", [HI * NCH * N], F16)
        OH = onehot[:, :].rearrange("p (n q v g) -> p n q v g", n=NCH * NT, q=4, v=HI)
        early = onehot[:, :].bitcast(F32)
        Q = NT * H * QD

        S, Sx = (early[:, i * 2 * Q:(i + 1) * 2 * Q].rearrange("p (t g e) -> p t g e", t=NT, g=2 * H)
                 for i in range(2))
        queries = sb("queries", [NT, H * QD])
        sq = qn = queries
        sqT = queries[:, :, :].rearrange("p t (c n) -> p t c n", c=4)
        qsT = sb("qsT", [NT, 4, P])
        ssq = sb("ssq", [NT, 2, H])
        qrstd = sb("qrstd", [NT, H])
        nrm = sb("nrm", [NT * 2 * H])
        inv = sb("inv", [NT * 2 * H])
        vraw = sb("vraw", [NT * H, 2, TOP])
        v16 = sb("v16", [NT * H, 2, TOP])
        i16 = sb("i16", [NT * H, 2, TOP], U16)
        act = sb("act", [NT, 32, 4, LO])
        if_ = sb("if", [NT * H, 2, TOP])
        ab = sb("ab", [NT * H, 2, TOP])
        dv = ab
        cands = sb("cands", [2 * NT * H * CELLS])
        cand, candx = (cands[:, i * NT * H * CELLS:(i + 1) * NT * H * CELLS].rearrange(
            "p (g c) -> p g c", g=NT * H) for i in range(2))
        candm = cand
        lom = cands[:, 0:LO * NCH * N // 2].bitcast(F16).rearrange("p (l n) -> p l n", l=LO)
        c8 = sb("c8", [NT * H, 2, 8])
        weights = sb("weights", [LO * NCH * N])
        we = weights[:, 0:2 * NT * H * CELLS].rearrange("p (a g c) -> p a g c", a=2, g=NT * H)
        R = weights[:, :].bitcast(F16).rearrange("p (s l n) -> p s l n", s=2, l=LO)
        masked = sb("masked", [2 * NT * H * CELLS])
        prod = masked[:, 0:NT * 32 * 4 * LO].rearrange("p (t g e) -> p t g e", t=NT, g=32)
        wem = masked[:, 0:2 * NT * H * CELLS].rearrange("p (a g c) -> p a g c", a=2, g=NT * H)
        zs = sb("zs", [3, NT * H])
        slots = sb("slots", [2, NT * H, SLOTS])
        wn = sb("wn", [NT * H, SLOTS])
        W2 = sb("W2", [2, NCH * N], F16)
        eT = sb("eT", [3, NCH * N], U16)
        YTs = W2[:, :, :].rearrange("p s n -> p (s n)")[:, 0:2 * N].bitcast(F32)
        outs = eT[:, 0, :].bitcast(F32).rearrange("p (t c) -> p t c", t=NT)
        kss = sb("kss", [3, 4])
        wmean = sb("wmean", [2, H])
        WqC = Bw("Wq")
        rpart = onehot[:, 0:NR].bitcast(BF16)
        ksq = early[:, 4 * NR:4 * NR + P]
        kn = early[:, 4 * NR + P:4 * NR + 2 * P]
        rows = early[:, 4 * NR + 2 * P:5 * NR + 2 * P]
        ws = early[:, 5 * NR + 2 * P:5 * NR + 2 * P + NS_]
        rows3 = sb("rows3", [NR], BF16)
        ones3 = sb("ones3", [P], BF16)
        ident16 = sb("ident16", [P], BF16)
        Epat16 = sb("Epat16", [N], BF16)

        def row3(n):
            at, k = offR[n]
            return rows3[0:3, at:at + k]

        psum = [ctx.enter_context(nc.psum_tensor(f"bank{k}", [P, 512], F32)) for k in range(8)]

        bank_full = [sem(f"bank_full{k}") for k in range(8)]
        bank_free = [sem(f"bank_free{k}") for k in range(8)]
        x_loaded = [sem(f"x_loaded{b}") for b in range(B)]
        wa_loaded = sem("wa_loaded")
        wb_loaded = sem("wb_loaded")
        bq_loaded = sem("bq_loaded")
        ws_loaded = sem("ws_loaded")
        rows_loaded = sem("rows_loaded")
        preset = sem("preset")
        taps_pool_ready = sem("taps_pool_ready")
        conv_ready = sem("conv_ready")
        osb_ready = sem("osb_ready")
        var_ready = [sem(f"var_ready{k}") for k in range(4)]
        rstd_ready = [sem(f"rstd_ready{k}") for k in range(4)]
        hat_ready = [sem(f"hat_ready{k}") for k in range(4)]
        xln_ready = sem("xln_ready")
        hatw_ready = sem("hatw_ready")
        kbd0_ready = sem("kbd0_ready")
        negm_ready = sem("negm_ready")
        t0_ready = sem("t0_ready")
        centbd_ready = sem("centbd_ready")
        kbd1_ready = sem("kbd1_ready")
        bias_ready = sem("bias_ready")
        kss_ready = sem("kss_ready")
        kinv_ready = sem("kinv_ready")
        kn_ready = sem("kn_ready")
        KB_ready = sem("KB_ready")
        WqC_ready = sem("WqC_ready")
        up_ready = sem("up_ready")
        sq_ready = sem("sq_ready")
        qvar_ready = sem("qvar_ready")
        qrstd_ready = sem("qrstd_ready")
        sqT_ready = sem("sqT_ready")
        inv_ready = sem("inv_ready")
        rows3_ready = sem("rows3_ready")
        v16_ready = sem("v16_ready")
        i16_ready = sem("i16_ready")
        dv_ready = sem("dv_ready")
        ab_ready = sem("ab_ready")
        if_ready = sem("if_ready")
        we_ready = sem("we_ready")
        wem_ready = sem("wem_ready")
        slots_ready = sem("slots_ready")
        eT_ready = sem("eT_ready")
        onehot_dve_ready = sem("onehot_dve_ready")
        onehot_pool_ready = sem("onehot_pool_ready")
        out_ready = sem("out_ready")
        out_stored = sem("out_stored")
        dve_chain = sem("dve_chain")
        act_chain = sem("act_chain")
        pool_chain = sem("pool_chain")

        def full(eng, job, b):
            k, n = jobs[job, b]
            eng.wait_ge(bank_full[k], n)
            return psum[k]

        def freed(ins, job, b):
            ins.then_inc(bank_free[jobs[job, b][0]], 1)

        def read_out(eng, job, b):
            k, n = jobs[job, b]
            eng.wait_ge(bank_free[k], n)

        def chained(eng, semaphore):
            count = [0]

            def link(ins):
                count[0] += 1
                ins.then_inc(semaphore, 1)
                eng.wait_ge(semaphore, count[0])
            return link

        def sampling_free(eng, b):
            if b >= 1:
                read_out(eng, "kh", b - 1)
                read_out(eng, "vh", b - 1)
            if b >= 2:
                read_out(eng, "O0", b - 2)

        def stored(eng, b, back):
            if b >= back:
                eng.wait_ge(out_stored, 16 * (b - back + 1))

        def conv_rows(eng, first, last):
            dw = A("dw").rearrange("p (a b) -> p a b", a=KS)
            tv = taps[:, :, :].rearrange("p (a b) (y x) -> p y x a b", a=KS, y=G8)
            for ky in range(first, last):
                for kx in range(0, KS, 2):
                    n = min(2, KS - kx)
                    q = qpad[:, ky:ky + 15:2, kx:kx + 16].rearrange("p y (x r) -> p y x r", r=2)[:, :, :, 0:n]
                    ins = eng.tensor_tensor(tv[:, :, :, ky, kx:kx + n], q,
                                            dw[:, ky, kx:kx + n].unsqueeze(1).unsqueeze(1).broadcast_to(
                                                [P, G8, G8, n]), ALU.mult)
            return ins

        def sampling_weights(eng, unit, link, b):
            n = slice(0, NP_)
            read_out(eng, "offs", b)
            link(unit.tensor_tensor(crd[n, 0, :], tanh_[n, :], A("refs")[n, :], ALU.add))
            link(unit.tensor_scalar(crd[n, 1, :], crd[n, 0, :], 1.0, 4.0, ALU.add, ALU.mult))
            link(unit.tensor_scalar(crd[n, 2, :], crd[n, 1, :], 1.0, 0.5 * (SIDE - 1), ALU.add, ALU.mult))
            link(unit.tensor_tensor(hatw[n, 0, :, :], A("iota")[n, :].unsqueeze(1).broadcast_to([NP_, 2, SIDE]),
                                 crd[n, 2, :].unsqueeze(2).broadcast_to([NP_, 2, SIDE]), ALU.subtract))
            link(unit.tensor_scalar(hatw[n, 1, :, :], hatw[n, 0, :, :], 0.0, None, ALU.max))
            link(unit.tensor_scalar(hatw[n, 2, :, :], hatw[n, 0, :, :], 0.0, None, ALU.min))
            link(unit.tensor_tensor(hatw[n, 1, :, :], hatw[n, 2, :, :], hatw[n, 1, :, :], ALU.subtract))
            link(unit.tensor_scalar(hatw[n, 2, :, :], hatw[n, 1, :, :], 1.0, 0.0, ALU.add, ALU.max))
            unit.tensor_tensor(Wp[n, :, :], hatw[n, 2, 1, :].unsqueeze(2).broadcast_to([NP_, SIDE, SIDE]),
                            hatw[n, 2, 0, :].unsqueeze(1).broadcast_to([NP_, SIDE, SIDE]),
                            ALU.mult).then_inc(hatw_ready, 1)

        def hi_view(e):
            return e[0:KC, 2, :].rearrange("p (n q g) -> p n q g", n=NCH * NT, q=4)

        block = ctx.enter_context(nc.Block())

        @block.sync
        def _(sp):
            sp.dma_start(x_sb[:, 0, :, :], x_in[0]).then_inc(x_loaded[0], 16)
            sp.dma_start(wa[:, :], wa_in).then_inc(wa_loaded, 16)
            sp.dma_start(bq_row[0:1, :], rows_in[0:1, 0:C]).then_inc(bq_loaded, 16)
            sp.dma_start(rows[0:3, :], rows_in).then_inc(rows_loaded, 16)
            for b in range(1, B):
                sp.dma_start(x_sb[:, b, :, :], x_in[b]).then_inc(x_loaded[b], 16)
            sp.dma_start(wb[:, :], wb_in).then_inc(wb_loaded, 16)
            sp.dma_start(ws, ws_in).then_inc(ws_loaded, 16)
            for b in range(B):
                sp.wait_ge(out_ready, b + 1)
                sp.dma_start(out[b], outs[:, :, :]).then_inc(out_stored, 16)
            sp.wait_ge(out_stored, 16 * B)

        @block.tensor
        def _(pe):
            def take(job, b):
                k, n = jobs[job, b]
                if n > 1:
                    pe.wait_ge(bank_free[k], n - 1)
                return psum[k]

            def done(ins, job, b):
                ins.then_inc(bank_full[jobs[job, b][0]], 1)

            def transposes(job, b, pairs):
                o = take(job, b)
                for at, src in pairs:
                    k, m = src.shape
                    last = nc.tensor.transpose(o[0:m, at:at + k], src, ident[0:k, 0:k])
                done(last, job, b)

            mm = nc.tensor.matmul

            def A1a(b):
                if b == 0:
                    pe.wait_ge(wa_loaded, 16)
                    pe.wait_ge(bq_loaded, 16)
                    pe.wait_ge(preset, 1)
                pe.wait_ge(xln_ready, b + 1)
                o = take("qimg", b)
                for s in range(NT):
                    c = slice(s * P, s * P + P)
                    mm(o[:, c], xln[:, s, :], A("wq"), start=True, stop=False)
                    last = mm(o[:, c], ones[0:1, :], bq_row[0:1, :], start=False, stop=True)
                done(last, "qimg", b)
                o = take("qT", b)
                last = mm(o[:, 0:N], A("wq"), xln[:, :, :], start=True, stop=True)
                done(last, "qT", b)

            def A1b(b):
                read_out(pe, "qT", b)
                o = take("qhT", b)
                done(mm(o[:, 0:N], A("mq"), qT[:, :], start=True, stop=True), "qhT", b)

            def A2d(b):
                pe.wait_ge(osb_ready, b + 1)
                o = take("offs", b)
                done(mm(o[0:NP_, 0:2], osb[:, :], A("pw"), start=True, stop=True), "offs", b)

            def A3a(b):
                pe.wait_ge(hatw_ready, b + 1)
                Wf = Wp[0:NP_, :, :].rearrange("p a b -> p (a b)")
                transposes("WT", b, [(s * NP_, Wf[:, s * P:s * P + P]) for s in range(NT)])

            def A3b(b):
                read_out(pe, "WT", b)
                o = take("interp", b)
                for s in range(NT):
                    last = mm(o[0:NP_, 0:C], WTs[:, s, :], x_sb[:, b, s, :], start=(s == 0), stop=(s == NT - 1))
                done(last, "interp", b)

            def A3c(b):
                read_out(pe, "interp", b)
                o = take("vT", b)
                wv2 = A("wv2").rearrange("p (u n) -> p u n", u=2)
                for u in range(2):
                    last = mm(o[:, 0:NP_], wv2[0:NP_, u, :], ips[0:NP_, u:C:2], start=(u == 0), stop=(u == 1))
                done(last, "vT", b)

            def A4(b):
                if b == 0:
                    pe.wait_ge(rows3_ready, 1)
                    pe.wait_ge(wb_loaded, 16)
                read_out(pe, "vT", b)
                o = take("kh", b)
                done(mm(o[:, 0:NP_], A("mk"), vT[:, 0, :], start=True, stop=True), "kh", b)
                o = take("vh", b)
                mm(o[:, 0:C], vT[:, :, :], A("mv"), start=True, stop=False)
                done(mm(o[:, 0:C], ones3[0:3, :], row3("mvb"), start=False, stop=True), "vh", b)

            def F5a(b):
                read_out(pe, "qhT", b)
                pe.wait_ge(kbd0_ready, b + 1)
                for t in range(NT):
                    o = take(f"S0_{t}", b)
                    done(mm(o[:, :], qhT[:, b % 2, t * P:t * P + P], kBD0[:, b % 2, :, :], start=True, stop=True),
                         f"S0_{t}", b)

            def F5b(b):
                pe.wait_ge(negm_ready, b + 1)
                transposes("mT", b, [(t * P, negP[:, t, :, :].rearrange("p a h -> p (a h)")) for t in range(NT)])

            def F5c(b):
                read_out(pe, "mT", b)
                for j in range(2):
                    o = take(f"P0_{j}", b)
                    for i in range(2):
                        hp = 2 * j + i
                        mm(o[:, i * N:i * N + N], kBD0[:, b % 2, 2 * hp:2 * hp + 2, :], qhT[:, b % 2, :],
                           start=True, stop=False)
                        last = mm(o[:, i * N:i * N + N], E0[0:3 * H, hp * P:hp * P + P], negMT[0:3 * H, :],
                                  start=False, stop=True)
                    done(last, f"P0_{j}", b)

            def F6a(b):
                read_out(pe, "P0_0", b)
                read_out(pe, "P0_1", b)
                read_out(pe, "vh", b)
                o = take("O0", b)
                for t in range(NT):
                    for hp in range(4):
                        at = (t * H + 2 * hp) * (DH + 1)
                        last = mm(o[:, at:at + 2 * (DH + 1)], PT0[:, hp, t * P:t * P + P], vBD0[:, b % 2, hp, :, :],
                                  start=True, stop=True)
                done(last, "O0", b)

            def F6b(b):
                read_out(pe, "O0", b)
                transposes("aT", b, [(t * P, att[:, 0, t, :]) for t in range(NT)])

            def F6c(b):
                read_out(pe, "aT", b)
                o = take("msa", b)
                for t in range(NT):
                    c = slice(t * P, t * P + P)
                    mm(o[:, c], attT[:, 0, c], A("mo"), start=True, stop=False)
                    last = mm(o[:, c], ones3[0:3, :], row3("mob"), start=False, stop=True)
                done(last, "msa", b)

            def F7a(b):
                pe.wait_ge(hat_ready[1], b + 1)
                transposes("zT", b, [(t * P, hat[:, 1, t, :]) for t in range(NT)])

            def F7b(b):
                read_out(pe, "zT", b)
                o = take("mlp", b)
                for t in range(NT):
                    c = slice(t * P, t * P + P)
                    mm(o[:, c], zT[:, c], A("mlp"), start=True, stop=False)
                    last = mm(o[:, c], ones3[0:3, :], row3("mlpb"), start=False, stop=True)
                done(last, "mlp", b)

            def F8a(b):
                pe.wait_ge(hat_ready[2], b + 1)
                transposes("tT", b, [(t * P, hat[:, 2, t, :]) for t in range(NT)])

            def F8b(b):
                if b == 0:
                    pe.wait_ge(up_ready, 1)
                read_out(pe, "tT", b)
                wqk = Bw("wqk").rearrange("p (i j m) -> p i j m", i=2, j=2)
                for i, job in ((1, "k1"), (0, "q1")):
                    o = take(job, b)
                    for j in range(2):
                        c = slice(j * N, j * N + N)
                        last = mm(o[:, c], wqk[:, i, j, :], tlT[:, :], start=True, stop=(i == 0))
                        if i == 1:
                            last = mm(o[:, c], ident16[:, :], Epat16[:, :], start=False, stop=True)
                    done(last, job, b)

            def F8c(b):
                o = take("v1", b)
                for t in range(NT):
                    c = slice(t * P, t * P + P)
                    last = mm(o[:, c], tlT[:, c], Bw("wv1"), start=True, stop=True)
                done(last, "v1", b)

            def F9a(b):
                read_out(pe, "q1", b)
                pe.wait_ge(centbd_ready, b + 1)
                o = take("route", b)
                for t in range(NT):
                    for j in range(2):
                        last = mm(o[:, t * P + j * 64:t * P + j * 64 + 64], q1P[:, j, t * P:t * P + P],
                                  centBD[:, 4 * j:4 * j + 4, :], start=True, stop=True)
                done(last, "route", b)

            def segment_scores(b, t):
                for i in range(4):
                    job = f"S1_{t}{i}"
                    o = take(job, b)
                    done(mm(o[:, :], q1P[:, i // 2, t * P:t * P + P], kBD1[:, 2 * i:2 * i + 2, :],
                            start=True, stop=True), job, b)

            def F9b(b):
                pe.wait_ge(kbd1_ready, b + 1)
                segment_scores(b, 0)

            def F9c(b):
                segment_scores(b, 1)

            def F9d(b):
                pe.wait_ge(bias_ready, b + 1)
                bv = bias[:, :, :, :].rearrange("p (t j h) a s -> p t j (h a s)", t=NT, j=2)
                transposes("bT", b, [(j * N + t * P, bv[:, t, j, :]) for j in range(2) for t in range(NT)])

            def F10a(b):
                read_out(pe, "bT", b)
                weights_of(b, range(0, H // 2))

            def F10b(b):
                weights_of(b, range(H // 2, H))

            def weights_of(b, heads):
                for h in heads:
                    job = f"P1_{h}"
                    o = take(job, b)
                    for kc in range(NT):
                        last = mm(o[:, kc * N:kc * N + N], kBD1[:, h, kc * P:kc * P + P], qB[:, h // 4, :],
                                  start=True, stop=True)
                    done(last, job, b)

            def F11a(b):
                read_out(pe, "v1", b)
                o = take("O1", b)
                for h in range(H):
                    read_out(pe, f"P1_{h}", b)
                    for t in range(NT):
                        at = (t * H + h) * (DH + 1)
                        for kc in range(NT):
                            last = mm(o[:, at:at + DH + 1], PT1[:, h, kc, t * P:t * P + P], vA[:, kc, h, :],
                                      start=(kc == 0), stop=(kc == NT - 1))
                done(last, "O1", b)

            def F11b(b):
                read_out(pe, "O1", b)
                transposes("a1T", b, [(t * P, att[:, 1, t, :]) for t in range(NT)])

            def F11c(b):
                read_out(pe, "a1T", b)
                o = take("proj", b)
                for t in range(NT):
                    c = slice(t * P, t * P + P)
                    mm(o[:, c], attT[:, 1, c], Bw("wproj"), start=True, stop=False)
                    last = mm(o[:, c], ones3[0:3, :], row3("bproj"), start=False, stop=True)
                done(last, "proj", b)

            def F12(b):
                pe.wait_ge(hat_ready[3], b + 1)
                transposes("fT", b, [(t * P, hat[:, 3, t, :]) for t in range(NT)])

            def NS(b):
                pe.wait_ge(kn_ready, 1)
                transposes("keys", b, [(0, kn[0:NK, :])])

            def query(b, t):
                o = take(f"Q{t}", b)
                mm(o[:, :], fT[:, b % 2, t * P:t * P + P], WqC[:, :], start=True, stop=False)
                done(mm(o[:, :], ones3[0:3, :], row3("fbq"), start=False, stop=True), f"Q{t}", b)

            def N0a(b):
                if b == 0:
                    pe.wait_ge(WqC_ready, 1)
                    pe.wait_ge(rows3_ready, 2)
                read_out(pe, "fT", b)
                query(b, 0)

            def N0h(b):
                query(b, 1)

            def query_transposes(b, t):
                read_out(pe, f"Q{t}", b)
                transposes(f"qsT{t}", b, [(c * P, qn[:, t, c * P:c * P + P]) for c in range(4)])

            def key_scores(b, t):
                read_out(pe, f"qsT{t}", b)
                for j in range(2):
                    o = take(f"S2_{t}{j}", b)
                    for i in range(2):
                        last = mm(o[:, i * 256:i * 256 + 256], qsT[:, t, 2 * j + i, :], KB[:, :],
                                  start=True, stop=True)
                    done(last, f"S2_{t}{j}", b)

            def N0b(b):
                query_transposes(b, 0)

            def N0c(b):
                if b == 0:
                    pe.wait_ge(KB_ready, 1)
                key_scores(b, 0)

            def N0d(b):
                query_transposes(b, 1)

            def N0e(b):
                key_scores(b, 1)

            def norms(b, t):
                pe.wait_ge(sqT_ready, NT * b + t + 1)
                o = take(f"norm{t}", b)
                for c in range(4):
                    last = mm(o[:, 4 * c:4 * c + 4], sqT[:, t, c, :], Bw("hm32"), start=True, stop=True)
                done(last, f"norm{t}", b)

            def N0f(b):
                norms(b, 0)

            def N0g(b):
                norms(b, 1)

            def N3a(b):
                pe.wait_ge(slots_ready, NT * (b + 1))
                for job, src in (("wT", wn[:, :, :]), ("eT", slots[:, 1, :, :])):
                    transposes(job, b, [((c * NT + t) * P,
                                         src[:, t * H + c * HC:t * H + (c + 1) * HC, :].rearrange("p h s -> p (h s)"))
                                        for c in range(NCH) for t in range(NT)])

            def N4(b):
                p = b % 2
                down = Bw("down").rearrange("p (l m) -> p l m", l=LO)
                fq = fT[:, p, :].rearrange("p (t q g) -> p q t g", t=NT, q=4)
                o = take("I", b)
                for q in range(4):
                    for lo in range(LO):
                        last = mm(o[HI * q:HI * q + HI, lo * 64:lo * 64 + 64], down[:, lo, :], fq[:, q],
                                  start=True, stop=True)
                done(last, "I", b)

            def N5a(b):
                pe.wait_ge(onehot_dve_ready, b + 1)
                pe.wait_ge(onehot_pool_ready, b + 1)
                scatter(b, 0)

            def N5b(b):
                scatter(b, 1)

            def scatter(b, t):
                OHv = OH[0:KC, :, :, :, :].rearrange("p n q v g -> p n g (q v)")
                Rv = R[0:KC, :, :, :].rearrange("p s l (c t q g) -> p c t g s q l", c=NCH, t=NT, g=32)
                o = take(f"G{t}", b)
                for g in range(32):
                    for c in range(NCH):
                        for s in range(2):
                            last = mm(o[:, g * 16:g * 16 + 16], OHv[:, c * NT + t, g], Rv[:, c, t, g, s],
                                      start=(c == 0 and s == 0), stop=(c == NCH - 1 and s == 1))
                done(last, f"G{t}", b)

            def N6a(b):
                if b == 0:
                    pe.wait_ge(up_ready, 1)
                for t in range(NT):
                    read_out(pe, f"G{t}", b)
                o = take("Y", b)
                pv = prod[:, :, :, :].rearrange("p t g (q l) -> p l t q g", q=4)
                for lo in range(LO):
                    last = mm(o[:, 0:N], up[:, lo, :], pv[:, lo], start=(lo == 0), stop=(lo == LO - 1))
                done(last, "Y", b)

            def N6b(b):
                read_out(pe, "Y", b)
                transposes("YT", b, [(t * P, YTs[:, t * P:t * P + P]) for t in range(NT)])

            do = {"A1a": A1a, "A1b": A1b, "A2d": A2d, "A3a": A3a, "A3b": A3b, "A3c": A3c, "A4": A4, "F5a": F5a,
                  "F5b": F5b, "F5c": F5c, "F6a": F6a, "F6b": F6b, "F6c": F6c, "F7a": F7a, "F7b": F7b, "F8a":
                  F8a, "F8b": F8b, "F8c": F8c, "F9a": F9a, "F9b": F9b, "F9c": F9c, "F9d": F9d, "F10a": F10a,
                  "F10b": F10b, "F11a": F11a, "F11b": F11b, "F11c": F11c, "F12": F12, "NS": NS, "N0a": N0a,
                  "N0h": N0h, "N0b": N0b, "N0c": N0c, "N0d": N0d, "N0e": N0e, "N0f": N0f, "N0g": N0g, "N3a":
                  N3a, "N4": N4, "N5a": N5a, "N5b": N5b, "N6a": N6a, "N6b": N6b}
            for s, b in schedule("tensor"):
                if s in do:
                    do[s](b)

        @block.scalar
        def _(ac):
            fn = nc.scalar.activation
            link = chained(ac, act_chain)

            def normalized(k, src, b):
                ac.wait_ge(rstd_ready[k], b + 1)
                for t in range(NT):
                    last = fn(hat[:, k, t, :], src[:, t, :], ACT.Identity, scale=rstd[:, k, t:t + 1],
                              bias=shift[:, k, t:t + 1])
                last.then_inc(hat_ready[k], 1)

            def A0b(b):
                sampling_free(ac, b)
                normalized(0, x_sb[:, b, :, :], b)

            def A1a(b):
                sampling_free(ac, b)
                if b == 0:
                    ac.wait_ge(wa_loaded, 16)
                    ac.wait_ge(preset, 1)
                    fn(E0[0:3 * H, :], A("E0")[0:3 * H, :], ACT.Copy)
                o = full(ac, "qimg", b)
                inner = qpad[:, 3:3 + SIDE, 3:3 + SIDE]
                freed(fn(inner, o[:, 0:N].rearrange("p (a b) -> p a b", b=SIDE), ACT.Identity), "qimg", b)
                o = full(ac, "qT", b)
                freed(fn(qT[:, :].rearrange("p (c s) -> p s c", s=2),
                         o[:, 0:N].rearrange("p (s c) -> p s c", s=2), ACT.Identity, bias=vec("bq")), "qT", b)

            def A1b(b):
                o = full(ac, "qhT", b)
                freed(fn(qhT[:, b % 2, :], o[:, 0:N], ACT.Identity, bias=vec("mqb")), "qhT", b)

            def A2c(b):
                ac.wait_ge(conv_ready, b + 1)
                fn(osb[:, :], conv[:, :], ACT.Gelu, bias=vec("dwb")).then_inc(osb_ready, 1)

            def A2d(b):
                o = full(ac, "offs", b)
                freed(fn(tanh_[0:NP_, :], o[0:NP_, 0:2], ACT.Tanh), "offs", b)

            def A3a(b):
                o = full(ac, "WT", b)
                freed(fn(WTs[:, :, :], o[:, 0:NT * NP_].rearrange("p (s n) -> p s n", s=NT), ACT.Identity), "WT", b)

            def A3b(b):
                o = full(ac, "interp", b)
                freed(fn(ips[0:NP_, :], o[0:NP_, 0:C], ACT.Identity), "interp", b)

            def A3c(b):
                o = full(ac, "vT", b)
                freed(fn(vT[:, :, :], o[:, 0:NP_].unsqueeze(1).broadcast_to([P, 2, NP_]), ACT.Identity,
                         bias=vec("bv")), "vT", b)

            def A4(b):
                o = full(ac, "kh", b)
                freed(fn(khT[:, :], o[:, 0:NP_], ACT.Identity, bias=vec("mkb")), "kh", b)
                o = full(ac, "vh", b)
                for r in range(2):
                    q = slice(NP_ * r, NP_ * r + NP_)
                    last = fn(vBD0[q, b % 2, :, r, 0:DH],
                              o[q, 0:C].rearrange("p (a r d) -> p a r d", a=4, r=2)[:, :, r, :], ACT.Identity)
                freed(last, "vh", b)

            def F5b(b):
                o = full(ac, "mT", b)
                freed(fn(negMT[0:3 * H, :], o[0:3 * H, 0:N], ACT.Copy), "mT", b)

            def F5c(b):
                for j in range(2):
                    o = full(ac, f"P0_{j}", b)
                    freed(fn(PT0[:, 2 * j:2 * j + 2, :], o[:, :].rearrange("p (i n) -> p i n", i=2), ACT.Exp),
                          f"P0_{j}", b)

            def F6b(b):
                o = full(ac, "aT", b)
                freed(fn(attT[:, 0, :], o[:, 0:N], ACT.Identity), "aT", b)

            def F7a(b):
                normalized(1, z[:, :, :], b)
                o = full(ac, "zT", b)
                freed(fn(zT[:, :], o[:, 0:N], ACT.Identity, bias=vec("lnb"), scale=vec("lng")), "zT", b)

            def F7b(b):
                o = full(ac, "mlp", b)
                freed(fn(gl[:, :, :], o[:, 0:N].rearrange("p (t c) -> p t c", t=NT), ACT.Gelu), "mlp", b)

            def F8a(b):
                normalized(2, t0[:, b % 2, :, :], b)
                if b >= 1:
                    full(ac, "v1", b - 1)
                o = full(ac, "tT", b)
                freed(fn(tlT[:, :], o[:, 0:N], ACT.Identity), "tT", b)

            def F8b(b):
                if b >= 1:
                    ac.wait_ge(kbd1_ready, b)
                    ac.wait_ge(centbd_ready, b)
                    read_out(ac, "bT", b - 1)
                o = full(ac, "k1", b)
                freed(fn(kE[:, :, :], o[:, :].rearrange("p (j n) -> p j n", j=2), ACT.Identity), "k1", b)
                o = full(ac, "q1", b)
                freed(fn(q1P[:, :, :], o[:, :].rearrange("p (j n) -> p j n", j=2), ACT.Identity), "q1", b)

            def F8c(b):
                if b >= 1:
                    full(ac, "O1", b - 1)
                o = full(ac, "v1", b)
                freed(fn(vA[:, :, :, 0:DH], o[:, 0:N].rearrange("p (t h d) -> p t h d", t=NT, h=H), ACT.Identity),
                      "v1", b)

            def F9a(b):
                o = full(ac, "route", b)
                freed(fn(rts[:, :, 0:SEG], o[:, 0:N].rearrange("p (g s) -> p g s", s=SEG), ACT.Identity),
                      "route", b)

            def F10a(b):
                weights_of(b, range(0, H // 2))

            def F10b(b):
                weights_of(b, range(H // 2, H))

            def weights_of(b, heads):
                for h in heads:
                    o = full(ac, f"P1_{h}", b)
                    freed(fn(PT1[:, h, :, :], o[:, :].rearrange("p (k n) -> p k n", k=NT), ACT.Exp,
                             scale=DH ** -0.5), f"P1_{h}", b)

            def F11b(b):
                o = full(ac, "a1T", b)
                freed(fn(attT[:, 1, :], o[:, 0:N], ACT.Identity), "a1T", b)

            def F12(b):
                normalized(3, t1[:, b % 2, :, :], b)
                stored(ac, b, 2)
                o = full(ac, "fT", b)
                freed(fn(fT[:, b % 2, :], o[:, 0:N], ACT.Identity), "fT", b)

            def squares(b, t):
                if b >= 1:
                    full(ac, f"norm{t}", b - 1)
                o = full(ac, f"Q{t}", b)
                fn(sq[:, t, :], o[:, :], ACT.Square).then_inc(sq_ready, 1)

            def N0a(b):
                squares(b, 0)

            def N0h(b):
                squares(b, 1)

            def gain_and_bias(b, t):
                o = full(ac, f"qsT{t}", b)
                freed(fn(qsT[:, t, :, :], o[:, :].rearrange("p (c n) -> p c n", c=4), ACT.Identity,
                         scale=Bw("fln")[:, 0:1], bias=Bw("fln")[:, 1:2]), f"qsT{t}", b)
                read_out(ac, f"qsT{t}", b)
                fn(sqT[:, t, :, :], qsT[:, t, :, :], ACT.Square).then_inc(sqT_ready, 1)

            def key_scores(b, t):
                if b >= 1:
                    full(ac, "G1", b - 1)
                for j in range(2):
                    o = full(ac, f"S2_{t}{j}", b)
                    freed(fn(S[:, t, 8 * j:8 * j + 8, :], o[:, :].rearrange("p (l e) -> p l e", e=NK),
                             ACT.Identity), f"S2_{t}{j}", b)

            def N0b(b):
                gain_and_bias(b, 0)

            def N0c(b):
                key_scores(b, 0)

            def N0d(b):
                gain_and_bias(b, 1)

            def N0e(b):
                key_scores(b, 1)

            def experts_and_exponentials(b, t):
                h = slice(t * H, t * H + H)
                ac.wait_ge(i16_ready, NT * b + t + 1)
                fn(if_[:, h, :, :], i16[:, h, :, :], ACT.Copy).then_inc(if_ready, 1)
                ac.wait_ge(dv_ready, NT * b + t + 1)
                fn(ab[:, h, :, :], dv[:, h, :, :], ACT.Exp).then_inc(ab_ready, 1)

            def N2p(b):
                if b >= 1:
                    read_out(ac, "G1", b - 1)
                experts_and_exponentials(b, 0)

            def N2q(b):
                experts_and_exponentials(b, 1)

            def N3a(b):
                if b >= 1:
                    ac.wait_ge(onehot_dve_ready, b)
                    ac.wait_ge(onehot_pool_ready, b)
                    full(ac, "YT", b - 1)
                    stored(ac, b, 1)
                o = full(ac, "wT", b)
                link(fn(W2[0:KC, 0, :], o[0:KC, :], ACT.Copy))
                o = full(ac, "eT", b)
                freed(fn(eT[0:KC, 0, :], o[0:KC, :], ACT.Copy), "eT", b)

            def N4(b):
                if b >= 1:
                    read_out(ac, "G1", b - 1)
                o = full(ac, "I", b)
                for q in range(4):
                    r = slice(HI * q, HI * q + HI)
                    last = fn(act[r, :, :, q, :].rearrange("p t g l -> p (t g) l"),
                              o[r, 0:4 * 64].rearrange("p (l n) -> p n l", l=LO), ACT.Gelu)
                freed(last, "I", b)

            def N6a(b):
                o = full(ac, "Y", b)
                freed(fn(YTs[:, :], o[:, 0:N], ACT.Identity), "Y", b)

            do = {"A0b": A0b, "A1a": A1a, "A1b": A1b, "A2c": A2c, "A2d": A2d, "A3a": A3a, "A3b": A3b, "A3c":
                  A3c, "A4": A4, "F5b": F5b, "F5c": F5c, "F6b": F6b, "F7a": F7a, "F7b": F7b, "F8a": F8a, "F8b":
                  F8b, "F8c": F8c, "F9a": F9a, "F10a": F10a, "F10b": F10b, "F11b": F11b, "F12": F12, "N0a": N0a,
                  "N0h": N0h, "N0b": N0b, "N0c": N0c, "N0d": N0d, "N0e": N0e, "N2p": N2p, "N2q": N2q, "N3a":
                  N3a, "N4": N4, "N6a": N6a}
            for s, b in schedule("scalar"):
                if s in do:
                    do[s](b)

        @block.vector
        def _(dve):
            v = nc.vector
            link = chained(dve, dve_chain)

            def statistics(k, src):
                for t in range(NT):
                    last = v.bn_stats(stats[:, k, t, :], src[:, t, :])
                link(last)
                for t in range(NT):
                    last = v.bn_aggr(mv[:, k, t, :], stats[:, k, t, :])
                link(last)
                v.tensor_scalar(negmean[:, k, :], mv[:, k, :, 0], -1.0, None, ALU.mult)
                v.tensor_scalar(veps[:, k, :], mv[:, k, :, 1], LN_EPS, None, ALU.add).then_inc(var_ready[k], 1)

            def A0a(b):
                sampling_free(dve, b)
                dve.wait_ge(x_loaded[b], 16)
                statistics(0, x_sb[:, b, :, :])

            def A2c(b):
                if b == 0:
                    dve.wait_ge(wa_loaded, 16)
                    read_out(dve, "qimg", b)
                    link(conv_rows(v, 0, CONV_DVE))
                dve.wait_ge(taps_pool_ready, b + 1)
                n = KS * KS if b == 0 else FOLDED
                v.tensor_reduce(conv[:, :], taps[:, 0:n, :].rearrange("p k n -> p n k"), X,
                                ALU.add).then_inc(conv_ready, 1)

            def A3a(b):
                if b == 0:
                    sampling_weights(dve, v, link, b)

            def F5a(b):
                for t in range(NT):
                    o = full(dve, f"S0_{t}", b)
                    freed(v.tensor_reduce(negM[:, t, :], o[:, :].rearrange("p (h k) -> p h k", h=H), X, ALU.max,
                                          negate=True), f"S0_{t}", b)
                for t in range(NT):
                    read_out(dve, f"S0_{t}", b)
                nm = negM[:, :, :].rearrange("p t h -> p (t h)")
                link(v.tensor_copy(negB[:, 0, :], nm))
                link(v.tensor_tensor(negR[:, :], nm, negB[:, 0, :], ALU.subtract))
                link(v.tensor_copy(negB[:, 1, :], negR[:, :]))
                link(v.tensor_tensor(negB[:, 2, :], negR[:, :], negB[:, 1, :], ALU.subtract))
                v.tensor_copy(negP[:, :, :, :].rearrange("p t a h -> p a t h"),
                              negB[:, :, :].rearrange("p a (t h) -> p a t h", t=NT)).then_inc(negm_ready, 1)

            def normalize(job, k, b):
                o = full(dve, job, b)
                ov = o[:, 0:NT * H * (DH + 1)].rearrange("p (g d) -> p g d", d=DH + 1)
                link(v.reciprocal(rec[:, k, :], ov[:, :, DH]))
                freed(v.tensor_tensor(att[:, k, :, :].rearrange("p t (h d) -> p (t h) d", d=DH), ov[:, :, 0:DH],
                                      rec[:, k, :].unsqueeze(2).broadcast_to([P, NT * H, DH]), ALU.mult), job, b)

            def F6a(b):
                normalize("O0", 0, b)

            def F6c(b):
                o = full(dve, "msa", b)
                freed(v.tensor_tensor(z[:, :, :], o[:, 0:N].rearrange("p (t c) -> p t c", t=NT),
                                      x_sb[:, b, :, :], ALU.add), "msa", b)
                read_out(dve, "msa", b)
                statistics(1, z[:, :, :])

            def F7b(b):
                read_out(dve, "mlp", b)
                v.tensor_tensor(t0[:, b % 2, :, :], gl[:, :, :], z[:, :, :], ALU.add).then_inc(t0_ready, 1)
                dve.wait_ge(t0_ready, b + 1)
                statistics(2, t0[:, b % 2, :, :])

            def F8b(b):
                read_out(dve, "k1", b)
                link(v.tensor_reduce(cent[:, :, :], kE[:, :, :].rearrange("p j (s n) -> p j s n", n=SEG), X, ALU.add))
                v.tensor_tensor(centBD[:, :, :].rearrange("p (j h) s -> p j h s", j=2),
                                cent[:, :, :].unsqueeze(2).broadcast_to([P, 2, 4, SEG]),
                                Bw("hm32").unsqueeze(1).unsqueeze(3).broadcast_to([P, 2, 4, SEG]),
                                ALU.mult).then_inc(centbd_ready, 1)

            def F9a(b):
                read_out(dve, "route", b)
                for g in range(NT * H):
                    last = v.max(r8[:, g, :], rts[:, g, :])
                link(last)
                for g in range(NT * H):
                    last = v.match_replace(rtm[:, g, :], r8[:, g, :], rts[:, g, :], MARK)
                link(last)
                link(v.tensor_scalar(pen[:, :, :], rtm[:, :, 0:SEG], 0.5 * MARK, HIDE, ALU.is_gt, ALU.mult))

            def segment_maxima(b, t):
                for i in range(4):
                    job = f"S1_{t}{i}"
                    o = full(dve, job, b)
                    freed(v.tensor_reduce(segmax[:, t * H + 2 * i:t * H + 2 * i + 2, :],
                                          o[:, :].rearrange("p (g n) -> p g n", n=SEG), X, ALU.max), job, b)

            def F9b(b):
                segment_maxima(b, 0)

            def F9c(b):
                segment_maxima(b, 1)
                for i in range(4):
                    read_out(dve, f"S1_1{i}", b)
                link(v.tensor_tensor(sel[:, :, :], segmax[:, :, :], pen[:, :, :], ALU.add))
                link(v.tensor_reduce(selM[:, :], sel[:, :, :], X, ALU.max))
                v.tensor_tensor(bias[:, :, 1, :], pen[:, :, :],
                                selM[:, :].unsqueeze(2).broadcast_to([P, NT * H, SEG]),
                                ALU.subtract).then_inc(bias_ready, 1)

            def F9d(b):
                o = full(dve, "bT", b)
                freed(v.tensor_tensor(qB[:, :, :], o[:, :].rearrange("p (j n) -> p j n", j=2), q1P[:, :, :], ALU.add),
                      "bT", b)

            def F11a(b):
                normalize("O1", 1, b)

            def F11c(b):
                p = b % 2
                stored(dve, b, 2)
                o = full(dve, "proj", b)
                freed(v.tensor_tensor(t1[:, p, :, :], o[:, 0:N].rearrange("p (t c) -> p t c", t=NT),
                                      t0[:, p, :, :], ALU.add), "proj", b)
                read_out(dve, "proj", b)
                statistics(3, t1[:, p, :, :])

            def split_rows(first, last):
                r, c = slice(0, 3), slice(first, last)
                for i in range(2):
                    link(v.tensor_copy(rpart[r, c], rows[r, c]))
                    link(v.scalar_tensor_tensor(rows[r, c], rpart[r, c], A("less")[r, i:i + 1], rows[r, c],
                                                ALU.mult, ALU.add))
                v.tensor_copy(rows3[r, c], rows[r, c]).then_inc(rows3_ready, 1)

            def setup_rows(b):
                dve.wait_ge(rows_loaded, 16)
                dve.wait_ge(wa_loaded, 16)
                split_rows(offR["mvb"][0], offR["fbq"][0])

            def NS(b):
                k = slice(0, NK)
                dve.wait_ge(wb_loaded, 16)
                dve.wait_ge(ws_loaded, 16)
                keys = Sw("keys")
                link(v.tensor_tensor(ksq[k, :], keys[k, :], keys[k, :], ALU.mult))
                link(v.tensor_reduce(kss[k, 0, :], ksq[k, :].rearrange("p (a d) -> p a d", a=4), X, ALU.add))
                v.tensor_scalar(kss[k, 1, :], kss[k, 0, :], 1e-24, None, ALU.max).then_inc(kss_ready, 1)
                dve.wait_ge(kinv_ready, 1)
                v.tensor_tensor(kn[k, :].rearrange("p (a d) -> p a d", a=4),
                                keys[k, :].rearrange("p (a d) -> p a d", a=4),
                                kss[k, 2, :].unsqueeze(2).broadcast_to([NK, 4, 32]), ALU.mult).then_inc(kn_ready, 1)
                for i, (src, n) in enumerate(((Bw("Wq"), P), (rows[0:3, offR["fbq"][0]:NR], 3))):
                    sv = src.rearrange("p (h q) -> p h q", h=H)
                    link(v.tensor_reduce(wmean[0:n, i, :], sv, X, ALU.add))
                    last = v.scalar_tensor_tensor(sv, wmean[0:n, i, :].unsqueeze(2).broadcast_to([n, H, QD]),
                                                  -1.0 / QD, sv, ALU.mult, ALU.add)
                    if i == 0:
                        last.then_inc(WqC_ready, 1)
                    else:
                        link(last)
                split_rows(offR["fbq"][0], NR)
                link(v.memset(KB[:, :], 0.0))
                o = full(dve, "keys", b)
                for i in range(4):
                    q = slice(32 * i, 32 * i + 32)
                    last = v.tensor_copy(KB[q, NK * i:NK * i + NK], o[q, 0:NK])
                freed(last, "keys", b)
                read_out(dve, "keys", b)
                v.engine_nop().then_inc(KB_ready, 1)

            def variances(b, t):
                dve.wait_ge(sq_ready, NT * b + t + 1)
                link(v.tensor_reduce(ssq[:, t, 0, :], sq[:, t, :].rearrange("p (h q) -> p h q", h=H), X, ALU.add))
                v.tensor_scalar(ssq[:, t, 1, :], ssq[:, t, 0, :], 1.0 / QD, LN_EPS, ALU.mult,
                                ALU.add).then_inc(qvar_ready, 1)

            def normalized_queries(b, t):
                dve.wait_ge(qrstd_ready, NT * b + t + 1)
                o = full(dve, f"Q{t}", b)
                freed(v.tensor_tensor(qn[:, t, :].rearrange("p (h q) -> p h q", h=H),
                                      o[:, :].rearrange("p (h q) -> p h q", h=H),
                                      qrstd[:, t, :].unsqueeze(2).broadcast_to([P, H, QD]), ALU.mult),
                      f"Q{t}", b)

            def N0a(b):
                variances(b, 0)

            def N0h(b):
                variances(b, 1)

            def N0b(b):
                normalized_queries(b, 0)

            def N0d(b):
                normalized_queries(b, 1)

            def top_keys(b, i):
                t, half = i // 2, i % 2
                lists = slice(8 * half, 8 * half + 8)
                vt = vraw[:, t * H:t * H + H, :, :].rearrange("p h a k -> p (h a) k")[:, lists, :]
                it = i16[:, t * H:t * H + H, :, :].rearrange("p h a k -> p (h a) k")[:, lists, :]
                sv, sx = S[:, t, lists, :], Sx[:, t, lists, :]
                read_out(dve, f"S2_{t}{half}", b)
                for g in range(8):
                    last = v.max(vt[:, g, 0:8], sv[:, g, :])
                link(last)
                for g in range(8):
                    last = v.match_replace(sx[:, g, :], vt[:, g, 0:8], sv[:, g, :], MARK)
                link(last)
                for g in range(8):
                    last = v.max(vt[:, g, 8:16], sx[:, g, :])
                link(last)
                for g in range(8):
                    v.max_index(it[:, g, 0:8], vt[:, g, 0:8], sv[:, g, :])
                    last = v.max_index(it[:, g, 8:16], vt[:, g, 8:16], sx[:, g, :])
                return last

            def norms(b, t):
                n = slice(t * 2 * H, t * 2 * H + 2 * H)
                o = full(dve, f"norm{t}", b)
                freed(v.tensor_scalar(nrm[:, n], o[:, 0:2 * H], 1e-24, None, ALU.max), f"norm{t}", b)

            def N0f(b):
                norms(b, 0)

            def N0g(b):
                norms(b, 1)

            def N1_0(b):
                top_keys(b, 0)

            def N1_1(b):
                top_keys(b, 1).then_inc(i16_ready, 1)

            def N1_2(b):
                top_keys(b, 2)

            def N1_3(b):
                top_keys(b, 3).then_inc(i16_ready, 1)

            def sums(b, t):
                n, h = slice(t * 2 * H, t * 2 * H + 2 * H), slice(t * H, t * H + H)
                dve.wait_ge(inv_ready, NT * b + t + 1)
                dve.wait_ge(i16_ready, NT * b + t + 1)
                v.tensor_tensor(v16[:, h, :, :].rearrange("p g a k -> p (g a) k"),
                                vraw[:, h, :, :].rearrange("p g a k -> p (g a) k"),
                                inv[:, n].unsqueeze(2).broadcast_to([P, 2 * H, TOP]),
                                ALU.mult).then_inc(v16_ready, 1)
                dve.wait_ge(v16_ready, NT * b + t + 1)
                for i0, r, c, at in CELL_BLOCKS:
                    last = v.tensor_tensor(cand[:, h, at:at + r * c].rearrange("p g (r c) -> p g r c", r=r),
                                           v16[:, h, 0, i0:i0 + r].unsqueeze(3).broadcast_to([P, H, r, c]),
                                           v16[:, h, 1, 0:c].unsqueeze(2).broadcast_to([P, H, r, c]), ALU.add)
                link(last)

            def mark(b, t, i, src, dst):
                for g in range(t * H, t * H + H):
                    last = v.max(c8[:, g, i, :], src[:, g, :])
                link(last)
                for g in range(t * H, t * H + H):
                    last = v.match_replace(dst[:, g, :], c8[:, g, i, :], src[:, g, :], MARK)
                link(last)

            def chosen(b, t):
                h = slice(t * H, t * H + H)
                dve.wait_ge(we_ready, NT * b + t + 1)
                link(v.scalar_tensor_tensor(
                    wem[:, :, h, :].rearrange("p a g c -> p a (g c)"),
                    candm[:, h, :].rearrange("p g c -> p (g c)").unsqueeze(1).broadcast_to([P, 2, H * CELLS]), MARK,
                    we[:, :, h, :].rearrange("p a g c -> p a (g c)"), ALU.is_equal, ALU.mult))
                link(v.tensor_reduce(zs[:, 0, h], wem[:, 0, h, :], X, ALU.add))
                link(v.reciprocal(zs[:, 1, h], zs[:, 0, h]))
                v.tensor_scalar(zs[:, 2, h], zs[:, 1, h], W_SCALE, None, ALU.mult).then_inc(wem_ready, 1)

            def N2a(b):
                sums(b, 0)
                mark(b, 0, 0, cand, candx)

            def N2b(b):
                mark(b, 0, 1, candx, candm)

            def N2c(b):
                if b >= 1:
                    dve.wait_ge(slots_ready, NT * b)
                chosen(b, 0)

            def N2d(b):
                sums(b, 1)
                mark(b, 1, 0, cand, candx)

            def N2e(b):
                mark(b, 1, 1, candx, candm)

            def N2f(b):
                chosen(b, 1)

            def N3a(b):
                if b >= 1:
                    full(dve, "G1", b - 1)
                read_out(dve, "eT", b)
                v.tensor_scalar(eT[0:KC, 1, :], eT[0:KC, 0, :], LO - 1, None, ALU.bitwise_and)
                v.tensor_scalar(eT[0:KC, 2, :], eT[0:KC, 0, :], E - LO, None,
                                ALU.bitwise_and).then_inc(eT_ready, 1)
                o = full(dve, "wT", b)
                dve.wait_ge(act_chain, b + 1)
                freed(v.tensor_tensor(W2[0:KC, 1, :], o[0:KC, :], W2[0:KC, 0, :], ALU.subtract), "wT", b)
                dve.wait_ge(eT_ready, b + 1)
                for lo in range(LO):
                    last = v.tensor_scalar(lom[0:KC, lo, :], eT[0:KC, 1, :], float(lo), None, ALU.is_equal)
                link(last)
                read_out(dve, "wT", b)
                for lo in range(LO):
                    v.tensor_tensor(R[0:KC, :, lo, :], W2[0:KC, :, :],
                                    lom[0:KC, lo, :].unsqueeze(1).broadcast_to([KC, 2, NCH * N]), ALU.mult)

            def N3b(b):
                for hi in range(POOL_HI, HI):
                    last = v.tensor_scalar(OH[0:KC, :, :, hi, :], hi_view(eT), float(LO * hi), None, ALU.is_equal)
                last.then_inc(onehot_dve_ready, 1)

            def products(b, t):
                o = full(dve, f"G{t}", b)
                freed(v.tensor_tensor(
                    prod[:, t, :, :], o[:, :].rearrange("p (g e) -> p g e", g=32),
                    act[:, t, :, :, :].rearrange("p g q l -> p g (q l)"), ALU.mult), f"G{t}", b)

            def N5a(b):
                read_out(dve, "I", b)
                if b >= 1:
                    full(dve, "Y", b - 1)
                products(b, 0)

            def N5b(b):
                products(b, 1)

            def N6b(b):
                p = b % 2
                stored(dve, b, 1)
                o = full(dve, "YT", b)
                ins = v.tensor_tensor(outs[:, :, :], o[:, 0:N].rearrange("p (t c) -> p t c", t=NT),
                                      t1[:, p, :, :], ALU.add)
                freed(ins, "YT", b)
                read_out(dve, "YT", b)
                v.engine_nop().then_inc(out_ready, 1)

            do = {"A0a": A0a, "A2c": A2c, "A3a": A3a, "F5a": F5a, "F6a": F6a, "F6c": F6c, "F7b": F7b, "F8b":
                  F8b, "F9a": F9a, "F9b": F9b, "F9c": F9c, "F9d": F9d, "F11a": F11a, "F11c": F11c, "NS": NS,
                  "N0a": N0a, "N0h": N0h, "N0b": N0b, "N0d": N0d, "N0f": N0f, "N0g": N0g, "N1_0": N1_0, "N1_1":
                  N1_1, "N1_2": N1_2, "N1_3": N1_3, "N2a": N2a, "N2b": N2b, "N2c": N2c, "N2d": N2d, "N2e": N2e,
                  "N2f": N2f, "N3a": N3a, "N3b": N3b, "N5a": N5a, "N5b": N5b, "N6b": N6b, "NB": setup_rows}
            for s, b in schedule("vector"):
                if s in do:
                    do[s](b)

        @block.gpsimd
        def _(pool):
            g_ = nc.gpsimd
            link = chained(pool, pool_chain)

            g_.memset(mhalf[:, :], -0.5)
            g_.memset(ones[:, :], 1.0)
            g_.memset(qpad[:, :, :], 0.0)
            g_.memset(rts[:, :, :], LARGE)
            g_.memset(bias[:, :, :, :], 0.0)
            g_.memset(act[:, :, :, :, :], 0.0)
            g_.memset(ones3[:, :], 1.0)
            link(g_.memset(vBD0[:, :, :, :, :], 0.0))
            for r in range(2):
                link(g_.memset(vBD0[NP_ * r:NP_ * r + NP_, :, :, r, DH:DH + 1], 1.0))
            g_.memset(vA[:, :, :, DH:DH + 1], 1.0).then_inc(preset, 1)
            pool.wait_ge(preset, 1)

            def inverse_root(k, b):
                pool.wait_ge(var_ready[k], b + 1)
                link(g_.tensor_tensor(rstd[:, k, :], veps[:, k, :], mhalf[:, 0:NT], ALU.pow))
                g_.tensor_tensor(shift[:, k, :], negmean[:, k, :], rstd[:, k, :], ALU.mult).then_inc(rstd_ready[k], 1)

            def A0a(b):
                sampling_free(pool, b)
                inverse_root(0, b)

            def A0b(b):
                if b == 0:
                    pool.wait_ge(wa_loaded, 16)
                pool.wait_ge(hat_ready[0], b + 1)
                link(g_.tensor_tensor(xln[:, :, :], hat[:, 0, :, :],
                                      A("lng").unsqueeze(1).broadcast_to([P, NT, C]), ALU.mult))
                g_.tensor_tensor(xln[:, :, :], xln[:, :, :],
                                 A("lnb").unsqueeze(1).broadcast_to([P, NT, C]), ALU.add).then_inc(xln_ready, 1)

            def A2a(b):
                if b == 0:
                    pool.wait_ge(wa_loaded, 16)
                read_out(pool, "qimg", b)
                if b == 0:
                    conv_rows(g_, CONV_DVE, KS).then_inc(taps_pool_ready, 1)
                else:
                    pool.wait_ge(conv_ready, b)
                    link(conv_rows(g_, 0, KS // 2))

            def A2a2(b):
                if b >= 1:
                    link(conv_rows(g_, KS // 2, KS))

            def fold(n):
                return g_.tensor_tensor(taps[:, 1:1 + n, :], taps[:, 1:1 + n, :], taps[:, 1 + n:1 + 2 * n, :], ALU.add)

            def A2b(b):
                if b >= 1:
                    link(fold((KS * KS - 1) // 2))

            def A2b2(b):
                if b >= 1:
                    n = (KS * KS - 1) // 4
                    while n > FOLDED - 1:
                        link(fold(n))
                        n //= 2
                    fold(n).then_inc(taps_pool_ready, 1)

            def A3a(b):
                if b >= 1:
                    sampling_weights(pool, g_, link, b)

            def A4(b):
                read_out(pool, "kh", b)
                g_.tensor_tensor(kBD0[:, b % 2, :, :], khT[:, :].unsqueeze(1).broadcast_to([P, H, NP_]),
                                hm.unsqueeze(2).broadcast_to([P, H, NP_]), ALU.mult).then_inc(kbd0_ready, 1)

            def F6c(b):
                inverse_root(1, b)

            def F7b(b):
                inverse_root(2, b)

            def F8b(b):
                if b >= 1:
                    full(pool, "O1", b - 1)
                read_out(pool, "k1", b)
                g_.tensor_tensor(kBD1[:, :, :].rearrange("p (j h) n -> p j h n", j=2),
                                 kE[:, :, :].unsqueeze(2).broadcast_to([P, 2, 4, N]),
                                 Bw("hm32").unsqueeze(1).unsqueeze(3).broadcast_to([P, 2, 4, N]),
                                 ALU.mult).then_inc(kbd1_ready, 1)

            def F11c(b):
                inverse_root(3, b)

            def NS(b):
                k = slice(0, NK)
                pool.wait_ge(kss_ready, 1)
                g_.tensor_tensor(kss[k, 2, :], kss[k, 1, :], mhalf[k, 0:4], ALU.pow).then_inc(kinv_ready, 1)
                pool.wait_ge(ws_loaded, 16)
                g_.tensor_copy(ident16[:, :], ident)
                g_.tensor_copy(Epat16[:, :], Sw("Epat"))
                g_.tensor_scalar(up[:, :, :].rearrange("p l c -> p (l c)"), Sw("upR"), 1.0 / W_SCALE, None,
                                 ALU.mult).then_inc(up_ready, 1)

            def query_roots(b, t):
                pool.wait_ge(qvar_ready, NT * b + t + 1)
                g_.tensor_tensor(qrstd[:, t, :], ssq[:, t, 1, :], mhalf[:, 0:H], ALU.pow).then_inc(qrstd_ready, 1)

            def N0a(b):
                query_roots(b, 0)

            def N0h(b):
                query_roots(b, 1)

            def inverse_norms(b, t):
                n = slice(t * 2 * H, t * 2 * H + 2 * H)
                read_out(pool, f"norm{t}", b)
                g_.tensor_tensor(inv[:, n], nrm[:, n], mhalf[:, 0:2 * H], ALU.pow).then_inc(inv_ready, 1)

            def N0f(b):
                inverse_norms(b, 0)

            def N0g(b):
                inverse_norms(b, 1)

            def cells(b, t):
                h = slice(t * H, t * H + H)
                pool.wait_ge(v16_ready, NT * b + t + 1)
                vv = v16[:, h, :, :].rearrange("p g a k -> p (g a) k")
                g_.tensor_tensor(dv[:, h, :, :].rearrange("p g a k -> p (g a) k"), vv,
                                 vv[:, :, 0:1].broadcast_to([P, 2 * H, TOP]), ALU.subtract).then_inc(dv_ready, 1)
                for s, (src, ready, op) in enumerate(((ab, ab_ready, ALU.mult), (if_, if_ready, ALU.add))):
                    pool.wait_ge(ready, NT * b + t + 1)
                    for i0, r, c, at in CELL_BLOCKS:
                        last = g_.tensor_tensor(
                            we[:, s, h, at:at + r * c].rearrange("p g (r c) -> p g r c", r=r),
                            src[:, h, 0, i0:i0 + r].unsqueeze(3).broadcast_to([P, H, r, c]),
                            src[:, h, 1, 0:c].unsqueeze(2).broadcast_to([P, H, r, c]), op)
                last.then_inc(we_ready, 1)

            def merge(b, t):
                h = slice(t * H, t * H + H)
                pool.wait_ge(wem_ready, NT * b + t + 1)
                src, dst = wem[:, :, h, :], slots[:, :, h, :]
                for at, c, step, n in SLOT_COPIES:
                    g_.tensor_copy(dst[:, :, :, at:at + n], src[:, :, :, c:c + step * (n - 1) + 1:step])
                for at, c, step, c2, step2, n in SLOT_SUMS:
                    end = c2 + step2 * (n - 1) - 1
                    last = g_.tensor_tensor(dst[:, :, :, at:at + n], src[:, :, :, c:c + n],
                                            src[:, :, :, c2:end:step2], ALU.add)
                link(last)
                g_.tensor_tensor(wn[:, h, :], slots[:, 0, h, :],
                                 zs[:, 2, h].unsqueeze(2).broadcast_to([P, H, SLOTS]), ALU.mult)\
                    .then_inc(slots_ready, 1)

            def N2a(b):
                if b >= 1:
                    full(pool, "G1", b - 1)
                    read_out(pool, "G1", b - 1)
                cells(b, 0)

            def N2c(b):
                if b >= 1:
                    read_out(pool, "eT", b - 1)
                    read_out(pool, "wT", b - 1)
                merge(b, 0)

            def N2d(b):
                cells(b, 1)

            def N2f(b):
                merge(b, 1)

            def N3b(b):
                if b >= 1:
                    full(pool, "G1", b - 1)
                pool.wait_ge(eT_ready, b + 1)
                for hi in range(0, POOL_HI):
                    last = g_.tensor_scalar(OH[0:KC, :, :, hi, :], hi_view(eT), float(LO * hi), None, ALU.is_equal)
                last.then_inc(onehot_pool_ready, 1)

            do = {"A0a": A0a, "A0b": A0b, "A2a": A2a, "A2a2": A2a2, "A2b": A2b, "A2b2": A2b2, "A3a": A3a, "A4": A4, "F6c": F6c, "F7b": F7b,
                  "F8b": F8b, "F11c": F11c, "NS": NS, "N0a": N0a, "N0h": N0h, "N0f": N0f, "N0g": N0g, "N2a":
                  N2a, "N2c": N2c, "N2d": N2d, "N2f": N2f, "N3b": N3b}
            for s, b in schedule("gpsimd"):
                if s in do:
                    do[s](b)


def kernel(**inputs):
    import numpy as np
    import concourse.bacc as bacc
    from concourse.bass_utils import run_bass_kernel_spmd

    a = {k: np.asarray(v) for k, v in inputs.items()}
    f = np.float32

    def bc(v, n=P):
        return np.broadcast_to(v.reshape(1, -1), (n, v.size))

    def pad(v):
        out = np.zeros((P, v.shape[1]), f)
        out[:v.shape[0]] = v
        return out

    ch = np.arange(P)
    pos = np.arange(NP_)
    ref = ((np.arange(G8, dtype=f) + f(0.5)) * f(2.0 / G8) - f(1.0)).astype(f)
    heads = (ch[:, None] // DH == np.arange(H)[None, :]).astype(f)
    col0 = np.arange(H * NP_)
    E0 = ((np.arange(P)[:, None] % H == (col0 // NP_)[None, :]) & (np.arange(P)[:, None] < 3 * H)).astype(f)
    Epat = (ch[:, None] % 32 - DH == np.arange(N)[None, :] // SEG).astype(f)
    blocks = (ch[:, None] // 32 == np.arange(4)[None, :]).astype(f)
    less = -(ch[:, None] > np.arange(2)[None, :]).astype(f)

    vecs = np.stack([a["L0_conv_" + n] for n in ("ln_g", "ln_b", "bq", "bv", "dw_b", "mq_b", "mk_b")]
                    + [a["L0_conv_bq"]], axis=1)
    wv = a["L0_conv_wv"]
    down = a["L1_ffn_expert_down"][:E]
    up = a["L1_ffn_expert_up"][:E]
    upR = np.broadcast_to(up.reshape(1, HI, LO * C), (4, HI, LO * C))
    k0, k1 = a["L1_ffn_keys0"], a["L1_ffn_keys1"]
    A = {"ident": np.eye(P, dtype=f), "wq": a["L0_conv_wq"], "lng": bc(a["L0_conv_ln_g"]),
         "lnb": bc(a["L0_conv_ln_b"]), "vecs": vecs, "pw": a["L0_conv_pw_w"].reshape(2, C)[::-1].T,
         "less": less, "refs": pad(np.stack([ref[pos % G8], ref[pos // G8]], axis=1)), "iota": bc(np.arange(SIDE, dtype=f)),
         "hm": heads, "dw": a["L0_conv_dw_w"].reshape(C, KS * KS),
         "wv2": pad(wv.reshape(2, NP_, C).transpose(1, 0, 2).reshape(NP_, 2 * C)),
         "mq": a["L0_conv_mq_w"], "mk": a["L0_conv_mk_w"], "mv": a["L0_conv_mv_w"], "mo": a["L0_conv_mo_w"],
         "mlp": a["L0_conv_mlp_w"], "E0": E0}
    wqk = np.zeros((C, 2, H, 32), f)
    wqk[:, :, :, :DH] = a["L1_attn_w_qkv"].T[:, :2 * C].reshape(C, 2, H, DH)
    Bm = {"wqk": wqk.reshape(C, 4 * P), "wv1": a["L1_attn_w_qkv"].T[:, 2 * C:], "wproj": a["L1_attn_w_proj"].T, "Wq": a["L1_ffn_Wq"].T,
          "fln": np.tile(np.stack([a["L1_ffn_ln_g"], a["L1_ffn_ln_b"]], axis=1), (2, 1)), "down": down.reshape(HI, LO, C).transpose(2, 1, 0).reshape(C, E), "hm32": blocks}
    Sm = {"upR": upR.reshape(P, -1), "keys": pad(np.concatenate([k0, k1, k0, k1], axis=1)),
          "Epat": Epat}
    rows = {"bq": a["L0_conv_bq"], "mvb": a["L0_conv_mv_b"], "mob": a["L0_conv_mo_b"], "mlpb": a["L0_conv_mlp_b"],
            "bproj": a["L1_attn_b_proj"], "fbq": a["L1_ffn_bq"]}
    arrays = {
        "x": np.ascontiguousarray(a["x"].reshape(B, NT, P, C).transpose(0, 2, 1, 3)),
        "wa": np.ascontiguousarray(np.concatenate([A[n] for n, _ in WEIGHTS_A], axis=1)),
        "wb": np.ascontiguousarray(np.concatenate([Bm[n] for n, _ in WEIGHTS_B], axis=1)),
        "ws": np.ascontiguousarray(np.concatenate([Sm[n] for n, _ in WEIGHTS_S], axis=1)),
        "rows": np.ascontiguousarray(bc(np.concatenate([rows[n] for n, _ in ROWS]), 3)),
    }
    nc = bacc.Bacc("TRN2", target_bir_lowering=False, num_devices=1)
    args = [nc.dram_tensor(n + "_dram", v.shape, mybir.dt.from_np(v.dtype), kind="ExternalInput").ap()
            for n, v in arrays.items()]
    out = nc.dram_tensor("out_dram", (B, P, NT, C), F32, kind="ExternalOutput").ap()
    build(nc, *args, out)
    r = run_bass_kernel_spmd(nc, [{n + "_dram": v for n, v in arrays.items()}], core_ids=[0])
    got = r.results[0]["out_dram"]
    return np.ascontiguousarray(got.transpose(0, 2, 1, 3)).reshape(B, SIDE, SIDE, C)
```
